# Optimizing a Trainium2 kernel written in Bass

```python
import numpy as np
import jax
import jax.numpy as jnp

def _softmax(x, axis=-1):
    return jax.nn.softmax(x, axis=axis)

def _gelu(x):
    return jax.nn.gelu(x, approximate=True)

def _silu(x):
    return jax.nn.silu(x)

def _sigmoid(x):
    return jax.nn.sigmoid(x)

def _layernorm(x, axis=-1, eps=1e-05):
    m = jnp.mean(x, axis=axis, keepdims=True)
    v = jnp.var(x, axis=axis, keepdims=True)
    return (x - m) / jnp.sqrt(v + eps)

def _scatter_add(tgt, idx, src, axis=0):
    return tgt.at[idx].add(src)

def _segment_sum(src, seg, n):
    return jax.ops.segment_sum(src, seg, n)
kernel_name = 'mk_decoder_preln_d1_seqx_r2_47a5e5'

def setup_inputs(seed: int=0):
    np.random.seed(seed)
    _w = jnp.asarray

    def _rec_inputs():
        import jax
        import jax.numpy as jnp
        _rk = jax.random.key(seed)
        x = -0.0003929 + 0.9999 * jax.random.normal(jax.random.fold_in(_rk, 1), (8, 224, 512), jnp.float32)
        _lenS = 224 - jax.random.randint(jax.random.fold_in(_rk, 7), (8,), 0, max(1, 224 // 4) + 1, jnp.int32)
        _lenS2 = 750 - jax.random.randint(jax.random.fold_in(_rk, 8), (8,), 0, max(1, 750 // 4) + 1, jnp.int32)
        _ctx_512P = jax.random.normal(jax.random.fold_in(_rk, 11), (8, 16, 256), jnp.float32)
        _ctx_512c = jax.random.dirichlet(jax.random.fold_in(_rk, 511), 0.3 * jnp.ones((16,), jnp.float32), (8, 750))
        _ctx_512t = jnp.einsum('bsk,bkd->bsd', _ctx_512c, _ctx_512P)
        _ctx_512t = _ctx_512t * jax.lax.rsqrt(jnp.mean(jnp.square(_ctx_512t)) + 1e-12) * 0.953939
        ctx_512 = -1.39393e-06 + 0.999914 * (_ctx_512t + 0.3 * jax.random.normal(jax.random.fold_in(_rk, 611), (8, 750, 256), jnp.float32))
        return (x, ctx_512)
    x, ctx_512 = _rec_inputs()

    def _L0_attn_setup():
        import jax, jax.numpy as jnp
        import numpy as np
        D_CONV = 4
        DT_RANK = 64
        D_STATE = 16

        def silu(v):
            return v * jax.nn.sigmoid(v)
        key = jax.random.key(seed)
        ks = jax.random.split(key, 10)
        B, L, d_model, d_inner = (2, 1024, 512, 1024)

        def nrm(k, shape, scale):
            return jax.random.normal(k, shape, dtype=jnp.float32) * scale
        A = jnp.tile(jnp.arange(1, D_STATE + 1, dtype=jnp.float32), (d_inner, 1))
        return {'x': nrm(ks[0], (B, L, d_model), 1.0), 'W_in': nrm(ks[1], (d_model, 2 * d_inner), d_model ** (-0.5)), 'conv_w': nrm(ks[2], (d_inner, D_CONV), D_CONV ** (-0.5)), 'conv_b': nrm(ks[3], (d_inner,), 0.02), 'W_x': nrm(ks[4], (d_inner, DT_RANK + 2 * D_STATE), d_inner ** (-0.5)), 'W_dt': nrm(ks[5], (DT_RANK, d_inner), DT_RANK ** (-0.5)), 'b_dt': nrm(ks[6], (d_inner,), 0.02), 'A_log': jnp.log(A), 'D': jnp.ones((d_inner,), dtype=jnp.float32), 'W_out': nrm(ks[7], (d_inner, d_model), d_inner ** (-0.5))}
    _L0_attn_all = _L0_attn_setup()
    _L0_attn_in = {k: v for k, v in _L0_attn_all.items() if k in ('W_in', 'conv_w', 'conv_b', 'W_x', 'W_dt', 'b_dt', 'A_log', 'D', 'W_out')}
    del _L0_attn_all

    def _L0_xattn_setup():
        import jax, jax.numpy as jnp
        import numpy as np
        HEADS = 16
        D_MODEL = 512
        IMG_MODEL = 256
        D_K = D_MODEL // HEADS
        key = jax.random.key(seed)
        ks = jax.random.split(key, 12)
        B, LQ, LKV = (8, 1024, 512)
        s_dm = 1.0 / np.sqrt(D_MODEL)
        s_im = 1.0 / np.sqrt(IMG_MODEL)
        return {'q': jax.random.normal(ks[0], (B, LQ, D_MODEL), jnp.float32), 'k': jax.random.normal(ks[1], (B, LKV, IMG_MODEL), jnp.float32), 'v': jax.random.normal(ks[2], (B, LKV, IMG_MODEL), jnp.float32), 'Wq': jax.random.normal(ks[3], (D_MODEL, D_MODEL), jnp.float32) * s_dm, 'bq': jnp.zeros((D_MODEL,), jnp.float32), 'Wk': jax.random.normal(ks[4], (IMG_MODEL, D_MODEL), jnp.float32) * s_im, 'bk': jnp.zeros((D_MODEL,), jnp.float32), 'Wv': jax.random.normal(ks[5], (IMG_MODEL, D_MODEL), jnp.float32) * s_im, 'bv': jnp.zeros((D_MODEL,), jnp.float32), 'Wo': jax.random.normal(ks[6], (D_MODEL, D_MODEL), jnp.float32) * s_dm, 'bo': jnp.zeros((D_MODEL,), jnp.float32)}
    _L0_xattn_all = _L0_xattn_setup()
    _L0_xattn_in = {k: v for k, v in _L0_xattn_all.items() if k in ('Wq', 'bq', 'Wk', 'bk', 'Wv', 'bv', 'Wo', 'bo')}
    del _L0_xattn_all

    def _L0_ffn_setup():
        import jax, jax.numpy as jnp
        import numpy as np
        key = jax.random.key(seed)
        ks = jax.random.split(key, 6)
        B, L, D, E = (4, 1024, 512, 4)
        H = 4 * D
        x = jax.random.normal(ks[0], (B, L, D), dtype=jnp.float32)
        rW1 = jax.random.normal(ks[1], (D, 2 * D), dtype=jnp.float32) * (2.0 / D) ** 0.5
        rb1 = jnp.zeros((2 * D,), dtype=jnp.float32)
        rW2 = jax.random.normal(ks[2], (2 * D, E), dtype=jnp.float32) * (2.0 / (2 * D)) ** 0.5
        rb2 = jnp.zeros((E,), dtype=jnp.float32)
        We1 = jax.random.normal(ks[3], (E, D, H), dtype=jnp.float32) * (2.0 / D) ** 0.5
        be1 = jnp.zeros((E, H), dtype=jnp.float32)
        We2 = jax.random.normal(ks[4], (E, H, D), dtype=jnp.float32) * (2.0 / H) ** 0.5
        be2 = jnp.zeros((E, D), dtype=jnp.float32)
        return {'x': x, 'rW1': rW1, 'rb1': rb1, 'rW2': rW2, 'rb2': rb2, 'We1': We1, 'be1': be1, 'We2': We2, 'be2': be2}
    _L0_ffn_all = _L0_ffn_setup()
    _L0_ffn_in = {k: v for k, v in _L0_ffn_all.items() if k in ('rW1', 'rb1', 'rW2', 'rb2', 'We1', 'be1', 'We2', 'be2')}
    del _L0_ffn_all
    return {'x': x, 'ctx_512': ctx_512, 'L0_attn_W_in': _L0_attn_in['W_in'], 'L0_attn_conv_w': _L0_attn_in['conv_w'], 'L0_attn_conv_b': _L0_attn_in['conv_b'], 'L0_attn_W_x': _L0_attn_in['W_x'], 'L0_attn_W_dt': _L0_attn_in['W_dt'], 'L0_attn_b_dt': _L0_attn_in['b_dt'], 'L0_attn_A_log': _L0_attn_in['A_log'], 'L0_attn_D': _L0_attn_in['D'], 'L0_attn_W_out': _L0_attn_in['W_out'], 'L0_xattn_Wq': _L0_xattn_in['Wq'], 'L0_xattn_bq': _L0_xattn_in['bq'], 'L0_xattn_Wk': _L0_xattn_in['Wk'], 'L0_xattn_bk': _L0_xattn_in['bk'], 'L0_xattn_Wv': _L0_xattn_in['Wv'], 'L0_xattn_bv': _L0_xattn_in['bv'], 'L0_xattn_Wo': _L0_xattn_in['Wo'], 'L0_xattn_bo': _L0_xattn_in['bo'], 'L0_ffn_rW1': _L0_ffn_in['rW1'], 'L0_ffn_rb1': _L0_ffn_in['rb1'], 'L0_ffn_rW2': _L0_ffn_in['rW2'], 'L0_ffn_rb2': _L0_ffn_in['rb2'], 'L0_ffn_We1': _L0_ffn_in['We1'], 'L0_ffn_be1': _L0_ffn_in['be1'], 'L0_ffn_We2': _L0_ffn_in['We2'], 'L0_ffn_be2': _L0_ffn_in['be2']}

def reference(x, ctx_512, L0_attn_W_in, L0_attn_conv_w, L0_attn_conv_b, L0_attn_W_x, L0_attn_W_dt, L0_attn_b_dt, L0_attn_A_log, L0_attn_D, L0_attn_W_out, L0_xattn_Wq, L0_xattn_bq, L0_xattn_Wk, L0_xattn_bk, L0_xattn_Wv, L0_xattn_bv, L0_xattn_Wo, L0_xattn_bo, L0_ffn_rW1, L0_ffn_rb1, L0_ffn_rW2, L0_ffn_rb2, L0_ffn_We1, L0_ffn_be1, L0_ffn_We2, L0_ffn_be2):
    import jax
    import jax.numpy as jnp

    def _L0_attn_ref(x, W_in, conv_w, conv_b, W_x, W_dt, b_dt, A_log, D, W_out):
        import jax, jax.numpy as jnp
        import numpy as np
        D_CONV = 4
        DT_RANK = 64
        D_STATE = 16

        def silu(v):
            return v * jax.nn.sigmoid(v)
        B, L, _ = x.shape
        d_inner = W_dt.shape[1]
        xz = x @ W_in
        xb, z = jnp.split(xz, 2, axis=-1)
        xp = jnp.pad(xb, ((0, 0), (D_CONV - 1, 0), (0, 0)))
        xc = sum((xp[:, k:k + L, :] * conv_w[:, k] for k in range(D_CONV))) + conv_b
        xb = silu(xc)
        x_dbl = xb @ W_x
        dt_low, Bm, Cm = jnp.split(x_dbl, [DT_RANK, DT_RANK + D_STATE], axis=-1)
        dt = jax.nn.softplus(dt_low @ W_dt + b_dt)
        A = -jnp.exp(A_log)

        def step(h, inp):
            dt_t, B_t, C_t, x_t = inp
            dA = jnp.exp(A * dt_t[..., None])
            h = h * dA + (x_t * dt_t)[..., None] * B_t[:, None, :]
            y = jnp.einsum('bdn,bn->bd', h, C_t)
            return (h, y)
        xs = (dt.swapaxes(0, 1), Bm.swapaxes(0, 1), Cm.swapaxes(0, 1), xb.swapaxes(0, 1))
        h0 = jnp.zeros((B, d_inner, D_STATE), dtype=x.dtype)
        _, ys = jax.lax.scan(step, h0, xs)
        y = ys.swapaxes(0, 1) + xb * D
        out = y * silu(z)
        return out @ W_out

    def _L0_xattn_ref(q, k, v, Wq, bq, Wk, bk, Wv, bv, Wo, bo):
        import jax, jax.numpy as jnp
        import numpy as np
        HEADS = 16
        D_MODEL = 512
        IMG_MODEL = 256
        D_K = D_MODEL // HEADS
        B, LQ, _ = q.shape
        LKV = k.shape[1]
        qh = (q @ Wq + bq).reshape(B, LQ, HEADS, D_K).transpose(0, 2, 1, 3)
        kh = (k @ Wk + bk).reshape(B, LKV, HEADS, D_K).transpose(0, 2, 1, 3)
        vh = (v @ Wv + bv).reshape(B, LKV, HEADS, D_K).transpose(0, 2, 1, 3)
        scale = 1.0 / np.sqrt(D_K)
        scores = jnp.einsum('bhqd,bhkd->bhqk', qh, kh) * scale
        attn = jax.nn.softmax(scores, axis=-1)
        out = jnp.einsum('bhqk,bhkd->bhqd', attn, vh)
        concat = out.transpose(0, 2, 1, 3).reshape(B, LQ, D_MODEL)
        return concat @ Wo + bo

    def _L0_ffn_ref(x, rW1, rb1, rW2, rb2, We1, be1, We2, be2):
        import jax, jax.numpy as jnp
        import numpy as np
        E = We1.shape[0]
        top_k = min(2, E)
        rh = jax.nn.gelu(x @ rW1 + rb1, approximate=False)
        router_logits = rh @ rW2 + rb2
        router_probs = jax.nn.softmax(router_logits, axis=-1)
        expert_weights, expert_indices = jax.lax.top_k(router_probs, top_k)
        one_hot = jax.nn.one_hot(expert_indices, E, dtype=x.dtype)
        token_mask = one_hot.sum(axis=2)
        combine_w = (one_hot * expert_weights[..., None]).sum(axis=2)
        out = jnp.zeros_like(x)
        for e in range(E):
            xi = x * token_mask[..., e:e + 1]
            h = jax.nn.gelu(xi @ We1[e] + be1[e], approximate=False)
            yo = h @ We2[e] + be2[e]
            out = out + yo * combine_w[..., e:e + 1]
        return out
    x = x + _L0_attn_ref(_layernorm(x, axis=-1), L0_attn_W_in, L0_attn_conv_w, L0_attn_conv_b, L0_attn_W_x, L0_attn_W_dt, L0_attn_b_dt, L0_attn_A_log, L0_attn_D, L0_attn_W_out)
    x = x + _L0_xattn_ref(_layernorm(x, axis=-1), ctx_512, ctx_512, L0_xattn_Wq, L0_xattn_bq, L0_xattn_Wk, L0_xattn_bk, L0_xattn_Wv, L0_xattn_bv, L0_xattn_Wo, L0_xattn_bo)
    x = x + _L0_ffn_ref(_layernorm(x, axis=-1), L0_ffn_rW1, L0_ffn_rb1, L0_ffn_rW2, L0_ffn_rb2, L0_ffn_We1, L0_ffn_be1, L0_ffn_We2, L0_ffn_be2)
    return x

_drawn_inputs = setup_inputs


def setup_inputs(seed=0):
    import zlib

    import numpy as np

    out = dict(_drawn_inputs(seed))
    spreads = {'L0_attn_D': (1.0, 0.2),
     'L0_xattn_bq': (0.0, 0.286),
     'L0_xattn_bk': (0.0, 2.0),
     'L0_xattn_bv': (0.0, 0.1),
     'L0_xattn_bo': (0.0, 0.1),
     'L0_ffn_rb1': (0.0, 0.1),
     'L0_ffn_rb2': (0.0, 0.1),
     'L0_ffn_be1': (0.0, 0.1),
     'L0_ffn_be2': (0.0, 0.1)}
    factors = {'L0_attn_b_dt': 5.519, 'L0_attn_conv_b': 2.842}
    for name, (base, spread) in spreads.items():
        noise = np.random.default_rng([zlib.crc32(name.encode()), seed]).standard_normal(out[name].shape)
        drawn = base * np.exp(spread * noise) if base else spread * noise
        out[name] = jnp.asarray(drawn.astype(out[name].dtype))
    for name, factor in factors.items():
        out[name] = (out[name] * factor).astype(out[name].dtype)
    return out
```

```python
from contextlib import ExitStack

import concourse.bass as bass
from concourse import mybir

F32 = mybir.dt.float32
I32 = mybir.dt.int32
U32 = mybir.dt.uint32
ALU = mybir.AluOpType
ACT = mybir.ActivationFunctionType
AX = mybir.AxisListType

P = 128
EPS = 1e-5

B, L, DM = 8, 224, 512
T = B * L
TT = 112
NT = T // TT
KC = DM // P
DI = 1024
CC = DI // P
TAPS = 4
R, NS = 64, 16
XR = R + 2 * NS
GB = 2
G = B // GB
GL = GB * L
HS = NS // 2
HBUF, DBUF = 4, 2
UB_FREE = 3
CTX, CD = 750, 256
CT = 125
NC = CTX // CT
CK = CD // P
HEADS, DK = 16, 32
HALF = CTX // 2
RH = 1024
RC = RH // P
E, H = 4, 2048
HC = H // P
SLOTS = T
ET = SLOTS // P


def mamba_in(nc, x, W_in, conv_w, conv_b, W_x, W_dt, b_dt, ident_in, xb_d, z_d, dt_d, u_d, bc_d, xs_d):
    ctx = ExitStack()
    with ctx:
        def sb(name, shape, dt=F32):
            return ctx.enter_context(nc.sbuf_tensor("a_" + name, shape, dt))

        def sem(name):
            return ctx.enter_context(nc.semaphore("a_" + name))

        x_sb = sb("x", [TT, NT, DM])
        xn = sb("xn", [TT, 2, DM])
        xnT = sb("xnT", [P, KC, T])
        st = sb("st", [TT, NT, 6])
        mv = sb("mv", [TT, NT, 2])
        rstd = sb("rstd", [TT, NT])
        ident = sb("ident", [P, P])
        win = sb("win", [P, 2, KC, P])
        xpad = sb("xpad", [P, B, TAPS - 1 + L])
        acc = sb("acc", [P, 2, T])
        zs = sb("zs", [P, T])
        xb = sb("xb", [P, CC, T])
        cw = sb("cw", [P, CC, TAPS])
        cb = sb("cb", [P, CC])
        wx = sb("wx", [P, CC, XR])
        xdbl = sb("xdbl", [XR, T])
        wdt = sb("wdt", [R, DI])
        bdt = sb("bdt", [P, CC])
        zero = sb("zero", [P, 2048])
        ps = ctx.enter_context(nc.psum_tensor("a_ps", [P, 8, 512], F32))

        loaded = sem("loaded")
        w_in_loaded = [sem("xb_w_loaded"), sem("z_w_loaded")]
        stats_done, mv_done, var_done, std_done, rstd_done = (sem(n) for n in ("stats", "mv", "var", "std", "rstd"))
        xn_done, transposed, xnT_done = sem("xn_done"), sem("transposed"), sem("xnT_done")
        pad_zeroed, zero_set = sem("pad_zeroed"), sem("zero_set")
        xb_mm, z_mm, padded, conv_step, conv_done, silu_done, z_done = (
            sem(n) for n in ("xb_mm", "z_mm", "padded", "conv_step", "conv_done", "silu_done", "z_done"))
        z_stored, xb_stored, zero_stored = sem("z_stored"), sem("xb_stored"), sem("zero_stored")
        xdbl_mm, xdbl_done, xdbl_stored = sem("xdbl_mm"), sem("xdbl_done"), sem("xdbl_stored")
        dt_mm, ln_done, soft_step, relu_done, dt_done, u_done, u_stored = (
            sem(n) for n in ("dt_mm", "ln_done", "soft_step", "relu_done", "dt_done", "u_done", "u_stored"))
        dt_stored = [sem("dt_stored0"), sem("dt_stored1")]
        N_LOADS = 8

        win_v = W_in.rearrange("(k p) n -> p k n", p=P)
        block = ctx.enter_context(nc.Block())

        @block.sync
        def _(sp):
            sp.sem_inc(z_stored, 1)
            sp.dma_start(x_sb[:], x.rearrange("b (u p) d -> p (b u) d", p=TT)).then_inc(loaded, 16)
            sp.dma_start(ident[:], ident_in).then_inc(loaded, 16)
            sp.dma_start(cw[:], conv_w.rearrange("(c p) k -> p c k", p=P)).then_inc(loaded, 16)
            sp.dma_start(cb[:], conv_b).then_inc(loaded, 16)
            sp.dma_start(wx[:], W_x.rearrange("(c p) n -> p c n", p=P)).then_inc(loaded, 16)
            sp.dma_start(wdt[:], W_dt).then_inc(loaded, 16)
            sp.dma_start(bdt[:], b_dt).then_inc(loaded, 16)
            sp.dma_start(win[:, 0], win_v[:, :, 0:P]).then_inc(w_in_loaded[0], 16)
            sp.dma_start(win[:, 1], win_v[:, :, DI:DI + P]).then_inc(w_in_loaded[1], 16)
            with sp.Fori(0, CC - 1) as c:
                sp.wait_ge(xb_mm, c + 1)
                sp.dma_start(win[:, 0], win_v[:, :, bass.ds(c * P + P, P)]).then_inc(w_in_loaded[0], 16)
                sp.wait_ge(z_mm, c + 1)
                sp.dma_start(win[:, 1], win_v[:, :, bass.ds(c * P + (DI + P), P)]).then_inc(w_in_loaded[1], 16)
                sp.wait_ge(z_done, c + 2)
                sp.dma_start(z_d[bass.ds(c, 1)].rearrange("a p t -> (a p) t"), zs[:]).then_inc(z_stored, 16)
            sp.wait_ge(z_done, CC + 1)
            sp.dma_start(z_d[CC - 1], zs[:]).then_inc(z_stored, 16)
            sp.wait_ge(silu_done, CC + 1)
            sp.dma_start(xb_d.rearrange("c p t -> p c t"), xb[:]).then_inc(xb_stored, 16)
            sp.wait_ge(xdbl_done, 1)
            sp.dma_start(bc_d, xdbl[R:XR, :]).then_inc(xdbl_stored, 16)
            for c in range(CC):
                sp.wait_ge(dt_done, c + 1)
                sp.dma_start(dt_d[c], acc[:, c % 2]).then_inc(dt_stored[c % 2], 16)
                sp.wait_ge(u_done, c + 1)
                sp.dma_start(u_d[c], xb[:, c]).then_inc(u_stored, 16)
            sp.wait_ge(z_stored, 16 * CC + 1)
            sp.wait_ge(xb_stored, 16)
            sp.wait_ge(xdbl_stored, 16)
            for s in dt_stored:
                sp.wait_ge(s, 16 * CC // 2)
            sp.wait_ge(u_stored, 16 * CC)

        @block.gpsimd
        def _(pool):
            nc.gpsimd.memset(zero[:], 0.0).then_inc(zero_set, 1)
            pool.wait_ge(zero_set, 1)
            xs_v = xs_d.rearrange("(a p r) d -> a p (r d)", p=P, r=4)
            with pool.Fori(0, E * SLOTS // (P * 4)) as a:
                pool.dma_start(xs_v[bass.ds(a, 1)].rearrange("a p n -> (a p) n"), zero[:]).then_inc(zero_stored, 16)
            for c in range(CC):
                pool.wait_ge(xb_stored, 16)
                pool.wait_ge(xdbl_mm, 1)
                pool.wait_ge(dt_done, c + 1)
                nc.gpsimd.tensor_tensor(xb[:, c], xb[:, c], acc[:, c % 2], ALU.mult).then_inc(u_done, 1)
            pool.wait_ge(zero_stored, 16 * (E * SLOTS // (P * 4)))

        @block.vector
        def _(dve):
            nc.vector.memset(xpad[:, :, 0:TAPS - 1], 0.0).then_inc(pad_zeroed, 1)
            dve.wait_ge(loaded, 16 * (N_LOADS - 1))
            for i in range(NT):
                nc.vector.bn_stats(st[:, i], x_sb[:, i]).then_inc(stats_done, 1)
            for i in range(NT):
                dve.wait_ge(stats_done, i + 1)
                nc.vector.bn_aggr(mv[:, i], st[:, i]).then_inc(mv_done, 1)
            dve.wait_ge(mv_done, NT)
            nc.vector.tensor_scalar(rstd[:], mv[:, :, 1], EPS, None, ALU.add).then_inc(var_done, 1)
            dve.wait_ge(std_done, 1)
            nc.vector.reciprocal(rstd[:], rstd[:]).then_inc(rstd_done, 1)
            dve.wait_ge(rstd_done, 1)
            for i in range(NT):
                if i >= 2:
                    dve.wait_ge(transposed, i - 1)
                nc.vector.tensor_scalar(xn[:, i % 2], x_sb[:, i], mv[:, i, 0:1], rstd[:, i:i + 1],
                                        ALU.subtract, ALU.mult).then_inc(xn_done, 1)

            def taps(c, s):
                cwc = cw[:, c] if isinstance(c, int) else cw[:, bass.ds(c, 1)].rearrange("p a k -> p (a k)")
                out = acc[:, 0].rearrange("p (b t) -> p b t", b=B)
                for k in range(TAPS):
                    if k == 0:
                        nc.vector.tensor_scalar(out, xpad[:, :, 0:L], cwc[:, 0:1], None,
                                                ALU.mult).then_inc(conv_step, 1)
                    else:
                        dve.wait_ge(conv_step, s + k)
                        ins = nc.vector.scalar_tensor_tensor(out=out, in0=xpad[:, :, k:k + L], scalar=cwc[:, k:k + 1],
                                                             in1=out, op0=ALU.mult, op1=ALU.add)
                        ins.then_inc(conv_done if k == TAPS - 1 else conv_step, 1)

            with dve.Fori(0, CC) as c:
                dve.wait_ge(padded, c * G + (G + 1))
                dve.wait_ge(silu_done, c + 1)
                taps(c, c * (TAPS - 1))
            dve.wait_ge(xdbl_mm, 1)
            nc.vector.tensor_copy(xdbl[:].rearrange("p (g t) -> p g t", g=G), ps[0:XR, 0:G, 0:GL]).then_inc(xdbl_done, 1)
            dve.wait_ge(z_stored, 16 * CC + 1)
            for c in range(CC):
                q = 4 * (c % 2)
                dve.wait_ge(soft_step, 2 * c + 1)
                if c >= 1:
                    dve.wait_ge(dt_done, c)
                nc.vector.tensor_scalar(zs[:].rearrange("p (g t) -> p g t", g=G), ps[:, q:q + 4, 0:GL], bdt[:, c:c + 1],
                                        0.0, ALU.add, ALU.max).then_inc(relu_done, 1)
                dve.wait_ge(relu_done, c + 1)
                dve.wait_ge(ln_done, c + 1)
                nc.vector.tensor_tensor(acc[:, c % 2], acc[:, c % 2], zs[:], ALU.add).then_inc(dt_done, 1)

        @block.scalar
        def _(act):
            for s in (padded, z_done, silu_done):
                act.sem_inc(s, 1)
            act.wait_ge(var_done, 1)
            nc.scalar.activation(rstd[:], rstd[:], ACT.Sqrt).then_inc(std_done, 1)
            for i in range(NT):
                act.wait_ge(transposed, i + 1)
                nc.scalar.activation(xnT[:, :, i * TT:(i + 1) * TT],
                                     ps[:, i % 2, 0:KC * TT].rearrange("p (k t) -> p k t", k=KC),
                                     ACT.Copy).then_inc(xnT_done, 1)
            act.wait_ge(pad_zeroed, 1)
            act.wait_ge(loaded, 16 * (N_LOADS - 1))

            def evacuate(c):
                for g in range(G):
                    act.wait_ge(xb_mm, c + 1)
                    nc.scalar.activation(xpad[:, GB * g:GB * g + GB, TAPS - 1:],
                                         ps[:, g, 0:GL].rearrange("p (b t) -> p b t", b=GB),
                                         ACT.Copy).then_inc(padded, 1)

            def gates(c):
                act.wait_ge(z_mm, c + 1)
                act.wait_ge(z_stored, c * 16 + 1)
                nc.scalar.activation(zs[:].rearrange("p (g t) -> p g t", g=G), ps[:, G:2 * G, 0:GL],
                                     ACT.Silu).then_inc(z_done, 1)
                act.wait_ge(conv_done, c + 1)
                out = xb[:, bass.ds(c, 1)].rearrange("p a t -> p (a t)")
                nc.scalar.activation(out, acc[:, 0], ACT.Silu,
                                     bias=cb[:, bass.ds(c, 1)]).then_inc(silu_done, 1)

            with act.Fori(0, CC) as c:
                evacuate(c)
                gates(c)
            for c in range(CC):
                q, a = 4 * (c % 2), acc[:, c % 2]
                av = a.rearrange("p (g t) -> p g t", g=G)
                act.wait_ge(dt_mm, c + 1)
                if c >= 2:
                    act.wait_ge(dt_stored[c % 2], 16 * (c // 2))
                    act.wait_ge(u_done, c - 1)
                nc.scalar.activation(av, ps[:, q:q + 4, 0:GL], ACT.Abs, bias=bdt[:, c:c + 1]).then_inc(soft_step, 1)
                act.wait_ge(soft_step, 2 * c + 1)
                nc.scalar.activation(a, a, ACT.Exp, scale=-1.0).then_inc(soft_step, 1)
                act.wait_ge(soft_step, 2 * c + 2)
                nc.scalar.activation(a, a, ACT.Ln, bias=1.0).then_inc(ln_done, 1)

        @block.tensor
        def _(pe):
            pe.wait_ge(loaded, 16 * (N_LOADS - 1))
            for i in range(NT):
                pe.wait_ge(xn_done, i + 1)
                if i >= 2:
                    pe.wait_ge(xnT_done, i - 1)
                for k in range(KC):
                    ins = nc.tensor.transpose(ps[:, i % 2, k * TT:(k + 1) * TT], xn[:, i % 2, k * P:(k + 1) * P],
                                              ident[0:TT, 0:TT])
                ins.then_inc(transposed, 1)
            pe.wait_ge(xnT_done, NT)
            with pe.Fori(0, CC) as c:
                for half, done in ((0, xb_mm), (1, z_mm)):
                    pe.wait_ge(w_in_loaded[half], c * 16 + 16)
                    pe.wait_ge(padded if half == 0 else z_done, c * G + 1 if half == 0 else c + 1)
                    for g in range(G):
                        for k in range(KC):
                            ins = nc.tensor.matmul(ps[:, G * half + g, 0:GL], win[:, half, k], xnT[:, k, g * GL:(g + 1) * GL],
                                                   start=(k == 0), stop=(k == KC - 1))
                    ins.then_inc(done, 1)
            pe.wait_ge(silu_done, CC + 1)
            pe.wait_ge(z_done, CC + 1)
            for g in range(G):
                for c in range(CC):
                    ins = nc.tensor.matmul(ps[0:XR, g, 0:GL], wx[:, c], xb[:, c, g * GL:(g + 1) * GL],
                                           start=(c == 0), stop=(c == CC - 1))
            ins.then_inc(xdbl_mm, 1)
            pe.wait_ge(xdbl_done, 1)
            for c in range(CC):
                if c >= 2:
                    pe.wait_ge(dt_done, c - 1)
                for g in range(G):
                    ins = nc.tensor.matmul(ps[:, 4 * (c % 2) + g, 0:GL], wdt[:, c * P:(c + 1) * P],
                                           xdbl[0:R, g * GL:(g + 1) * GL], start=True, stop=True)
                ins.then_inc(dt_mm, 1)


def state_space(nc, A_log, D, ident_in, xb_d, z_d, dt_d, u_d, bc_d, y_d):
    ctx = ExitStack()
    with ctx:
        def sb(name, shape, dt=F32):
            return ctx.enter_context(nc.sbuf_tensor("s_" + name, shape, dt))

        def sem(name):
            return ctx.enter_context(nc.semaphore("s_" + name))

        ident = sb("ident", [P, P])
        A = sb("A", [P, CC, NS])
        Dv = sb("D", [P, CC])
        Bc = sb("Bc", [P, NS, GL])
        Cc = sb("Cc", [P, 2, NS, GL])
        decay = sb("decay", [P, DBUF, HS, GL])
        h = sb("h", [P, HBUF, HS, GL])
        early = sb("early", [P, 2, 2, GL])
        late = sb("late", [P, 2, 2, GL])
        y1 = sb("y1", [P, 2, GL])
        y = sb("y", [P, 2, GL])
        ps = ctx.enter_context(nc.psum_tensor("s_ps", [P, 2, 512], F32))

        consts = sem("consts")
        a_step, a_done = sem("a_step"), sem("a_done")
        b_loaded = sem("b_loaded")
        c_loaded = [sem("c_loaded0"), sem("c_loaded1")]
        early_loaded = [sem("early_loaded0"), sem("early_loaded1")]
        late_loaded = [sem("late_loaded0"), sem("late_loaded1")]
        y_stored = [sem("y_stored0"), sem("y_stored1")]
        edge_done = sem("edge_done")
        decay_done, ub_done, scan_done, hc_done, sum_done, y1_done, y_done = (
            sem(n) for n in ("decay_done", "ub_done", "scan_done", "hc_done", "sum_done", "y1_done", "y_done"))
        block = ctx.enter_context(nc.Block())

        UNITS = 2 * CC

        def unit(gg, pair, n):
            return gg * (2 * UNITS) + (pair * UNITS + n)

        def chunk(gg, pair, n):
            return gg * (2 * CC) + (pair * CC + n)

        def cols(t, gg, pair):
            return t[:, bass.ds(gg * (2 * GL) + pair * GL, GL)]

        def wait_slot(eng, loaded, gg, pair, c, dmas):
            eng.wait_ge(loaded[c % 2], gg * (16 * dmas * CC) + 16 * dmas * ((pair * CC + c) // 2 + 1))

        @block.sync
        def _(sp):
            sp.dma_start(ident[:], ident_in).then_inc(consts, 16)
            sp.dma_start(A[:], A_log.rearrange("(c p) n -> p c n", p=P)).then_inc(consts, 16)
            sp.dma_start(Dv[:], D).then_inc(consts, 16)
            with sp.Fori(0, G // 2) as gg:
                for pair in range(2):
                    for c in range(CC):
                        sp.wait_ge(decay_done, unit(gg, pair, 2 * c + 1))
                        sp.wait_ge(ub_done, unit(gg, pair, 2 * c + 1))
                        for j, src in enumerate((dt_d, u_d)):
                            sp.dma_start(early[:, c % 2, j], cols(src[c], gg, pair)).then_inc(early_loaded[c % 2], 16)
                        if c == 0:
                            sp.wait_ge(ub_done, unit(gg, pair, UB_FREE))
                            sp.dma_start(Bc[:], cols(bc_d[0:NS], gg, pair).partition_broadcast(P)).then_inc(b_loaded, 16)

        @block.gpsimd
        def _(pool):
            nc.gpsimd.sem_inc(ub_done, UB_FREE)
            with pool.Fori(0, G // 2) as gg:
                for pair in range(2):
                    for c in range(CC):
                        wait_slot(pool, early_loaded, gg, pair, c, 2)
                        if c == 0:
                            pool.wait_ge(b_loaded, gg * 32 + pair * 16 + 16)
                        for s in range(2):
                            pool.wait_ge(sum_done, unit(gg, pair, 2 * c + s + 1))
                            u = early[:, c % 2, 1].unsqueeze(1).to_broadcast([P, HS, GL])
                            nc.gpsimd.tensor_tensor(h[:, (2 * c + s) % HBUF], Bc[:, s * HS:(s + 1) * HS], u,
                                                    ALU.mult).then_inc(ub_done, 1)

        @block.scalar
        def _(act):
            act.sem_inc(decay_done, UB_FREE)
            for s in y_stored:
                act.sem_inc(s, 1)
            act.wait_ge(consts, 48)
            nc.scalar.activation(A[:], A[:], ACT.Exp).then_inc(a_step, 1)
            act.wait_ge(a_step, 1)
            nc.scalar.activation(A[:], A[:], ACT.Copy, scale=-1.0).then_inc(a_done, 1)
            act.wait_ge(a_done, 1)

            def store(gg, pair, c):
                act.wait_ge(y_done, chunk(gg, pair, c + 3))
                act.dma_start(cols(y_d[c], gg, pair), y[:, c % 2]).then_inc(y_stored[c % 2], 16)

            with act.Fori(0, G // 2) as gg:
                for pair in range(2):
                    act.wait_ge(hc_done, unit(gg, pair, 1))
                    act.dma_start(Cc[:, pair], cols(bc_d[NS:], gg, pair).partition_broadcast(P)).then_inc(c_loaded[pair], 16)
                    for c in range(CC):
                        wait_slot(act, early_loaded, gg, pair, c, 2)
                        for s in range(2):
                            act.wait_ge(scan_done, unit(gg, pair, 2 * c + s + 1))
                            for n in range(HS):
                                ins = nc.scalar.activation(decay[:, s, n], early[:, c % 2, 0], ACT.Exp,
                                                           scale=A[:, c, s * HS + n:s * HS + n + 1])
                            ins.then_inc(decay_done, 1)
                        act.wait_ge(y_done, chunk(gg, pair, c + 1))
                        for j, src in enumerate((xb_d, z_d)):
                            act.dma_start(late[:, c % 2, j], cols(src[c], gg, pair)).then_inc(late_loaded[c % 2], 16)
                        if c >= 2:
                            store(gg, pair, c - 2)
                    store(gg, pair, CC - 2)
                    store(gg, pair, CC - 1)
            for s in y_stored:
                act.wait_ge(s, 16 * G * CC // 2 + 1)

        @block.vector
        def _(dve):
            def outputs(gg, pair, c):
                wait_slot(dve, late_loaded, gg, pair, c, 2)
                dve.wait_ge(sum_done, unit(gg, pair, 2 * c + 2 + HBUF))
                nc.vector.scalar_tensor_tensor(out=y1[:, c % 2], in0=late[:, c % 2, 0], scalar=Dv[:, c:c + 1],
                                               in1=ps[:, c % 2, 0:GL], op0=ALU.mult, op1=ALU.add).then_inc(y1_done, 1)
                dve.wait_ge(y1_done, chunk(gg, pair, c + 3))
                dve.wait_ge(y_stored[c % 2], gg * (16 * CC) + (16 * ((pair * CC + c) // 2) + 1))
                nc.vector.tensor_tensor(y[:, c % 2], y1[:, c % 2], late[:, c % 2, 1], ALU.mult).then_inc(y_done, 1)

            dve.sem_inc(scan_done, DBUF)
            dve.sem_inc(hc_done, UNITS + 1)
            dve.sem_inc(y1_done, 2)
            dve.sem_inc(y_done, 2)
            dve.wait_ge(consts, 48)
            with dve.Fori(0, G // 2) as gg:
                for pair in range(2):
                    for n in range(UNITS):
                        c, s, buf = n // 2, n % 2, n % HBUF
                        dve.wait_ge(decay_done, unit(gg, pair, n + 1 + UB_FREE))
                        nc.vector.memset(decay[:, s].rearrange("p n (b t) -> p (n b) t", b=GB)[:, :, 0:1],
                                         0.0).then_inc(edge_done, 1)
                        dve.wait_ge(edge_done, unit(gg, pair, n + 1))
                        dve.wait_ge(ub_done, unit(gg, pair, n + 1 + UB_FREE))
                        hv = h[:, buf].rearrange("p n t -> p (n t)")
                        nc.vector.tensor_tensor_scan(hv, decay[:, s].rearrange("p n t -> p (n t)"), hv, 0.0,
                                                     ALU.mult, ALU.add).then_inc(scan_done, 1)
                        dve.wait_ge(scan_done, unit(gg, pair, n + 1 + DBUF))
                        if n == 0:
                            dve.wait_ge(c_loaded[pair], gg * 16 + 16)
                        nc.vector.tensor_tensor(h[:, buf], h[:, buf], Cc[:, pair, s * HS:(s + 1) * HS],
                                                ALU.mult).then_inc(hc_done, 1)
                        if s == 1 and c >= 1:
                            outputs(gg, pair, c - 1)
                    outputs(gg, pair, CC - 1)

        @block.tensor
        def _(pe):
            pe.sem_inc(sum_done, HBUF)
            pe.wait_ge(consts, 48)
            with pe.Fori(0, G // 2) as gg:
                for pair in range(2):
                    for c in range(CC):
                        pe.wait_ge(y1_done, chunk(gg, pair, c + 1))
                        for s in range(2):
                            pe.wait_ge(hc_done, unit(gg, pair, 2 * c + s + 2 + UNITS))
                            for n in range(HS):
                                ins = nc.tensor.matmul(ps[:, c % 2, 0:GL], ident[:], h[:, (2 * c + s) % HBUF, n],
                                                       start=(s == 0 and n == 0), stop=(s == 1 and n == HS - 1))
                            ins.then_inc(sum_done, 1)


def attention(nc, x, ctx_in, y_d, W_out, Wq, bq, Wk, bk, Wv, bv, Wo, bo, rW1, rb1, rW2, rb2, ident_in,
              x2_d, xn_d, logits_d):
    ctx = ExitStack()
    ITEMS = 2 * HEADS
    with ctx:
        def sb(name, shape, dt=F32):
            return ctx.enter_context(nc.sbuf_tensor("t_" + name, shape, dt))

        def sem(name):
            return ctx.enter_context(nc.semaphore("t_" + name))

        ident = sb("ident", [P, P])
        wout, wq, wk, wv = sb("wout", [P, CC, DM]), sb("wq", [P, KC, DM]), sb("wk", [P, CK, DM]), sb("wv", [P, CK, DM])
        wo, rw1, rw2 = sb("wo", [P, KC, DM]), sb("rw1", [P, KC, RH]), sb("rw2", [P, RC, E])
        bqc, bkc, rb1c = sb("bqc", [P, KC]), sb("bkc", [P, KC]), sb("rb1c", [P, RC])
        bvr, bor, rb2r = sb("bvr", [P, DM]), sb("bor", [P, DM]), sb("rb2r", [P, E])
        gT = sb("gT", [P, CC, L])
        xt = sb("xt", [TT, 2, DM])
        cx = sb("cx", [CT, NC, CD])
        cxT = sb("cxT", [P, CK, CTX])
        kT = sb("kT", [P, KC, CTX])
        v = sb("v", [CT, NC, DM])
        qz = sb("qz", [P, HEADS, L])
        x1 = sb("x1", [TT, 2, DM])
        xn = sb("xn", [TT, 2, DM])
        xnT = sb("xnT", [P, KC, L])
        probs = sb("probs", [TT, 3, CTX])
        pT = sb("pT", [CT, 2, 4, NC, L])
        oT = sb("oT", [P, KC, L])
        rh = sb("rh", [P, RC, L])
        lg = sb("lg", [TT, 2, E])
        st, mv, rstd = sb("st", [TT, 4, 6]), sb("mv", [TT, 4, 2]), sb("rstd", [TT, 2, 2])
        nmax, rsum, rinv = sb("nmax", [TT, ITEMS]), sb("rsum", [TT, ITEMS]), sb("rinv", [TT, ITEMS])
        ps = ctx.enter_context(nc.psum_tensor("t_ps", [P, 8, 512], F32))

        S = {n: sem(n) for n in (
            "consts g_loaded x_loaded ctx_loaded q_zeroed "
            "ctx_mm ctxT_done out_mm x1_done stat stat_seen mv_done var_done std_done rstd_done xn_done xn_mm xnT_done "
            "k_mm k_done v_mm v_done q_mm q_done score_mm max_done exp_done rinv_done norm_done turn_mm turn_done "
            "pv_mm o_done wo_mm x1b_done x2_done x2_stored xn_stored rh_mm rh_done lg_mm lg_done lg_stored").split()}
        N_CONST = 14

        def start(eng, names):
            for name in names.split():
                eng.sem_inc(S[name], 1)

        def wait(eng, name, n):
            eng.wait_ge(S[name], n + 1)

        block = ctx.enter_context(nc.Block())

        @block.sync
        def _(sp):
            start(sp, "consts ctx_loaded g_loaded x_loaded x2_stored xn_stored lg_stored")

            def const(dst, src):
                sp.dma_start(dst, src).then_inc(S["consts"], 16)

            def rows(w):
                return w.rearrange("(k p) n -> p k n", p=P)

            const(ident[:], ident_in)
            const(wout[:], rows(W_out))
            for dst, src in ((wk, Wk), (wv, Wv), (wq, Wq), (wo, Wo), (rw1, rW1), (rw2, rW2)):
                const(dst[:], rows(src))
            for dst, src in ((bqc, bq), (bkc, bk), (rb1c, rb1)):
                const(dst[:], src)
            for dst, src in ((bvr, bv), (bor, bo), (rb2r, rb2)):
                const(dst[:], src.partition_broadcast(P))

            def loads(b, used):
                if used is not None:
                    wait(sp, "ctx_mm", used * 2)
                sp.dma_start(cx[:], ctx_in[bass.ds(b, 1)].rearrange("a (i p) d -> p (a i) d", p=CT)).then_inc(S["ctx_loaded"], 16)
                if used is not None:
                    wait(sp, "out_mm", used * 2)
                sp.dma_start(gT[:], y_d[:, :, bass.ds(b * L, L)].rearrange("c p t -> p c t")).then_inc(S["g_loaded"], 16)
                if used is not None:
                    wait(sp, "x1_done", used * 2)
                sp.dma_start(xt[:], x[bass.ds(b, 1)].rearrange("a (u p) d -> p (a u) d", p=TT)).then_inc(S["x_loaded"], 16)

            def stores(b):
                for done, n, dst, src, stored in (("x2_done", 2, x2_d, x1, "x2_stored"), ("xn_done", 4, xn_d, xn, "xn_stored"),
                                                  ("lg_done", 2, logits_d, lg, "lg_stored")):
                    wait(sp, done, b * n + n)
                    sp.dma_start(dst[bass.ds(b, 1)].rearrange("a p u d -> p (a u) d"), src[:]).then_inc(S[stored], 16)

            loads(0, None)
            with sp.Fori(0, B - 1) as b:
                loads(b + 1, b + 1)
                stores(b)
            stores(B - 1)
            for stored in ("x2_stored", "xn_stored", "lg_stored"):
                wait(sp, stored, 16 * B)

        @block.gpsimd
        def _(pool):
            start(pool, "q_zeroed x1b_done")

            nc.gpsimd.memset(qz[:], 0.0).then_inc(S["q_zeroed"], 1)
            wait(pool, "consts", 16 * N_CONST)
            with pool.Fori(0, B) as b:
                for u in range(2):
                    wait(pool, "xn_done", b * 4 + u + 1)
                    nc.gpsimd.tensor_tensor(x1[:, u], x1[:, u], bor[0:TT], ALU.add).then_inc(S["x1b_done"], 1)

        @block.vector
        def _(dve):
            start(dve, "stat stat_seen mv_done var_done rstd_done xn_done max_done rinv_done norm_done o_done x1_done "
                  "v_done q_done x2_done lg_done")

            def norm(b, which):
                for u in range(2):
                    i = 2 * which + u
                    wait(dve, "x2_done" if which else "x1_done", b * 2 + u + 1)
                    nc.vector.bn_stats(st[:, i], x1[:, u]).then_inc(S["stat"], 1)
                    wait(dve, "stat", b * 4 + i + 1)
                    dve.sem_inc(S["stat_seen"])
                    nc.vector.bn_aggr(mv[:, i], st[:, i]).then_inc(S["mv_done"], 1)
                wait(dve, "mv_done", b * 4 + 2 * which + 2)
                r = rstd[:, which]
                nc.vector.tensor_scalar(r, mv[:, 2 * which:2 * which + 2, 1], EPS, None, ALU.add).then_inc(S["var_done"], 1)
                wait(dve, "std_done", b * 2 + which + 1)
                nc.vector.reciprocal(r, r).then_inc(S["rstd_done"], 1)
                wait(dve, "rstd_done", b * 2 + which + 1)
                if which == 0:
                    wait(dve, "xn_stored", b * 16)
                else:
                    wait(dve, "xn_mm", b * 4 + 2)
                for u in range(2):
                    i = 2 * which + u
                    nc.vector.tensor_scalar(xn[:, u], x1[:, u], mv[:, i, 0:1], rstd[:, which, u:u + 1],
                                            ALU.subtract, ALU.mult).then_inc(S["xn_done"], 1)

            def negative_max(b, n):
                wait(dve, "score_mm", b * ITEMS + n + 1)
                nc.vector.tensor_reduce(nmax[:, n:n + 1], ps[0:TT, 2 * (n % 2):2 * (n % 2) + 2, 0:HALF], AX.XY, ALU.max,
                                        negate=True).then_inc(S["max_done"], 1)

            def normalise(b, n):
                wait(dve, "exp_done", b * ITEMS + n + 1)
                nc.vector.reciprocal(rinv[:, n:n + 1], rsum[:, n:n + 1]).then_inc(S["rinv_done"], 1)
                wait(dve, "rinv_done", b * ITEMS + n + 1)
                nc.vector.tensor_scalar(probs[:, n % 3], probs[:, n % 3], rinv[:, n:n + 1], None,
                                        ALU.mult).then_inc(S["norm_done"], 1)

            def outputs(b, j):
                wait(dve, "pv_mm", b * KC + j + 1)
                nc.vector.tensor_copy(oT[:, j], ps[:, 6 + j % 2, 0:L]).then_inc(S["o_done"], 1)

            wait(dve, "consts", 16 * N_CONST)
            wait(dve, "q_zeroed", 1)
            with dve.Fori(0, B) as b:
                wait(dve, "x_loaded", b * 16 + 16)
                wait(dve, "x2_stored", b * 16)
                for u in range(2):
                    wait(dve, "out_mm", b * 2 + u + 1)
                    nc.vector.tensor_tensor(x1[:, u], ps[0:TT, 4 + u], xt[:, u], ALU.add).then_inc(S["x1_done"], 1)
                norm(b, 0)
                for i in range(NC):
                    wait(dve, "v_mm", b * NC + i + 1)
                    nc.vector.tensor_tensor(v[:, i], ps[0:CT, 4 + i % 2], bvr[0:CT], ALU.add).then_inc(S["v_done"], 1)
                for j in range(KC):
                    wait(dve, "q_mm", b * KC + j + 1)
                    for r in range(4):
                        rows = slice(DK * r, DK * r + DK)
                        ins = nc.vector.tensor_scalar(qz[rows, 4 * j + r], ps[rows, 4 + j % 2, 0:L], bqc[rows, j:j + 1],
                                                      float(DK) ** -0.5, ALU.add, ALU.mult)
                    ins.then_inc(S["q_done"], 1)
                negative_max(b, 0)
                for n in range(ITEMS):
                    if n + 1 < ITEMS:
                        negative_max(b, n + 1)
                    normalise(b, n)
                    if n >= 8 and n % 8 == 3:
                        outputs(b, n // 8 - 1)
                outputs(b, KC - 1)
                for u in range(2):
                    wait(dve, "wo_mm", b * 2 + u + 1)
                    wait(dve, "x1b_done", b * 2 + u + 1)
                    nc.vector.tensor_tensor(x1[:, u], ps[0:TT, 4 + u], x1[:, u], ALU.add).then_inc(S["x2_done"], 1)
                norm(b, 1)
                for u in range(2):
                    wait(dve, "lg_stored", b * 16)
                    wait(dve, "lg_mm", b * 2 + u + 1)
                    nc.vector.tensor_tensor(lg[:, u], ps[0:TT, 6 + u, 0:E], rb2r[0:TT], ALU.add).then_inc(S["lg_done"], 1)

        @block.scalar
        def _(act):
            start(act, "std_done xnT_done exp_done turn_done ctxT_done k_done rh_done")

            def deviation(b, which):
                wait(act, "var_done", b * 2 + which + 1)
                nc.scalar.activation(rstd[:, which], rstd[:, which], ACT.Sqrt).then_inc(S["std_done"], 1)

            def turned_norm(b, which):
                for u in range(2):
                    wait(act, "xn_mm", b * 4 + 2 * which + u + 1)
                    nc.scalar.activation(xnT[:, :, u * TT:(u + 1) * TT],
                                         ps[:, 6 + u, 0:KC * TT].rearrange("p (k t) -> p k t", k=KC),
                                         ACT.Copy).then_inc(S["xnT_done"], 1)

            def exponentials(b, n):
                wait(act, "max_done", b * ITEMS + n + 1)
                wait(act, "turn_mm", b * ITEMS + max(n - 2, 0))
                nc.scalar.activation(probs[:, n % 3].rearrange("p (a c) -> p a c", a=2),
                                     ps[0:TT, 2 * (n % 2):2 * (n % 2) + 2, 0:HALF], ACT.Exp, bias=nmax[:, n:n + 1],
                                     accum_out=rsum[:, n:n + 1]).then_inc(S["exp_done"], 1)

            def turned_probs(b, n):
                h, u = n // 2, n % 2
                j = h // 4
                wait(act, "turn_mm", b * ITEMS + n + 1)
                wait(act, "pv_mm", b * KC + max(j - 1, 0))
                nc.scalar.activation(pT[:, j % 2, h % 4, :, u * TT:(u + 1) * TT].rearrange("p (a i) t -> p a i t", a=2),
                                     ps[0:CT, 4:6, 0:3 * TT].rearrange("p a (i t) -> p a i t", i=3),
                                     ACT.Copy).then_inc(S["turn_done"], 1)

            wait(act, "consts", 16 * N_CONST)
            with act.Fori(0, B) as b:
                for k in range(CK):
                    wait(act, "ctx_mm", b * 2 + k + 1)
                    nc.scalar.activation(cxT[:, k].rearrange("p (a c) -> p a c", a=2),
                                         ps[:, 2 * k:2 * k + 2, 0:HALF], ACT.Copy).then_inc(S["ctxT_done"], 1)
                for j in range(KC):
                    if j == 2:
                        deviation(b, 0)
                    wait(act, "k_mm", b * KC + j + 1)
                    nc.scalar.activation(kT[:, j].rearrange("p (a c) -> p a c", a=2),
                                         ps[:, 2 * (j % 2):2 * (j % 2) + 2, 0:HALF], ACT.Identity,
                                         bias=bkc[:, j:j + 1]).then_inc(S["k_done"], 1)
                turned_norm(b, 0)
                exponentials(b, 0)
                for n in range(ITEMS):
                    if n + 1 < ITEMS:
                        exponentials(b, n + 1)
                    turned_probs(b, n)
                deviation(b, 1)
                turned_norm(b, 1)
                for c in range(RC):
                    wait(act, "rh_mm", b * RC + c + 1)
                    nc.scalar.activation(rh[:, c], ps[:, c % 4, 0:L], ACT.Gelu, bias=rb1c[:, c:c + 1]).then_inc(S["rh_done"], 1)

        @block.tensor
        def _(pe):
            start(pe, "xn_mm score_mm turn_mm pv_mm ctx_mm out_mm k_mm v_mm q_mm wo_mm rh_mm lg_mm")

            def turn_norm(b, which):
                for u in range(2):
                    wait(pe, "xn_done", b * 4 + 2 * which + u + 1)
                    if u == 0 and which == 0:
                        wait(pe, "lg_done", b * 2)
                    if u == 0 and which == 1:
                        wait(pe, "o_done", b * KC + KC)
                    for k in range(KC):
                        ins = nc.tensor.transpose(ps[:, 6 + u, k * TT:(k + 1) * TT], xn[:, u, k * P:(k + 1) * P],
                                                  ident[0:TT, 0:TT])
                    ins.then_inc(S["xn_mm"], 1)

            def scores(b, n):
                h, u = n // 2, n % 2
                wait(pe, "exp_done", b * ITEMS + max(n - 1, 0))
                for a in range(2):
                    ins = nc.tensor.matmul(ps[0:TT, 2 * (n % 2) + a, 0:HALF], qz[:, h, u * TT:(u + 1) * TT],
                                           kT[:, h // 4, a * HALF:(a + 1) * HALF], start=True, stop=True)
                ins.then_inc(S["score_mm"], 1)

            def turn_probs(b, n):
                wait(pe, "norm_done", b * ITEMS + n + 1)
                wait(pe, "turn_done", b * ITEMS + n)
                for i in range(NC):
                    ins = nc.tensor.transpose(ps[0:CT, 4 + i // 3, (i % 3) * TT:(i % 3 + 1) * TT],
                                              probs[:, n % 3, i * CT:(i + 1) * CT], ident[0:TT, 0:TT])
                ins.then_inc(S["turn_mm"], 1)

            def values(b, j):
                wait(pe, "turn_done", b * ITEMS + 8 * j + 8)
                wait(pe, "o_done", b * KC + max(j - 1, 0))
                for i in range(NC):
                    for r in range(4):
                        h = 4 * j + r
                        ins = nc.tensor.matmul(ps[DK * r:DK * r + DK, 6 + j % 2, 0:L], v[:, i, h * DK:(h + 1) * DK],
                                               pT[:, j % 2, r, i], start=(i == 0), stop=(i == NC - 1),
                                               tile_position=(0, DK * r))
                ins.then_inc(S["pv_mm"], 1)

            wait(pe, "consts", 16 * N_CONST)
            with pe.Fori(0, B) as b:
                wait(pe, "ctx_loaded", b * 16 + 16)
                wait(pe, "rh_done", b * RC)
                for k in range(CK):
                    for i in range(NC):
                        ins = nc.tensor.transpose(ps[:, 2 * k + i // 3, (i % 3) * CT:(i % 3 + 1) * CT],
                                                  cx[:, i, k * P:(k + 1) * P], ident[0:CT, 0:CT])
                    ins.then_inc(S["ctx_mm"], 1)
                wait(pe, "g_loaded", b * 16 + 16)
                wait(pe, "x2_done", b * 2)
                for u in range(2):
                    for c in range(CC):
                        ins = nc.tensor.matmul(ps[0:TT, 4 + u], gT[:, c, u * TT:(u + 1) * TT], wout[:, c],
                                               start=(c == 0), stop=(c == CC - 1))
                    ins.then_inc(S["out_mm"], 1)
                for j in range(KC):
                    if j < 2:
                        wait(pe, "ctxT_done", b * CK + CK)
                    else:
                        wait(pe, "k_done", b * KC + j - 1)
                    for a in range(2):
                        for k in range(CK):
                            ins = nc.tensor.matmul(ps[:, 2 * (j % 2) + a, 0:HALF], wk[:, k, j * P:(j + 1) * P],
                                                   cxT[:, k, a * HALF:(a + 1) * HALF], start=(k == 0), stop=(k == CK - 1))
                    ins.then_inc(S["k_mm"], 1)
                for i in range(NC):
                    if i < 2:
                        wait(pe, "x1_done", b * 2 + 2)
                    else:
                        wait(pe, "v_done", b * NC + i - 1)
                    for k in range(CK):
                        ins = nc.tensor.matmul(ps[0:CT, 4 + i % 2], cxT[:, k, i * CT:(i + 1) * CT], wv[:, k],
                                               start=(k == 0), stop=(k == CK - 1))
                    ins.then_inc(S["v_mm"], 1)
                turn_norm(b, 0)
                wait(pe, "xnT_done", b * 4 + 2)
                for j in range(KC):
                    if j < 2:
                        wait(pe, "v_done", b * NC + NC)
                    else:
                        wait(pe, "q_done", b * KC + j - 1)
                    for k in range(KC):
                        ins = nc.tensor.matmul(ps[:, 4 + j % 2, 0:L], wq[:, k, j * P:(j + 1) * P], xnT[:, k],
                                               start=(k == 0), stop=(k == KC - 1))
                    ins.then_inc(S["q_mm"], 1)
                wait(pe, "k_done", b * KC + KC)
                wait(pe, "q_done", b * KC + KC)
                scores(b, 0)
                scores(b, 1)
                for n in range(ITEMS):
                    if n + 2 < ITEMS:
                        scores(b, n + 2)
                    turn_probs(b, n)
                    if n >= 8 and n % 8 == 1:
                        values(b, n // 8 - 1)
                values(b, KC - 1)
                wait(pe, "o_done", b * KC + KC)
                for u in range(2):
                    for j in range(KC):
                        ins = nc.tensor.matmul(ps[0:TT, 4 + u], oT[:, j, u * TT:(u + 1) * TT], wo[:, j],
                                               start=(j == 0), stop=(j == KC - 1))
                    ins.then_inc(S["wo_mm"], 1)
                turn_norm(b, 1)
                wait(pe, "xnT_done", b * 4 + 4)
                for c in range(RC):
                    if c >= 4:
                        wait(pe, "rh_done", b * RC + c - 3)
                    for k in range(KC):
                        ins = nc.tensor.matmul(ps[:, c % 4, 0:L], rw1[:, k, c * P:(c + 1) * P], xnT[:, k],
                                               start=(k == 0), stop=(k == KC - 1))
                    ins.then_inc(S["rh_mm"], 1)
                wait(pe, "rh_done", b * RC + RC)
                for u in range(2):
                    for c in range(RC):
                        ins = nc.tensor.matmul(ps[0:TT, 6 + u, 0:E], rh[:, c, u * TT:(u + 1) * TT], rw2[:, c],
                                               start=(c == 0), stop=(c == RC - 1))
                    ins.then_inc(S["lg_mm"], 1)


def experts(nc, We1, be1, We2, be2, upper_in, ident_in, tile_starts_in, x2_d, xn_d, logits_d, xs_d, out):
    ctx = ExitStack()
    PAIRS = [(a, b) for a in range(E) for b in range(a + 1, E)]
    with ctx:
        def sb(name, shape, dt=F32):
            return ctx.enter_context(nc.sbuf_tensor("e_" + name, shape, dt))

        def sem(name):
            return ctx.enter_context(nc.semaphore("e_" + name))

        w1, w2 = sb("w1", [P, 2, KC, H]), sb("w2", [P, 2, HC, DM])
        b1, b2 = sb("b1", [P, E * HC]), sb("b2", [P, E, DM])
        ident, upper, ones = sb("ident", [P, P]), sb("upper", [TT, TT]), sb("ones", [TT, TT])
        starts = sb("starts", [1, ET])
        lg, p, m, pm = (sb(n, [TT, NT, E]) for n in ("lg", "p", "m", "pm"))
        mx, total = sb("mx", [TT, NT]), sb("total", [TT, NT])
        ge = sb("ge", [TT, len(PAIRS), NT])
        r = sb("r", [TT, 2, NT])
        incl, slot, tmp, eq = (sb(n, [TT, NT, E]) for n in ("incl", "slot", "tmp", "eq"))
        choice = sb("choice", [TT, 2, NT])
        gate = sb("gate", [TT, 2, NT])
        index = sb("index", [TT, 2, NT], I32)
        taken = sb("taken", [1, E, ET])
        tiles = sb("tiles", [1, 4, E + 1])
        tiles_i = sb("tiles_i", [1, 4, E + 1], I32)
        parity = sb("parity", [1, 3, E])
        xt = sb("xt", [P, 2, DM])
        xT = sb("xT", [P, 2, KC, P])
        hT = sb("hT", [P, HC, P])
        y = sb("y", [P, 2, DM])
        buf = sb("buf", [TT, 3, 2, DM])
        obuf = sb("obuf", [TT, 3, DM])
        ps = ctx.enter_context(nc.psum_tensor("e_ps", [P, 8, 512], F32))

        S = {n: sem(n) for n in (
            "consts lg_loaded step ones_set exped rank_mm slots_done tiles_done "
            "scattered results_seen combined x_mm xT_done h_mm h_done y_mm y_done").split()}
        w_loaded = [sem(f"w_loaded{i}") for i in range(E)]
        n_loaded = [sem(f"n_loaded{i}") for i in range(3)]
        n_scattered = [sem(f"n_scattered{i}") for i in range(3)]
        x_loaded = [sem("x_loaded0"), sem("x_loaded1")]
        y_stored = [sem("y_stored0"), sem("y_stored1")]
        r_loaded = [sem(f"r_loaded{i}") for i in range(3)]
        r_gathered = [sem(f"r_gathered{i}") for i in range(3)]
        out_stored = [sem(f"out_stored{i}") for i in range(3)]

        def start(eng, names):
            for name in names.split():
                eng.sem_inc(S[name], 1)

        def wait(eng, name, n):
            eng.wait_ge(S[name], n + 1)

        block = ctx.enter_context(nc.Block())
        N_CONST = 5
        xs_v = xs_d.rearrange("(e i p) d -> e i p d", e=E, p=P)
        out_v = out.rearrange("b (u p) d -> (b u) p d", p=TT)
        xn_v = xn_d.rearrange("b p u d -> b u p d")
        x2_v = x2_d.rearrange("b p u d -> b u p d")

        STEPS_TO_MASK = 5 + len(PAIRS) + E * (len(PAIRS) * 2 // E + 1)

        def counts(eng, e):
            return [eng.value_load(tiles_i[0:1, j, e:e + 1], min_val=0, max_val=E * ET) for j in range(4)]

        def totals(eng):
            return [eng.value_load(tiles_i[0:1, j, E:E + 1], min_val=0, max_val=E * ET) for j in (2, 3)]

        def expert_tiles(eng, e, body):
            taken_e, before, *before_k = counts(eng, e)
            with eng.Fori(0, ET // 2) as half:
                for k in range(2):
                    i = half * 2 + k
                    with eng.If(i < taken_e):
                        body(i, before + i, k, before_k[k] + half)

        @block.sync
        def _(sp):
            start(sp, "lg_loaded consts")

            sp.dma_start(lg[:].rearrange("p (b u) e -> p b u e", u=2), logits_d.rearrange("b p u e -> p b u e")).then_inc(S["lg_loaded"], 16)

            def weights(e):
                sp.dma_start(w1[:, e % 2], We1[e].rearrange("(k p) n -> p k n", p=P)).then_inc(w_loaded[e], 16)
                sp.dma_start(w2[:, e % 2], We2[e].rearrange("(c p) n -> p c n", p=P)).then_inc(w_loaded[e], 16)

            for dst, src in ((ident[:], ident_in), (upper[:], upper_in), (starts[:], tile_starts_in), (b1[:], be1),
                             (b2[:], be2.partition_broadcast(P))):
                sp.dma_start(dst, src).then_inc(S["consts"], 16)
            for i in range(NT):
                if i >= 3:
                    sp.wait_ge(n_scattered[i % 3], 32 * (i // 3))
                sp.dma_start(buf[:, i % 3, 0], xn_v[i // 2, i % 2]).then_inc(n_loaded[i % 3], 16)
                if i == 2:
                    weights(0)
                    weights(1)
            wait(sp, "tiles_done", 1)
            wait(sp, "scattered", 1)
            for e in range(E):
                if e >= 2:
                    before = counts(sp, e - 1)[1]
                    wait(sp, "y_mm", before)
                    weights(e)

                def load(i, n, k, nk):
                    wait(sp, "x_mm", n)
                    sp.dma_start(xt[:, k], xs_v[e, bass.ds(i, 1)].rearrange("a p d -> (a p) d")).then_inc(x_loaded[k], 16)

                expert_tiles(sp, e, load)

        @block.gpsimd
        def _(pool):
            start(pool, "ones_set scattered results_seen")

            nc.gpsimd.memset(ones[:], 1.0).then_inc(S["ones_set"], 1)
            wait(pool, "slots_done", 2)
            for i in range(NT):
                pool.wait_ge(n_loaded[i % 3], 16 * (i // 3 + 1))
                for k in range(2):
                    pool.indirect_dma_start(
                        out=xs_d, out_offset=bass.IndirectOffsetOnAxis(ap=index[:, k, i:i + 1], axis=0),
                        in_=buf[:, i % 3, 0], in_offset=None).then_inc(n_scattered[i % 3], 16)
            for j in range(3):
                pool.wait_ge(n_scattered[j], 32 * len(range(j, NT, 3)))
            pool.sem_inc(S["scattered"], 1)

            wait(pool, "tiles_done", 1)
            last = totals(pool)
            for k in range(2):
                pool.wait_ge(y_stored[k], last[k] * 16 + 1)
            pool.sem_inc(S["results_seen"])
            for i in range(NT):
                j = i % 3
                if i >= 3:
                    wait(pool, "combined", 2 * (i - 3) + 2)
                for k in range(2):
                    pool.indirect_dma_start(
                        out=buf[:, j, k], out_offset=None, in_=xs_d,
                        in_offset=bass.IndirectOffsetOnAxis(ap=index[:, k, i:i + 1], axis=0)).then_inc(r_gathered[j], 16)

        @block.vector
        def _(dve):
            start(dve, "step slots_done tiles_done y_done combined")

            step = [0]

            def then(ins):
                step[0] += 1
                ins.then_inc(S["step"], 1)
                wait(dve, "step", step[0])

            def over_e(a):
                return a.unsqueeze(2).to_broadcast([TT, NT, E])

            v = nc.vector
            wait(dve, "lg_loaded", 16)
            then(v.tensor_reduce(mx[:], lg[:], AX.X, ALU.max))
            then(v.tensor_tensor(p[:], lg[:], over_e(mx[:]), ALU.subtract))
            wait(dve, "exped", 1)
            then(v.tensor_reduce(total[:], p[:], AX.X, ALU.add))
            then(v.reciprocal(total[:], total[:]))
            then(v.tensor_tensor(p[:], p[:], over_e(total[:]), ALU.mult))
            for n, (a, b) in enumerate(PAIRS):
                then(v.tensor_tensor(ge[:, n], p[:, :, a], p[:, :, b], ALU.is_ge))
            for e in range(E):
                lower = [n for n, (a, b) in enumerate(PAIRS) if b == e]
                higher = [n for n, (a, b) in enumerate(PAIRS) if a == e]
                terms = [(n, 1.0) for n in lower] + [(n, -1.0) for n in higher]
                then(v.tensor_scalar(r[:, 0], ge[:, terms[0][0]], terms[0][1], float(len(higher)), ALU.mult, ALU.add))
                for n, sign in terms[1:]:
                    then(v.scalar_tensor_tensor(out=r[:, 0], in0=ge[:, n], scalar=sign, in1=r[:, 0], op0=ALU.mult, op1=ALU.add))
                then(v.tensor_scalar(m[:, :, e], r[:, 0], 1.5, None, ALU.is_lt))
            then(v.tensor_tensor(pm[:], p[:], m[:], ALU.mult))
            wait(dve, "rank_mm", 1)
            for e in range(E):
                then(v.tensor_tensor_scan(incl[:, :, e], ones[:, 0:NT], ps[0:TT, 1, 0:NT * E].rearrange("p (i e) -> p i e", e=E)[:, :, e],
                                          0.0, ALU.mult, ALU.add))
            then(v.tensor_tensor(slot[:], incl[:], ps[0:TT, 1, 0:NT * E].rearrange("p (i e) -> p i e", e=E), ALU.subtract))
            then(v.tensor_tensor(slot[:], slot[:], ps[0:TT, 0, 0:NT * E].rearrange("p (i e) -> p i e", e=E), ALU.add))
            for e in range(E):
                then(v.tensor_scalar(slot[:, :, e], slot[:, :, e], float(e * SLOTS), None, ALU.add))
            FAR = float(E * SLOTS)
            then(v.tensor_scalar(tmp[:], slot[:], FAR, None, ALU.subtract))
            then(v.tensor_tensor(tmp[:], tmp[:], m[:], ALU.mult))
            then(v.tensor_reduce(choice[:, 0], tmp[:], AX.X, ALU.min))
            then(v.tensor_scalar(choice[:, 0], choice[:, 0], FAR, None, ALU.add))
            then(v.tensor_tensor(tmp[:], slot[:], m[:], ALU.mult))
            then(v.tensor_reduce(choice[:, 1], tmp[:], AX.X, ALU.max))
            for k in range(2):
                v.tensor_copy(index[:, k], choice[:, k]).then_inc(S["slots_done"], 1)
            for e in range(E):
                then(v.tensor_scalar(taken[:, e], starts[:], incl[0:1, NT - 1, e:e + 1], None, ALU.is_lt))
            pairs = taken[:].rearrange("a e (h k) -> a e h k", k=2)
            for j, src in enumerate((taken[:], pairs[:, :, :, 0], pairs[:, :, :, 1])):
                then(v.tensor_reduce(parity[:, j], src, AX.X, ALU.add))
            then(v.memset(tiles[:], 0.0))
            then(v.tensor_copy(tiles[:, 0, 0:E], parity[:, 0]))
            for e in range(E):
                then(v.tensor_tensor(tiles[:, 1:4, e + 1], tiles[:, 1:4, e], parity[:, :, e], ALU.add))
            v.tensor_copy(tiles_i[:], tiles[:]).then_inc(S["tiles_done"], 1)
            for k in range(2):
                then(v.tensor_tensor(eq[:], slot[:], over_e(choice[:, k]), ALU.is_equal))
                then(v.tensor_tensor(eq[:], eq[:], pm[:], ALU.mult))
                then(v.tensor_reduce(gate[:, k], eq[:], AX.X, ALU.add))
            wait(dve, "consts", 16 * N_CONST)
            wait(dve, "tiles_done", 1)
            for e in range(E):
                def results(i, n, k, nk):
                    wait(dve, "y_mm", n + 1)
                    dve.wait_ge(y_stored[k], nk * 16 + 1)
                    v.tensor_tensor(y[:, k], ps[:, 5 + k], b2[:, e], ALU.add).then_inc(S["y_done"], 1)

                expert_tiles(dve, e, results)
            for i in range(NT):
                j = i % 3
                dve.wait_ge(r_gathered[j], 32 * (i // 3 + 1))
                dve.wait_ge(r_loaded[j], 16 * (i // 3 + 1))
                for k in range(2):
                    v.scalar_tensor_tensor(out=obuf[:, j], in0=buf[:, j, k], scalar=gate[:, k, i:i + 1],
                                           in1=obuf[:, j], op0=ALU.mult, op1=ALU.add).then_inc(S["combined"], 1)
                    if k == 0:
                        wait(dve, "combined", 2 * i + 1)

        @block.scalar
        def _(act):
            start(act, "exped xT_done h_done")

            for s in y_stored:
                act.sem_inc(s, 1)
            wait(act, "step", 2)
            nc.scalar.activation(p[:], p[:], ACT.Exp).then_inc(S["exped"], 1)
            wait(act, "consts", 16 * N_CONST)
            wait(act, "tiles_done", 1)
            for e in range(E):
                def hidden(i, n, k, nk):
                    wait(act, "x_mm", n + 1)
                    nc.scalar.activation(xT[:, k].rearrange("p k t -> p (k t)"), ps[:, 0], ACT.Copy).then_inc(S["xT_done"], 1)
                    for c in range(HC):
                        wait(act, "h_mm", n * HC + c + 1)
                        nc.scalar.activation(hT[:, c], ps[:, 1 + c % 4, 0:P], ACT.Gelu,
                                             bias=b1[:, e * HC + c:e * HC + c + 1]).then_inc(S["h_done"], 1)
                    wait(act, "y_done", n + 1)
                    act.dma_start(xs_v[e, bass.ds(i, 1)].rearrange("a p d -> (a p) d"), y[:, k]).then_inc(y_stored[k], 16)

                expert_tiles(act, e, hidden)
            for i in range(NT):
                j = i % 3
                if i >= 3:
                    act.wait_ge(out_stored[j], 16 * (i // 3))
                act.dma_start(obuf[:, j], x2_v[i // 2, i % 2]).then_inc(r_loaded[j], 16)
                if i >= 2:
                    wait(act, "combined", 2 * (i - 2) + 2)
                    act.dma_start(out_v[i - 2], obuf[:, (i - 2) % 3]).then_inc(out_stored[(i - 2) % 3], 16)
            for i in range(NT - 2, NT):
                wait(act, "combined", 2 * i + 2)
                act.dma_start(out_v[i], obuf[:, i % 3]).then_inc(out_stored[i % 3], 16)
            for j in range(3):
                act.wait_ge(out_stored[j], 16 * len(range(j, NT, 3)))

        @block.tensor
        def _(pe):
            start(pe, "rank_mm x_mm h_mm y_mm")

            wait(pe, "consts", 16 * N_CONST)
            wait(pe, "ones_set", 1)
            wait(pe, "step", STEPS_TO_MASK)
            for bank, w in ((0, upper), (1, ones)):
                ins = nc.tensor.matmul(ps[0:TT, bank, 0:NT * E], w[:], m[:].rearrange("p i e -> p (i e)"), start=True, stop=True)
            ins.then_inc(S["rank_mm"], 1)
            wait(pe, "tiles_done", 1)
            for e in range(E):
                pe.wait_ge(w_loaded[e], 32)

                def tile(i, n, k, nk):
                    pe.wait_ge(x_loaded[k], nk * 16 + 16)
                    wait(pe, "xT_done", n)
                    for q in range(KC):
                        ins = nc.tensor.transpose(ps[:, 0, q * P:(q + 1) * P], xt[:, k, q * P:(q + 1) * P], ident[:])
                    ins.then_inc(S["x_mm"], 1)
                    wait(pe, "xT_done", n + 1)
                    for c in range(HC):
                        if c < 4:
                            wait(pe, "h_done", n * HC)
                        else:
                            wait(pe, "h_done", n * HC + c - 3)
                        for q in range(KC):
                            ins = nc.tensor.matmul(ps[:, 1 + c % 4, 0:P], w1[:, e % 2, q, c * P:(c + 1) * P], xT[:, k, q],
                                                   start=(q == 0), stop=(q == KC - 1))
                        ins.then_inc(S["h_mm"], 1)
                    wait(pe, "y_done", n)
                    for c in range(HC):
                        wait(pe, "h_done", n * HC + c + 1)
                        ins = nc.tensor.matmul(ps[:, 5 + k], hT[:, c], w2[:, e % 2, c], start=(c == 0), stop=(c == HC - 1))
                    ins.then_inc(S["y_mm"], 1)

                expert_tiles(pe, e, tile)


def decoder(nc, a, out):
    def scratch(name, shape):
        return nc.dram_tensor(name, shape, F32, kind="Internal").ap()

    xb_d, z_d, dt_d, u_d, y_d = (scratch(n, (CC, P, T)) for n in ("xb_d", "z_d", "dt_d", "u_d", "y_d"))
    bc_d = scratch("bc_d", (2 * NS, T))
    x2_d, xn_d, logits_d = (scratch(n, (B, TT, 2, w)) for n, w in (("x2_d", DM), ("xn_d", DM), ("logits_d", E)))
    xs_d = scratch("xs_d", (E * SLOTS, DM))
    s, t, f = "L0_attn_", "L0_xattn_", "L0_ffn_"
    mamba_in(nc, a["x"], a[s + "W_in"], a[s + "conv_w"], a[s + "conv_b"], a[s + "W_x"], a[s + "W_dt"], a[s + "b_dt"],
             a["identity"], xb_d, z_d, dt_d, u_d, bc_d, xs_d)
    state_space(nc, a[s + "A_log"], a[s + "D"], a["identity"], xb_d, z_d, dt_d, u_d, bc_d, y_d)
    attention(nc, a["x"], a["ctx_512"], y_d, a[s + "W_out"], a[t + "Wq"], a[t + "bq"], a[t + "Wk"], a[t + "bk"],
              a[t + "Wv"], a[t + "bv"], a[t + "Wo"], a[t + "bo"], a[f + "rW1"], a[f + "rb1"], a[f + "rW2"], a[f + "rb2"],
              a["identity"], x2_d, xn_d, logits_d)
    experts(nc, a[f + "We1"], a[f + "be1"], a[f + "We2"], a[f + "be2"], a["upper"], a["identity"], a["tile_starts"],
            x2_d, xn_d, logits_d, xs_d, out)


_INS = ["x", "ctx_512"] + ["L0_attn_" + n for n in ("W_in", "conv_w", "conv_b", "W_x", "W_dt", "b_dt", "A_log", "D", "W_out")] \
    + ["L0_xattn_" + n for n in ("Wq", "bq", "Wk", "bk", "Wv", "bv", "Wo", "bo")] \
    + ["L0_ffn_" + n for n in ("rW1", "rb1", "rW2", "rb2", "We1", "be1", "We2", "be2")]
_COLUMNS = ["L0_attn_conv_b", "L0_attn_b_dt", "L0_attn_D", "L0_xattn_bq", "L0_xattn_bk", "L0_ffn_rb1", "L0_ffn_be1"]


def kernel(**inputs):
    import numpy as np
    import concourse.bacc as bacc
    from concourse.bass_utils import run_bass_kernel_spmd

    arrays = {name: np.asarray(inputs[name]) for name in _INS}
    for name in _COLUMNS:
        arrays[name] = arrays[name].reshape(-1, P).T
    arrays["identity"] = np.eye(P, dtype=np.float32)
    arrays["upper"] = np.triu(np.ones((TT, TT), np.float32), 1)
    arrays["tile_starts"] = np.arange(0, SLOTS, P, dtype=np.float32)[None]
    arrays = {name: np.ascontiguousarray(a) for name, a in arrays.items()}

    nc = bacc.Bacc("TRN2", target_bir_lowering=False, num_devices=1)
    a = {name: nc.dram_tensor("in_" + name, v.shape, F32, kind="ExternalInput").ap() for name, v in arrays.items()}
    out = nc.dram_tensor("out", (B, L, DM), F32, kind="ExternalOutput").ap()
    decoder(nc, a, out)
    r = run_bass_kernel_spmd(nc, [{"in_" + name: v for name, v in arrays.items()}], core_ids=[0])
    return r.results[0]["out"]
```

```python
from contextlib import ExitStack

import concourse.bass as bass
from concourse import mybir

F32 = mybir.dt.float32
F32R = mybir.dt.float32r
I32 = mybir.dt.int32
U32 = mybir.dt.uint32
ALU = mybir.AluOpType
ACT = mybir.ActivationFunctionType
AX = mybir.AxisListType

P = 128
EPS = 1e-5

B, L, DM = 8, 224, 512
T = B * L
TT = 112
NT = T // TT
KC = DM // P
DI = 1024
CC = DI // P
TAPS = 4
R, NS = 64, 16
XR = R + 2 * NS
GB = 2
G = B // GB
GL = GB * L
HS = NS // 2
HBUF, DBUF = 4, 2
UB_FREE = 3
CTX, CD = 750, 256
CT = 125
NC = CTX // CT
CK = CD // P
HEADS, DK = 16, 32
HALF = CTX // 2
RH = 1024
RC = RH // P
E, H = 4, 2048
HC = H // P
SLOTS = T
GT = 2 * P
EG = SLOTS // GT
XS = (E * SLOTS // 512 + 1) * 512


def mamba_in(nc, x, W_in, conv_w, conv_b, W_x, W_dt, b_dt, ident_in, xb_d, z_d, dt_d, u_d, bc_d, xs_d):
    ctx = ExitStack()
    with ctx:
        def sb(name, shape, dt=F32):
            return ctx.enter_context(nc.sbuf_tensor("a_" + name, shape, dt))

        def sem(name):
            return ctx.enter_context(nc.semaphore("a_" + name))

        x_sb = sb("x", [TT, NT, DM])
        xn = sb("xn", [TT, 2, DM])
        xnT = sb("xnT", [P, KC, T])
        st = sb("st", [TT, NT, 6])
        mv = sb("mv", [TT, NT, 2])
        rstd = sb("rstd", [TT, NT])
        ident = sb("ident", [P, P])
        win = sb("win", [P, 2, KC, P])
        xpad = sb("xpad", [P, B, TAPS - 1 + L])
        acc = sb("acc", [P, 2, T])
        zs = sb("zs", [P, T])
        xb = sb("xb", [P, CC, T])
        cw = sb("cw", [P, CC, TAPS])
        cb = sb("cb", [P, CC])
        wx = sb("wx", [P, CC, XR])
        xdbl = sb("xdbl", [XR, T])
        wdt = sb("wdt", [R, DI])
        bdt = sb("bdt", [P, CC])
        zero = sb("zero", [P, 2048])
        ps = ctx.enter_context(nc.psum_tensor("a_ps", [P, 8, 512], F32))

        loaded = sem("loaded")
        w_in_loaded = [sem("xb_w_loaded"), sem("z_w_loaded")]
        stats_done, mv_done, var_done, std_done, rstd_done = (sem(n) for n in ("stats", "mv", "var", "std", "rstd"))
        xn_done, transposed, xnT_done = sem("xn_done"), sem("transposed"), sem("xnT_done")
        pad_zeroed, zero_set = sem("pad_zeroed"), sem("zero_set")
        xb_mm, z_mm, padded, conv_step, conv_done, silu_done, z_done = (
            sem(n) for n in ("xb_mm", "z_mm", "padded", "conv_step", "conv_done", "silu_done", "z_done"))
        z_stored, xb_stored, zero_stored = sem("z_stored"), sem("xb_stored"), sem("zero_stored")
        xdbl_mm, xdbl_done, xdbl_stored = sem("xdbl_mm"), sem("xdbl_done"), sem("xdbl_stored")
        dt_mm, ln_done, soft_step, relu_done, dt_done, u_done, u_stored = (
            sem(n) for n in ("dt_mm", "ln_done", "soft_step", "relu_done", "dt_done", "u_done", "u_stored"))
        dt_stored = [sem("dt_stored0"), sem("dt_stored1")]
        N_LOADS = 8

        win_v = W_in.rearrange("(k p) n -> p k n", p=P)
        block = ctx.enter_context(nc.Block())

        @block.sync
        def _(sp):
            sp.sem_inc(z_stored, 1)
            sp.dma_start(x_sb[:], x.rearrange("b (u p) d -> p (b u) d", p=TT)).then_inc(loaded, 16)
            sp.dma_start(ident[:], ident_in).then_inc(loaded, 16)
            sp.dma_start(cw[:], conv_w.rearrange("(c p) k -> p c k", p=P)).then_inc(loaded, 16)
            sp.dma_start(cb[:], conv_b).then_inc(loaded, 16)
            sp.dma_start(wx[:], W_x.rearrange("(c p) n -> p c n", p=P)).then_inc(loaded, 16)
            sp.dma_start(wdt[:], W_dt).then_inc(loaded, 16)
            sp.dma_start(bdt[:], b_dt).then_inc(loaded, 16)
            sp.dma_start(win[:, 0], win_v[:, :, 0:P]).then_inc(w_in_loaded[0], 16)
            sp.dma_start(win[:, 1], win_v[:, :, DI:DI + P]).then_inc(w_in_loaded[1], 16)
            with sp.Fori(0, CC - 1) as c:
                sp.wait_ge(xb_mm, c + 1)
                sp.dma_start(win[:, 0], win_v[:, :, bass.ds(c * P + P, P)]).then_inc(w_in_loaded[0], 16)
                sp.wait_ge(z_mm, c + 1)
                sp.dma_start(win[:, 1], win_v[:, :, bass.ds(c * P + (DI + P), P)]).then_inc(w_in_loaded[1], 16)
                sp.wait_ge(z_done, c + 2)
                sp.dma_start(z_d[bass.ds(c, 1)].rearrange("a p t -> (a p) t"), zs[:]).then_inc(z_stored, 16)
            sp.wait_ge(z_done, CC + 1)
            sp.dma_start(z_d[CC - 1], zs[:]).then_inc(z_stored, 16)
            sp.wait_ge(silu_done, CC + 1)
            sp.dma_start(xb_d.rearrange("c p t -> p c t"), xb[:]).then_inc(xb_stored, 16)
            sp.wait_ge(xdbl_done, 1)
            sp.dma_start(bc_d, xdbl[R:XR, :]).then_inc(xdbl_stored, 16)
            for c in range(CC):
                sp.wait_ge(dt_done, c + 1)
                sp.dma_start(dt_d[c], acc[:, c % 2]).then_inc(dt_stored[c % 2], 16)
                sp.wait_ge(u_done, c + 1)
                sp.dma_start(u_d[c], xb[:, c]).then_inc(u_stored, 16)
            sp.wait_ge(z_stored, 16 * CC + 1)
            sp.wait_ge(xb_stored, 16)
            sp.wait_ge(xdbl_stored, 16)
            for s in dt_stored:
                sp.wait_ge(s, 16 * CC // 2)
            sp.wait_ge(u_stored, 16 * CC)

        @block.gpsimd
        def _(pool):
            nc.gpsimd.memset(zero[:], 0.0).then_inc(zero_set, 1)
            pool.wait_ge(zero_set, 1)
            xs_v = xs_d.rearrange("(a p r) d -> a p (r d)", p=P, r=4)
            with pool.Fori(0, XS // (P * 4)) as a:
                pool.dma_start(xs_v[bass.ds(a, 1)].rearrange("a p n -> (a p) n"), zero[:]).then_inc(zero_stored, 16)
            for c in range(CC):
                pool.wait_ge(xb_stored, 16)
                pool.wait_ge(xdbl_mm, 1)
                pool.wait_ge(dt_done, c + 1)
                nc.gpsimd.tensor_tensor(xb[:, c], xb[:, c], acc[:, c % 2], ALU.mult).then_inc(u_done, 1)
            pool.wait_ge(zero_stored, 16 * (XS // (P * 4)))

        @block.vector
        def _(dve):
            nc.vector.memset(xpad[:, :, 0:TAPS - 1], 0.0).then_inc(pad_zeroed, 1)
            dve.wait_ge(loaded, 16 * (N_LOADS - 1))
            for i in range(NT):
                nc.vector.bn_stats(st[:, i], x_sb[:, i]).then_inc(stats_done, 1)
            for i in range(NT):
                dve.wait_ge(stats_done, i + 1)
                nc.vector.bn_aggr(mv[:, i], st[:, i]).then_inc(mv_done, 1)
            dve.wait_ge(mv_done, NT)
            nc.vector.tensor_scalar(rstd[:], mv[:, :, 1], EPS, None, ALU.add).then_inc(var_done, 1)
            dve.wait_ge(std_done, 1)
            nc.vector.reciprocal(rstd[:], rstd[:]).then_inc(rstd_done, 1)
            dve.wait_ge(rstd_done, 1)
            for i in range(NT):
                if i >= 2:
                    dve.wait_ge(transposed, i - 1)
                nc.vector.tensor_scalar(xn[:, i % 2], x_sb[:, i], mv[:, i, 0:1], rstd[:, i:i + 1],
                                        ALU.subtract, ALU.mult).then_inc(xn_done, 1)

            def taps(c, s):
                cwc = cw[:, c] if isinstance(c, int) else cw[:, bass.ds(c, 1)].rearrange("p a k -> p (a k)")
                out = acc[:, 0].rearrange("p (b t) -> p b t", b=B)
                for k in range(TAPS):
                    if k == 0:
                        nc.vector.tensor_scalar(out, xpad[:, :, 0:L], cwc[:, 0:1], None,
                                                ALU.mult).then_inc(conv_step, 1)
                    else:
                        dve.wait_ge(conv_step, s + k)
                        ins = nc.vector.scalar_tensor_tensor(out=out, in0=xpad[:, :, k:k + L], scalar=cwc[:, k:k + 1],
                                                             in1=out, op0=ALU.mult, op1=ALU.add)
                        ins.then_inc(conv_done if k == TAPS - 1 else conv_step, 1)

            with dve.Fori(0, CC) as c:
                dve.wait_ge(padded, c * G + (G + 1))
                dve.wait_ge(silu_done, c + 1)
                taps(c, c * (TAPS - 1))
            dve.wait_ge(xdbl_mm, 1)
            nc.vector.tensor_copy(xdbl[:].rearrange("p (g t) -> p g t", g=G), ps[0:XR, 0:G, 0:GL]).then_inc(xdbl_done, 1)
            dve.wait_ge(z_stored, 16 * CC + 1)
            for c in range(CC):
                q = 4 * (c % 2)
                dve.wait_ge(soft_step, 2 * c + 1)
                if c >= 1:
                    dve.wait_ge(dt_done, c)
                nc.vector.tensor_scalar(zs[:].rearrange("p (g t) -> p g t", g=G), ps[:, q:q + 4, 0:GL], bdt[:, c:c + 1],
                                        0.0, ALU.add, ALU.max).then_inc(relu_done, 1)
                dve.wait_ge(relu_done, c + 1)
                dve.wait_ge(ln_done, c + 1)
                nc.vector.tensor_tensor(acc[:, c % 2], acc[:, c % 2], zs[:], ALU.add).then_inc(dt_done, 1)

        @block.scalar
        def _(act):
            for s in (padded, z_done, silu_done):
                act.sem_inc(s, 1)
            act.wait_ge(var_done, 1)
            nc.scalar.activation(rstd[:], rstd[:], ACT.Sqrt).then_inc(std_done, 1)
            for i in range(NT):
                act.wait_ge(transposed, i + 1)
                nc.scalar.activation(xnT[:, :, i * TT:(i + 1) * TT],
                                     ps[:, i % 2, 0:KC * TT].rearrange("p (k t) -> p k t", k=KC),
                                     ACT.Copy).then_inc(xnT_done, 1)
            act.wait_ge(pad_zeroed, 1)
            act.wait_ge(loaded, 16 * (N_LOADS - 1))

            def evacuate(c):
                for g in range(G):
                    act.wait_ge(xb_mm, c + 1)
                    nc.scalar.activation(xpad[:, GB * g:GB * g + GB, TAPS - 1:],
                                         ps[:, g, 0:GL].rearrange("p (b t) -> p b t", b=GB),
                                         ACT.Copy).then_inc(padded, 1)

            def gates(c):
                act.wait_ge(z_mm, c + 1)
                act.wait_ge(z_stored, c * 16 + 1)
                nc.scalar.activation(zs[:].rearrange("p (g t) -> p g t", g=G), ps[:, G:2 * G, 0:GL],
                                     ACT.Silu).then_inc(z_done, 1)
                act.wait_ge(conv_done, c + 1)
                out = xb[:, bass.ds(c, 1)].rearrange("p a t -> p (a t)")
                nc.scalar.activation(out, acc[:, 0], ACT.Silu,
                                     bias=cb[:, bass.ds(c, 1)]).then_inc(silu_done, 1)

            with act.Fori(0, CC) as c:
                evacuate(c)
                gates(c)
            for c in range(CC):
                q, a = 4 * (c % 2), acc[:, c % 2]
                av = a.rearrange("p (g t) -> p g t", g=G)
                act.wait_ge(dt_mm, c + 1)
                if c >= 2:
                    act.wait_ge(dt_stored[c % 2], 16 * (c // 2))
                    act.wait_ge(u_done, c - 1)
                nc.scalar.activation(av, ps[:, q:q + 4, 0:GL], ACT.Abs, bias=bdt[:, c:c + 1]).then_inc(soft_step, 1)
                act.wait_ge(soft_step, 2 * c + 1)
                nc.scalar.activation(a, a, ACT.Exp, scale=-1.0).then_inc(soft_step, 1)
                act.wait_ge(soft_step, 2 * c + 2)
                nc.scalar.activation(a, a, ACT.Ln, bias=1.0).then_inc(ln_done, 1)

        @block.tensor
        def _(pe):
            pe.wait_ge(loaded, 16 * (N_LOADS - 1))
            for i in range(NT):
                pe.wait_ge(xn_done, i + 1)
                if i >= 2:
                    pe.wait_ge(xnT_done, i - 1)
                for k in range(KC):
                    ins = nc.tensor.transpose(ps[:, i % 2, k * TT:(k + 1) * TT], xn[:, i % 2, k * P:(k + 1) * P],
                                              ident[0:TT, 0:TT])
                ins.then_inc(transposed, 1)
            pe.wait_ge(xnT_done, NT)
            with pe.Fori(0, CC) as c:
                for half, done in ((0, xb_mm), (1, z_mm)):
                    pe.wait_ge(w_in_loaded[half], c * 16 + 16)
                    pe.wait_ge(padded if half == 0 else z_done, c * G + 1 if half == 0 else c + 1)
                    for g in range(G):
                        for k in range(KC):
                            ins = nc.tensor.matmul(ps[:, G * half + g, 0:GL], win[:, half, k], xnT[:, k, g * GL:(g + 1) * GL],
                                                   start=(k == 0), stop=(k == KC - 1))
                    ins.then_inc(done, 1)
            pe.wait_ge(silu_done, CC + 1)
            pe.wait_ge(z_done, CC + 1)
            for g in range(G):
                for c in range(CC):
                    ins = nc.tensor.matmul(ps[0:XR, g, 0:GL], wx[:, c], xb[:, c, g * GL:(g + 1) * GL],
                                           start=(c == 0), stop=(c == CC - 1))
            ins.then_inc(xdbl_mm, 1)
            pe.wait_ge(xdbl_done, 1)
            for c in range(CC):
                if c >= 2:
                    pe.wait_ge(dt_done, c - 1)
                for g in range(G):
                    ins = nc.tensor.matmul(ps[:, 4 * (c % 2) + g, 0:GL], wdt[:, c * P:(c + 1) * P],
                                           xdbl[0:R, g * GL:(g + 1) * GL], start=True, stop=True)
                ins.then_inc(dt_mm, 1)


def state_space(nc, A_log, D, ident_in, xb_d, z_d, dt_d, u_d, bc_d, y_d, ctxT_in, Wk, bk, Wv, k_d, v_d):
    ctx = ExitStack()
    with ctx:
        def sb(name, shape, dt=F32):
            return ctx.enter_context(nc.sbuf_tensor("s_" + name, shape, dt))

        def sem(name):
            return ctx.enter_context(nc.semaphore("s_" + name))

        ident = sb("ident", [P, P])
        A = sb("A", [P, CC, NS])
        Dv = sb("D", [P, CC])
        Bc = sb("Bc", [P, NS, GL])
        Cc = sb("Cc", [P, 2, NS, GL])
        decay = sb("decay", [P, DBUF, HS, GL])
        h = sb("h", [P, HBUF, HS, GL])
        early = sb("early", [P, 2, 2, GL])
        late = sb("late", [P, 2, 2, GL])
        y1 = sb("y1", [P, GL])
        y = sb("y", [P, GL])
        wk, wv, bkc = sb("wk", [P, CK, DM]), sb("wv", [P, CK, DM]), sb("bkc", [P, KC])
        cxT = sb("cxT", [P, CK, CTX])
        kT, v = sb("kT", [P, CTX]), sb("v", [CT, 2, DM])
        ps = ctx.enter_context(nc.psum_tensor("s_ps", [P, 2, 512], F32))
        kps = ctx.enter_context(nc.psum_tensor("s_kps", [P, 2, 512], F32))
        vps = ctx.enter_context(nc.psum_tensor("s_vps", [P, 2, 512], F32))

        consts = sem("consts")
        a_step, a_done = sem("a_step"), sem("a_done")
        b_loaded = sem("b_loaded")
        c_loaded = [sem("c_loaded0"), sem("c_loaded1")]
        early_loaded = [sem("early_loaded0"), sem("early_loaded1")]
        late_loaded = [sem("late_loaded0"), sem("late_loaded1")]
        y_stored = sem("y_stored")
        edge_done = sem("edge_done")
        decay_done, ub_done, scan_done, hc_done, sum_done, y1_done, y_done = (
            sem(n) for n in ("decay_done", "ub_done", "scan_done", "hc_done", "sum_done", "y1_done", "y_done"))
        ctx_loaded, kv_free, k_mm, v_mm, k_done, v_done, k_stored = (
            sem(n) for n in ("ctx_loaded", "kv_free", "k_mm", "v_mm", "k_done", "v_done", "k_stored"))
        v_stored = [sem("v_stored0"), sem("v_stored1")]
        V_TILES = [(0, 1), (2, 3), (4,), (5,)]
        block = ctx.enter_context(nc.Block())

        def batch(gg, pair, c):
            return gg * (2 * GB) + (GB * pair + c // 4)

        UNITS = 2 * CC

        def unit(gg, pair, n):
            return gg * (2 * UNITS) + (pair * UNITS + n)

        def chunk(gg, pair, n):
            return gg * (2 * CC) + (pair * CC + n)

        def cols(t, gg, pair):
            return t[:, bass.ds(gg * (2 * GL) + pair * GL, GL)]

        def wait_slot(eng, loaded, gg, pair, c, dmas):
            eng.wait_ge(loaded[c % 2], gg * (16 * dmas * CC) + 16 * dmas * ((pair * CC + c) // 2 + 1))

        @block.sync
        def _(sp):
            sp.dma_start(ident[:], ident_in).then_inc(consts, 16)
            sp.dma_start(A[:], A_log.rearrange("(c p) n -> p c n", p=P)).then_inc(consts, 16)
            sp.dma_start(Dv[:], D).then_inc(consts, 16)
            sp.dma_start(wk[:], Wk.rearrange("(k p) n -> p k n", p=P)).then_inc(consts, 16)
            sp.dma_start(wv[:], Wv.rearrange("(k p) n -> p k n", p=P)).then_inc(consts, 16)
            sp.dma_start(bkc[:], bk).then_inc(consts, 16)
            with sp.Fori(0, G // 2) as gg:
                for pair in range(2):
                    for c in range(CC):
                        sp.wait_ge(decay_done, unit(gg, pair, 2 * c + 1))
                        sp.wait_ge(ub_done, unit(gg, pair, 2 * c + 1))
                        for j, src in enumerate((dt_d, u_d)):
                            sp.dma_start(early[:, c % 2, j], cols(src[c], gg, pair)).then_inc(early_loaded[c % 2], 16)
                        if c == 0:
                            sp.wait_ge(ub_done, unit(gg, pair, UB_FREE))
                            sp.dma_start(Bc[:], cols(bc_d[0:NS], gg, pair).partition_broadcast(P)).then_inc(b_loaded, 16)
                        if c % 4 == 0:
                            b = batch(gg, pair, c)
                            sp.wait_ge(kv_free, b + 1)
                            sp.dma_start(cxT[:], ctxT_in[bass.ds(b, 1)].rearrange("a (k p) t -> p (a k) t", p=P)).then_inc(ctx_loaded, 16)

        @block.gpsimd
        def _(pool):
            nc.gpsimd.sem_inc(ub_done, UB_FREE)
            with pool.Fori(0, G // 2) as gg:
                for pair in range(2):
                    for c in range(CC):
                        wait_slot(pool, early_loaded, gg, pair, c, 2)
                        if c == 0:
                            pool.wait_ge(b_loaded, gg * 32 + pair * 16 + 16)
                        for s in range(2):
                            pool.wait_ge(sum_done, unit(gg, pair, 2 * c + s + 1))
                            u = early[:, c % 2, 1].unsqueeze(1).to_broadcast([P, HS, GL])
                            nc.gpsimd.tensor_tensor(h[:, (2 * c + s) % HBUF], Bc[:, s * HS:(s + 1) * HS], u,
                                                    ALU.mult).then_inc(ub_done, 1)

        @block.scalar
        def _(act):
            act.sem_inc(decay_done, UB_FREE)
            for s in (y_stored, k_stored, *v_stored, k_done, v_done):
                act.sem_inc(s, 1)
            act.wait_ge(consts, 96)
            nc.scalar.activation(A[:], A[:], ACT.Exp).then_inc(a_step, 1)
            act.wait_ge(a_step, 1)
            nc.scalar.activation(A[:], A[:], ACT.Copy, scale=-1.0).then_inc(a_done, 1)
            act.wait_ge(a_done, 1)

            def store(gg, pair, c):
                act.wait_ge(y_done, chunk(gg, pair, c + 3))
                act.dma_start(cols(y_d[c], gg, pair), y[:]).then_inc(y_stored, 16)

            def keys_values(gg, pair, c):
                b, q = batch(gg, pair, c), c % 4
                act.wait_ge(k_mm, b * KC + (q + 1))
                act.wait_ge(k_stored, b * (16 * KC) + (16 * q + 1))
                nc.scalar.activation(kT[:].rearrange("p (a c) -> p a c", a=2), kps[:, :, 0:HALF], ACT.Identity,
                                     bias=bkc[:, q:q + 1]).then_inc(k_done, 1)
                for i in V_TILES[q]:
                    act.wait_ge(v_mm, b * NC + (i + 1))
                    act.wait_ge(v_stored[i % 2], b * (16 * NC // 2) + (16 * (i // 2) + 1))
                    nc.scalar.activation(v[:, i % 2], vps[0:CT, i % 2], ACT.Copy).then_inc(v_done, 1)
                act.wait_ge(k_done, b * KC + (q + 2))
                act.dma_start(k_d[bass.ds(b, 1), q].rearrange("a p t -> (a p) t"), kT[:]).then_inc(k_stored, 16)
                for i in V_TILES[q]:
                    act.wait_ge(v_done, b * NC + (i + 2))
                    act.dma_start(v_d[bass.ds(b, 1), i].rearrange("a p d -> (a p) d"), v[:, i % 2]).then_inc(v_stored[i % 2], 16)

            with act.Fori(0, G // 2) as gg:
                for pair in range(2):
                    act.wait_ge(hc_done, unit(gg, pair, 1))
                    act.dma_start(Cc[:, pair], cols(bc_d[NS:], gg, pair).partition_broadcast(P)).then_inc(c_loaded[pair], 16)
                    for c in range(CC):
                        wait_slot(act, early_loaded, gg, pair, c, 2)
                        for s in range(2):
                            act.wait_ge(scan_done, unit(gg, pair, 2 * c + s + 1))
                            for n in range(HS):
                                ins = nc.scalar.activation(decay[:, s, n], early[:, c % 2, 0], ACT.Exp,
                                                           scale=A[:, c, s * HS + n:s * HS + n + 1])
                            ins.then_inc(decay_done, 1)
                        act.wait_ge(y_done, chunk(gg, pair, c + 1))
                        for j, src in enumerate((xb_d, z_d)):
                            act.dma_start(late[:, c % 2, j], cols(src[c], gg, pair)).then_inc(late_loaded[c % 2], 16)
                        keys_values(gg, pair, c)
                        if c >= 1:
                            store(gg, pair, c - 1)
                    store(gg, pair, CC - 1)
            act.wait_ge(y_stored, 16 * G * CC + 1)
            act.wait_ge(k_stored, 16 * B * KC + 1)
            for s in v_stored:
                act.wait_ge(s, 16 * B * NC // 2 + 1)

        @block.vector
        def _(dve):
            def outputs(gg, pair, c):
                wait_slot(dve, late_loaded, gg, pair, c, 2)
                dve.wait_ge(sum_done, unit(gg, pair, 2 * c + 2 + HBUF))
                dve.wait_ge(y_done, chunk(gg, pair, c + 2))
                nc.vector.scalar_tensor_tensor(out=y1[:], in0=late[:, c % 2, 0], scalar=Dv[:, c:c + 1],
                                               in1=ps[:, c % 2, 0:GL], op0=ALU.mult, op1=ALU.add).then_inc(y1_done, 1)
                dve.wait_ge(y1_done, chunk(gg, pair, c + 3))
                dve.wait_ge(y_stored, gg * (32 * CC) + (16 * (pair * CC + c) + 1))
                nc.vector.tensor_tensor(y[:], y1[:], late[:, c % 2, 1], ALU.mult).then_inc(y_done, 1)

            dve.sem_inc(scan_done, DBUF)
            dve.sem_inc(hc_done, UNITS + 1)
            dve.sem_inc(y1_done, 2)
            dve.sem_inc(y_done, 2)
            dve.wait_ge(consts, 96)
            with dve.Fori(0, G // 2) as gg:
                for pair in range(2):
                    for n in range(UNITS):
                        c, s, buf = n // 2, n % 2, n % HBUF
                        dve.wait_ge(decay_done, unit(gg, pair, n + 1 + UB_FREE))
                        nc.vector.memset(decay[:, s].rearrange("p n (b t) -> p (n b) t", b=GB)[:, :, 0:1],
                                         0.0).then_inc(edge_done, 1)
                        dve.wait_ge(edge_done, unit(gg, pair, n + 1))
                        dve.wait_ge(ub_done, unit(gg, pair, n + 1 + UB_FREE))
                        hv = h[:, buf].rearrange("p n t -> p (n t)")
                        nc.vector.tensor_tensor_scan(hv, decay[:, s].rearrange("p n t -> p (n t)"), hv, 0.0,
                                                     ALU.mult, ALU.add).then_inc(scan_done, 1)
                        dve.wait_ge(scan_done, unit(gg, pair, n + 1 + DBUF))
                        if n == 0:
                            dve.wait_ge(c_loaded[pair], gg * 16 + 16)
                        nc.vector.tensor_tensor(h[:, buf], h[:, buf], Cc[:, pair, s * HS:(s + 1) * HS],
                                                ALU.mult).then_inc(hc_done, 1)
                        if s == 1 and c >= 1:
                            outputs(gg, pair, c - 1)
                    outputs(gg, pair, CC - 1)

        @block.tensor
        def _(pe):
            pe.sem_inc(sum_done, HBUF)
            pe.sem_inc(kv_free, 1)
            pe.wait_ge(consts, 96)
            with pe.Fori(0, G // 2) as gg:
                for pair in range(2):
                    for c in range(CC):
                        b, q = batch(gg, pair, c), c % 4
                        pe.wait_ge(ctx_loaded, b * 16 + 16)
                        pe.wait_ge(k_done, b * KC + (q + 1))
                        for a in range(2):
                            for k in range(CK):
                                ins = nc.tensor.matmul(kps[:, a, 0:HALF], wk[:, k, q * P:(q + 1) * P],
                                                       cxT[:, k, a * HALF:(a + 1) * HALF], start=(k == 0), stop=(k == CK - 1))
                        ins.then_inc(k_mm, 1)
                        for i in V_TILES[q]:
                            pe.wait_ge(v_done, b * NC + max(i, 1))
                            for k in range(CK):
                                ins = nc.tensor.matmul(vps[0:CT, i % 2], cxT[:, k, i * CT:(i + 1) * CT], wv[:, k],
                                                       start=(k == 0), stop=(k == CK - 1))
                            ins.then_inc(v_mm, 1)
                        if q == 3:
                            pe.wait_ge(v_mm, b * NC + NC)
                            pe.sem_inc(kv_free, 1)
                        pe.wait_ge(y1_done, chunk(gg, pair, c + 1))
                        for s in range(2):
                            pe.wait_ge(hc_done, unit(gg, pair, 2 * c + s + 2 + UNITS))
                            for n in range(HS):
                                ins = nc.tensor.matmul(ps[:, c % 2, 0:GL], ident[:], h[:, (2 * c + s) % HBUF, n],
                                                       start=(s == 0 and n == 0), stop=(s == 1 and n == HS - 1))
                            ins.then_inc(sum_done, 1)

def attention(nc, x, k_d, v_d, y_d, W_out, Wq, bq, bv, Wo, bo, rW1, rb1, rW2, rb2, ident_in,
              x2_d, xn_d, logits_d):
    ctx = ExitStack()
    ITEMS = 2 * HEADS
    with ctx:
        def sb(name, shape, dt=F32):
            return ctx.enter_context(nc.sbuf_tensor("t_" + name, shape, dt))

        def sem(name):
            return ctx.enter_context(nc.semaphore("t_" + name))

        ident = sb("ident", [P, P])
        wout, wq = sb("wout", [P, CC, DM]), sb("wq", [P, KC, DM])
        wo, rw1, rw2 = sb("wo", [P, KC, DM]), sb("rw1", [P, KC, RH]), sb("rw2", [P, RC, E])
        bqc, bvc, rb1c = sb("bqc", [P, KC]), sb("bvc", [P, KC]), sb("rb1c", [P, RC])
        bor, rb2r = sb("bor", [P, DM]), sb("rb2r", [P, E])
        gT = sb("gT", [P, CC, L])
        xt = sb("xt", [TT, 2, DM])
        kT = sb("kT", [P, KC, CTX])
        v = sb("v", [CT, NC, DM])
        qz = sb("qz", [P, HEADS, L])
        xr = [sb("x1", [TT, 2, DM]), sb("x2", [TT, 2, DM])]
        xn = [sb("xn1", [TT, 2, DM]), sb("xn2", [TT, 2, DM])]
        xnT = [sb("xnT1", [P, KC, L]), sb("xnT2", [P, KC, L])]
        probs = sb("probs", [TT, 3, CTX])
        pT = sb("pT", [CT, 2, 4, NC, L])
        oT = sb("oT", [P, KC, L])
        rh = sb("rh", [P, RC, L])
        lg = sb("lg", [TT, 2, E])
        st, mv, rstd = sb("st", [TT, 4, 6]), sb("mv", [TT, 4, 2]), sb("rstd", [TT, 2, 2])
        nmax, rsum, rinv = sb("nmax", [TT, ITEMS]), sb("rsum", [TT, ITEMS]), sb("rinv", [TT, ITEMS])
        ps = ctx.enter_context(nc.psum_tensor("t_ps", [P, 8, 512], F32))

        S = {n: sem(n) for n in (
            "w_out w_q w_rest g_loaded x_loaded q_zeroed out_mm x1_done x2_done stat1 stat2 stat_seen mv1 mv2 var1 var2 "
            "std1 std2 rstd1 rstd2 xn1 xn2 xn1_mm xn2_mm xn1T xn2T "
            "q_mm q_done score_mm max_done exp_done rinv_done norm_done turn_mm turn_done "
            "pv_mm o_done wo_mm x1b_done x2_stored xn_stored rh_mm rh_done lg_mm lg_done lg_stored").split()}
        k_loaded = [sem(f"k_loaded{j}") for j in range(KC)]
        v_loaded = [sem(f"v_loaded{j}") for j in range(KC)]
        N_OUT, N_Q, N_REST = 2, 3, 6

        def start(eng, names):
            for name in names.split():
                eng.sem_inc(S[name], 1)

        def wait(eng, name, n):
            eng.wait_ge(S[name], n + 1)

        block = ctx.enter_context(nc.Block())

        @block.sync
        def _(sp):
            start(sp, "w_out w_q w_rest g_loaded x_loaded x2_stored xn_stored lg_stored")

            def rows(w):
                return w.rearrange("(k p) n -> p k n", p=P)

            def loads(b, used):
                if used is not None:
                    wait(sp, "out_mm", used * 2)
                sp.dma_start(gT[:], y_d[:, :, bass.ds(b * L, L)].rearrange("c p t -> p c t")).then_inc(S["g_loaded"], 16)
                if used is not None:
                    wait(sp, "x1_done", used * 2)
                sp.dma_start(xt[:], x[bass.ds(b, 1)].rearrange("a (u p) d -> p (a u) d", p=TT)).then_inc(S["x_loaded"], 16)

            def load_heads(b, used, j):
                if used is not None:
                    wait(sp, "score_mm", used * ITEMS - (ITEMS - 8 * j - 8))
                sp.dma_start(kT[:, j], k_d[bass.ds(b, 1), j].rearrange("a p t -> (a p) t")).then_inc(k_loaded[j], 16)
                if used is not None:
                    wait(sp, "pv_mm", used * KC - (KC - j - 1))
                sp.dma_start(v[:, :, j * P:(j + 1) * P],
                             v_d[bass.ds(b, 1), :, :, j * P:(j + 1) * P].rearrange("a i p d -> p (a i) d")).then_inc(v_loaded[j], 16)

            def store(done, n, dst, src, stored):
                def of(b):
                    wait(sp, done, b * n + n)
                    sp.dma_start(dst[bass.ds(b, 1)].rearrange("a p u d -> p (a u) d"), src[:]).then_inc(S[stored], 16)
                return of

            store_x2 = store("x2_done", 2, x2_d, xr[1], "x2_stored")
            store_xn = store("xn2", 2, xn_d, xn[1], "xn_stored")
            store_logits = store("lg_done", 2, logits_d, lg, "lg_stored")

            sp.dma_start(ident[:], ident_in).then_inc(S["w_out"], 16)
            loads(0, None)
            sp.dma_start(wout[:], rows(W_out)).then_inc(S["w_out"], 16)
            for dst, src in ((bqc[:], bq), (bvc[:], bv), (wq[:], rows(Wq))):
                sp.dma_start(dst, src).then_inc(S["w_q"], 16)
            for j in range(KC):
                load_heads(0, None, j)
            for dst, src in ((bor[:], bo.partition_broadcast(P)), (wo[:], rows(Wo)), (rb1c[:], rb1), (rw1[:], rows(rW1)),
                             (rw2[:], rows(rW2)), (rb2r[:], rb2.partition_broadcast(P))):
                sp.dma_start(dst, src).then_inc(S["w_rest"], 16)
            with sp.Fori(1, B) as b:
                loads(b, b)
                for j in range(KC):
                    load_heads(b, b, j)
                store_x2(b - 1)
                store_xn(b - 1)
                store_logits(b - 1)
            store_x2(B - 1)
            store_xn(B - 1)
            store_logits(B - 1)
            for stored in ("x2_stored", "xn_stored", "lg_stored"):
                wait(sp, stored, 16 * B)

        @block.gpsimd
        def _(pool):
            start(pool, "q_zeroed x1b_done")
            nc.gpsimd.memset(qz[:], 0.0).then_inc(S["q_zeroed"], 1)
            wait(pool, "w_rest", 16 * N_REST)
            with pool.Fori(0, B) as b:
                for u in range(2):
                    wait(pool, "xn1", b * 2 + u + 1)
                    nc.gpsimd.tensor_tensor(xr[0][:, u], xr[0][:, u], bor[0:TT], ALU.add).then_inc(S["x1b_done"], 1)

        @block.vector
        def _(dve):
            start(dve, "x1_done x2_done stat1 stat2 stat_seen mv1 mv2 var1 var2 rstd1 rstd2 xn1 xn2 q_done "
                       "max_done rinv_done norm_done o_done lg_done")

            def norm(b, w):
                nth = str(w + 1)
                for u in range(2):
                    wait(dve, "x" + nth + "_done", b * 2 + u + 1)
                    nc.vector.bn_stats(st[:, 2 * w + u], xr[w][:, u]).then_inc(S["stat" + nth], 1)
                wait(dve, "stat" + nth, b * 2 + 2)
                dve.sem_inc(S["stat_seen"])
                for u in range(2):
                    nc.vector.bn_aggr(mv[:, 2 * w + u], st[:, 2 * w + u]).then_inc(S["mv" + nth], 1)
                wait(dve, "mv" + nth, b * 2 + 2)
                r = rstd[:, w]
                nc.vector.tensor_scalar(r, mv[:, 2 * w:2 * w + 2, 1], EPS, None, ALU.add).then_inc(S["var" + nth], 1)
                wait(dve, "std" + nth, b + 1)
                nc.vector.reciprocal(r, r).then_inc(S["rstd" + nth], 1)
                wait(dve, "rstd" + nth, b + 1)
                wait(dve, "xn" + nth + "_mm", b * 2)
                if w == 1:
                    wait(dve, "xn_stored", b * 16)
                for u in range(2):
                    nc.vector.tensor_scalar(xn[w][:, u], xr[w][:, u], mv[:, 2 * w + u, 0:1], rstd[:, w, u:u + 1],
                                            ALU.subtract, ALU.mult).then_inc(S["xn" + nth], 1)

            def negative_max(b, n):
                wait(dve, "score_mm", b * ITEMS + n + 1)
                nc.vector.tensor_reduce(nmax[:, n:n + 1], ps[0:TT, 2 * (n % 2):2 * (n % 2) + 2, 0:HALF], AX.XY, ALU.max,
                                        negate=True).then_inc(S["max_done"], 1)

            def normalise(b, n):
                wait(dve, "exp_done", b * ITEMS + n + 1)
                nc.vector.reciprocal(rinv[:, n:n + 1], rsum[:, n:n + 1]).then_inc(S["rinv_done"], 1)
                wait(dve, "rinv_done", b * ITEMS + n + 1)
                nc.vector.tensor_scalar(probs[:, n % 3], probs[:, n % 3], rinv[:, n:n + 1], None,
                                        ALU.mult).then_inc(S["norm_done"], 1)

            def outputs(b, j):
                wait(dve, "pv_mm", b * KC + j + 1)
                nc.vector.tensor_scalar(oT[:, j], ps[:, 6 + j % 2, 0:L], bvc[:, j:j + 1], None, ALU.add).then_inc(S["o_done"], 1)

            def logits(b):
                for u in range(2):
                    wait(dve, "lg_stored", b * 16)
                    wait(dve, "lg_mm", b * 2 + u + 1)
                    nc.vector.tensor_tensor(lg[:, u], ps[0:TT, 6 + u, 0:E], rb2r[0:TT], ALU.add).then_inc(S["lg_done"], 1)

            def batch(b, first):
                wait(dve, "x_loaded", b * 16 + 16)
                wait(dve, "x2_done", b * 2)
                for u in range(2):
                    wait(dve, "out_mm", b * 2 + u + 1)
                    nc.vector.tensor_tensor(xr[0][:, u], ps[0:TT, 4 + u], xt[:, u], ALU.add).then_inc(S["x1_done"], 1)
                norm(b, 0)
                if not first:
                    logits(b - 1)
                for j in range(KC):
                    wait(dve, "q_mm", b * KC + j + 1)
                    for r in range(4):
                        rows = slice(DK * r, DK * r + DK)
                        ins = nc.vector.tensor_scalar(qz[rows, 4 * j + r], ps[rows, 4 + j % 2, 0:L], bqc[rows, j:j + 1],
                                                      float(DK) ** -0.5, ALU.add, ALU.mult)
                    ins.then_inc(S["q_done"], 1)
                negative_max(b, 0)
                for n in range(ITEMS):
                    if n + 1 < ITEMS:
                        negative_max(b, n + 1)
                    normalise(b, n)
                    if n >= 8 and n % 8 == 3:
                        outputs(b, n // 8 - 1)
                outputs(b, KC - 1)
                wait(dve, "x2_stored", b * 16)
                for u in range(2):
                    wait(dve, "wo_mm", b * 2 + u + 1)
                    wait(dve, "x1b_done", b * 2 + u + 1)
                    nc.vector.tensor_tensor(xr[1][:, u], ps[0:TT, 4 + u], xr[0][:, u], ALU.add).then_inc(S["x2_done"], 1)
                norm(b, 1)

            wait(dve, "w_q", 16 * N_Q)
            wait(dve, "q_zeroed", 1)
            batch(0, True)
            wait(dve, "w_rest", 16 * N_REST)
            with dve.Fori(1, B) as b:
                batch(b, False)
            logits(B - 1)

        @block.scalar
        def _(act):
            start(act, "std1 std2 xn1T xn2T exp_done turn_done rh_done")

            def deviation(b, w):
                wait(act, f"var{w + 1}", b + 1)
                nc.scalar.activation(rstd[:, w], rstd[:, w], ACT.Sqrt).then_inc(S[f"std{w + 1}"], 1)

            def turned_norm(b, w):
                for u in range(2):
                    wait(act, f"xn{w + 1}_mm", b * 2 + u + 1)
                    nc.scalar.activation(xnT[w][:, :, u * TT:(u + 1) * TT],
                                         ps[:, 6 + u, 0:KC * TT].rearrange("p (k t) -> p k t", k=KC),
                                         ACT.Copy).then_inc(S[f"xn{w + 1}T"], 1)

            def router(b):
                turned_norm(b, 1)
                for c in range(RC):
                    wait(act, "rh_mm", b * RC + c + 1)
                    nc.scalar.activation(rh[:, c], ps[:, c % 4, 0:L], ACT.Gelu, bias=rb1c[:, c:c + 1]).then_inc(S["rh_done"], 1)

            def exponentials(b, n):
                wait(act, "max_done", b * ITEMS + n + 1)
                wait(act, "turn_mm", b * ITEMS + max(n - 2, 0))
                nc.scalar.activation(probs[:, n % 3].rearrange("p (a c) -> p a c", a=2),
                                     ps[0:TT, 2 * (n % 2):2 * (n % 2) + 2, 0:HALF], ACT.Exp, bias=nmax[:, n:n + 1],
                                     accum_out=rsum[:, n:n + 1]).then_inc(S["exp_done"], 1)

            def turned_probs(b, n):
                h, u = n // 2, n % 2
                j = h // 4
                wait(act, "turn_mm", b * ITEMS + n + 1)
                wait(act, "pv_mm", b * KC + max(j - 1, 0))
                nc.scalar.activation(pT[:, j % 2, h % 4, :, u * TT:(u + 1) * TT].rearrange("p (a i) t -> p a i t", a=2),
                                     ps[0:CT, 4:6, 0:3 * TT].rearrange("p a (i t) -> p a i t", i=3),
                                     ACT.Copy).then_inc(S["turn_done"], 1)

            def batch(b, first):
                deviation(b, 0)
                if not first:
                    router(b - 1)
                turned_norm(b, 0)
                exponentials(b, 0)
                for n in range(ITEMS):
                    if n + 1 < ITEMS:
                        exponentials(b, n + 1)
                    turned_probs(b, n)
                deviation(b, 1)

            batch(0, True)
            wait(act, "w_rest", 16 * N_REST)
            with act.Fori(1, B) as b:
                batch(b, False)
            router(B - 1)

        @block.tensor
        def _(pe):
            start(pe, "out_mm xn1_mm xn2_mm q_mm score_mm turn_mm pv_mm wo_mm rh_mm lg_mm")

            def turn_norm(b, w):
                for u in range(2):
                    wait(pe, f"xn{w + 1}", b * 2 + u + 1)
                    for k in range(KC):
                        ins = nc.tensor.transpose(ps[:, 6 + u, k * TT:(k + 1) * TT], xn[w][:, u, k * P:(k + 1) * P],
                                                  ident[0:TT, 0:TT])
                    ins.then_inc(S[f"xn{w + 1}_mm"], 1)

            def router(b):
                wait(pe, "o_done", b * KC + KC)
                turn_norm(b, 1)
                wait(pe, "xn2T", b * 2 + 2)
                for c in range(RC):
                    wait(pe, "rh_done", b * RC + max(c - 3, 0))
                    for k in range(KC):
                        ins = nc.tensor.matmul(ps[:, c % 4, 0:L], rw1[:, k, c * P:(c + 1) * P], xnT[1][:, k],
                                               start=(k == 0), stop=(k == KC - 1))
                    ins.then_inc(S["rh_mm"], 1)
                wait(pe, "rh_done", b * RC + RC)
                for u in range(2):
                    for c in range(RC):
                        ins = nc.tensor.matmul(ps[0:TT, 6 + u, 0:E], rh[:, c, u * TT:(u + 1) * TT], rw2[:, c],
                                               start=(c == 0), stop=(c == RC - 1))
                    ins.then_inc(S["lg_mm"], 1)

            def scores(b, n):
                h, u = n // 2, n % 2
                if n % 8 == 0:
                    pe.wait_ge(k_loaded[h // 4], b * 16 + 16)
                wait(pe, "exp_done", b * ITEMS + max(n - 1, 0))
                for a in range(2):
                    ins = nc.tensor.matmul(ps[0:TT, 2 * (n % 2) + a, 0:HALF], qz[:, h, u * TT:(u + 1) * TT],
                                           kT[:, h // 4, a * HALF:(a + 1) * HALF], start=True, stop=True)
                ins.then_inc(S["score_mm"], 1)

            def turn_probs(b, n):
                wait(pe, "norm_done", b * ITEMS + n + 1)
                wait(pe, "turn_done", b * ITEMS + n)
                for i in range(NC):
                    ins = nc.tensor.transpose(ps[0:CT, 4 + i // 3, (i % 3) * TT:(i % 3 + 1) * TT],
                                              probs[:, n % 3, i * CT:(i + 1) * CT], ident[0:TT, 0:TT])
                ins.then_inc(S["turn_mm"], 1)

            def values(b, j):
                pe.wait_ge(v_loaded[j], b * 16 + 16)
                wait(pe, "turn_done", b * ITEMS + 8 * j + 8)
                wait(pe, "o_done", b * KC + max(j - 1, 0))
                for i in range(NC):
                    for r in range(4):
                        h = 4 * j + r
                        ins = nc.tensor.matmul(ps[DK * r:DK * r + DK, 6 + j % 2, 0:L], v[:, i, h * DK:(h + 1) * DK],
                                               pT[:, j % 2, r, i], start=(i == 0), stop=(i == NC - 1),
                                               tile_position=(0, DK * r))
                ins.then_inc(S["pv_mm"], 1)

            def batch(b, first):
                wait(pe, "g_loaded", b * 16 + 16)
                wait(pe, "x2_done", b * 2)
                for u in range(2):
                    for c in range(CC):
                        ins = nc.tensor.matmul(ps[0:TT, 4 + u], gT[:, c, u * TT:(u + 1) * TT], wout[:, c],
                                               start=(c == 0), stop=(c == CC - 1))
                    ins.then_inc(S["out_mm"], 1)
                if first:
                    wait(pe, "w_q", 16 * N_Q)
                else:
                    router(b - 1)
                wait(pe, "lg_done", b * 2)
                turn_norm(b, 0)
                wait(pe, "xn1T", b * 2 + 2)
                for j in range(KC):
                    if j < 2:
                        wait(pe, "x1_done", b * 2 + 2)
                    else:
                        wait(pe, "q_done", b * KC + j - 1)
                    for k in range(KC):
                        ins = nc.tensor.matmul(ps[:, 4 + j % 2, 0:L], wq[:, k, j * P:(j + 1) * P], xnT[0][:, k],
                                               start=(k == 0), stop=(k == KC - 1))
                    ins.then_inc(S["q_mm"], 1)
                wait(pe, "q_done", b * KC + KC)
                scores(b, 0)
                scores(b, 1)
                for n in range(ITEMS):
                    if n + 2 < ITEMS:
                        scores(b, n + 2)
                    turn_probs(b, n)
                    if n >= 8 and n % 8 == 1:
                        values(b, n // 8 - 1)
                values(b, KC - 1)
                if first:
                    wait(pe, "w_rest", 16 * N_REST)
                wait(pe, "o_done", b * KC + KC)
                for u in range(2):
                    for j in range(KC):
                        ins = nc.tensor.matmul(ps[0:TT, 4 + u], oT[:, j, u * TT:(u + 1) * TT], wo[:, j],
                                               start=(j == 0), stop=(j == KC - 1))
                    ins.then_inc(S["wo_mm"], 1)

            wait(pe, "w_out", 16 * N_OUT)
            batch(0, True)
            with pe.Fori(1, B) as b:
                batch(b, False)
            router(B - 1)


def experts(nc, We1, be1, We2, be2, upper_in, ident_in, tile_starts_in, x2_d, xn_d, logits_d, xs_d, out):
    ctx = ExitStack()
    PAIRS = [(a, b) for a in range(E) for b in range(a + 1, E)]
    WG = 4
    CW = HC // WG
    GW = CW * P
    RING = 4
    AHEAD = 2
    HALVES = GT // P
    with ctx:
        def sb(name, shape, dt=F32):
            return ctx.enter_context(nc.sbuf_tensor("e_" + name, shape, dt))

        def sem(name):
            return ctx.enter_context(nc.semaphore("e_" + name))

        w1h, w1l = (sb(n, [P, WG, KC, GW], F32R) for n in ("w1h", "w1l"))
        w2h, w2l = (sb(n, [P, WG, CW, DM], F32R) for n in ("w2h", "w2l"))
        stage = sb("stage", [P, 4, 4, 512])
        b1, b2 = sb("b1", [P, E * HC]), sb("b2", [P, E, DM])
        ident, upper, ones = sb("ident", [P, P]), sb("upper", [TT, TT]), sb("ones", [TT, TT])
        one = sb("one", [P, 1])
        starts = sb("starts", [1, EG])
        lg, p, m, pm = (sb(n, [TT, NT, E]) for n in ("lg", "p", "m", "pm"))
        mx, total = sb("mx", [TT, NT]), sb("total", [TT, NT])
        ge = sb("ge", [TT, len(PAIRS), NT])
        r = sb("r", [TT, 2, NT])
        incl, slot, tmp, eq = (sb(n, [TT, NT, E]) for n in ("incl", "slot", "tmp", "eq"))
        choice = sb("choice", [TT, 2, NT])
        gate = sb("gate", [TT, 2, NT])
        index = sb("index", [TT, 2, NT], I32)
        taken = sb("taken", [1, E, EG])
        count = sb("count", [1, E])
        tiles = sb("tiles", [1, 2, E + 1])
        tiles_i = sb("tiles_i", [1, 2, E + 1], I32)
        xt = sb("xt", [P, HALVES, DM])
        xTh, xTl = sb("xTh", [P, KC, GT], F32R), sb("xTl", [P, KC, GT], F32R)
        h = sb("h", [P, RING, GT])
        hh, hl = sb("hh", [P, RING, GT], F32R), sb("hl", [P, RING, GT], F32R)
        y = sb("y", [P, HALVES, DM])
        ps = ctx.enter_context(nc.psum_tensor("e_ps", [P, 8, 512], F32))
        H_BANK, Y_BANK, X_BANK = 0, 4, 6

        xn = [part[0:TT, g].bitcast(F32) for part, g in ((w1l, 2), (w1l, 3), (w2l, 2), (w2l, 3))]
        back = [w1h[0:TT].bitcast(F32), w1l[0:TT].bitcast(F32)]

        S = {n: sem(n) for n in (
            "consts lg_loaded step ones_set exped n_loaded rank_mm slots_done tiles_done n_scattered "
            "w_high w_split waited x_loaded x_mm x_high x_split h_mm h_done h_high h_split l2_mm y_done y_stored "
            "x2_loaded combined out_stored").split()}
        w_first = [sem(f"w_first{i}") for i in range(4)]
        w_loaded = [sem(f"w_loaded{i}") for i in range(4)]
        r_gathered = [sem(f"r_gathered{i}") for i in range(4)]
        FIRST = {n: 1 + HC for n in ("h_mm", "h_done", "h_high", "h_split", "l2_mm")}

        def start(eng, names):
            for name in names.split():
                eng.sem_inc(S[name], FIRST.get(name, 1))

        def wait(eng, name, n):
            eng.wait_ge(S[name], n + FIRST.get(name, 1))

        block = ctx.enter_context(nc.Block())
        N_CONST = 5
        xs_v = xs_d.rearrange("(i h p) d -> i p h d", h=HALVES, p=P)
        out_v = out.rearrange("b (u p) d -> (b u) p d", p=TT)
        xn_v = xn_d.rearrange("(g b) p u d -> g p b u d", g=4)
        x2_v = x2_d.rearrange("(g b) p u d -> g p b u d", g=4)

        def weights(eng, n):
            e, g, second = n // (2 * WG), n % (2 * WG) // 2, n % 2
            src = We2[e].rearrange("(g c p) n -> g p c n", p=P, g=WG)[g] if second else \
                We1[e].rearrange("(k p) n -> p k n", p=P)[:, :, g * GW:(g + 1) * GW]
            eng.dma_start(stage[:, n % 4], src).then_inc(w_first[n] if n < 4 else w_loaded[n % 4], 16)

        def wait_weights(eng, n):
            if n < 4:
                eng.wait_ge(w_first[n], 16)
            else:
                eng.wait_ge(w_loaded[n % 4], 16 * (n // 4))

        def parts(n):
            g = n % (2 * WG) // 2
            return (w2h[:, g], w2l[:, g]) if n % 2 else (w1h[:, g], w1l[:, g])

        STEPS_TO_MASK = 5 + len(PAIRS) + E * (len(PAIRS) * 2 // E + 1)

        def counts(eng, e):
            return [eng.value_load(tiles_i[0:1, j, e:e + 1], min_val=0, max_val=E * EG) for j in range(2)]

        def expert_tiles(eng, e, first, body):
            taken_e, before = counts(eng, e)
            first(before + e)
            with eng.Fori(0, EG) as i:
                with eng.If(i < taken_e):
                    body(i, before + i, before + e + i)

        @block.sync
        def _(sp):
            start(sp, "lg_loaded consts x_loaded")

            sp.dma_start(lg[:].rearrange("p (b u) e -> p b u e", u=2), logits_d.rearrange("b p u e -> p b u e")).then_inc(S["lg_loaded"], 16)
            for dst, src in ((upper[:], upper_in), (ident[:], ident_in), (starts[:], tile_starts_in), (b1[:], be1)):
                sp.dma_start(dst, src).then_inc(S["consts"], 16)
            weights(sp, 0)
            weights(sp, 1)
            for g in range(4):
                sp.dma_start(xn[g].rearrange("p (b u) d -> p b u d", u=2), xn_v[g]).then_inc(S["n_loaded"], 16)
            weights(sp, 2)
            weights(sp, 3)
            sp.dma_start(b2[:], be2.partition_broadcast(P)).then_inc(S["consts"], 16)
            wait(sp, "tiles_done", 1)
            sp.wait_ge(S["n_scattered"], 32 * NT)
            for e in range(E):
                def load(row, t):
                    wait(sp, "x_mm", t)
                    sp.dma_start(xt[:], xs_v[bass.ds(row, 1)].rearrange("a p h d -> (a p) h d")).then_inc(S["x_loaded"], 16)

                expert_tiles(sp, e, lambda t: load(e * EG, t), lambda i, n, t: load(i + (e * EG + 1), t + 1))
            sp.wait_ge(S["w_split"], 2 * WG * E)
            for g in range(4):
                sp.dma_start(stage[0:TT, g].rearrange("p (b u) d -> p b u d", u=2), x2_v[g]).then_inc(S["x2_loaded"], 16)
            for i in range(0, NT, 2):
                wait(sp, "combined", 2 * i + 2)
                sp.dma_start(out_v[i], stage[0:TT, i // 4, i % 4]).then_inc(S["out_stored"], 16)
            sp.wait_ge(S["out_stored"], 16 * NT)

        @block.gpsimd
        def _(pool):
            start(pool, "ones_set waited")

            nc.gpsimd.memset(ones[:], 1.0).then_inc(S["ones_set"], 1)
            nc.gpsimd.memset(one[:], 1.0).then_inc(S["ones_set"], 1)
            wait(pool, "ones_set", 2)

            def split(n):
                high, low = parts(n)
                wait_weights(pool, n)
                raw = stage[:, n % 4]
                if n >= 2 * WG:
                    nc.gpsimd.tensor_tensor(high, raw, one[:].unsqueeze(2).to_broadcast([P, 4, 512]), ALU.mult).then_inc(S["w_high"], 1)
                pool.wait_ge(S["w_high"], n + 1)
                nc.gpsimd.tensor_tensor(low, raw, high.bitcast(F32), ALU.subtract).then_inc(S["w_split"], 1)
                if n + 4 < 2 * WG * E:
                    pool.wait_ge(S["w_split"], n + 1)
                    weights(pool, n + 4)

            for n in range(4):
                split(n)
            wait(pool, "slots_done", 2)
            pool.wait_ge(S["n_loaded"], 16 * 4)
            for i in range(NT):
                for k in range(2):
                    pool.indirect_dma_start(
                        out=xs_d, out_offset=bass.IndirectOffsetOnAxis(ap=index[:, k, i:i + 1], axis=0),
                        in_=xn[i // 4][:, i % 4], in_offset=None).then_inc(S["n_scattered"], 16)
            pool.wait_ge(S["n_scattered"], 32 * NT)
            for n in range(4, 2 * WG):
                split(n)
            wait(pool, "tiles_done", 1)
            for e in range(1, E):
                before = counts(pool, e)[1]
                for n in range(2 * WG * e, 2 * WG * (e + 1)):
                    g = n % (2 * WG) // 2
                    wait(pool, "l2_mm" if n % 2 else "h_mm", before * HC + (g + 1) * CW - HC)
                    pool.sem_inc(S["waited"])
                    split(n)

            last = counts(pool, E)[1]
            wait(pool, "y_stored", last * 16)
            pool.sem_inc(S["waited"])
            for i in range(NT):
                for k in range(2):
                    pool.indirect_dma_start(
                        out=back[k][:, i // 4, i % 4], out_offset=None, in_=xs_d,
                        in_offset=bass.IndirectOffsetOnAxis(ap=index[:, k, i:i + 1], axis=0)).then_inc(r_gathered[i // 4], 16)

        @block.vector
        def _(dve):
            start(dve, "step slots_done tiles_done x_split h_high h_split y_done combined")

            step = [0]

            def then(ins):
                step[0] += 1
                ins.then_inc(S["step"], 1)
                wait(dve, "step", step[0])

            def over_e(a):
                return a.unsqueeze(2).to_broadcast([TT, NT, E])

            v = nc.vector
            wait(dve, "lg_loaded", 16)
            then(v.tensor_reduce(mx[:], lg[:], AX.X, ALU.max))
            then(v.tensor_tensor(p[:], lg[:], over_e(mx[:]), ALU.subtract))
            wait(dve, "exped", 1)
            then(v.tensor_reduce(total[:], p[:], AX.X, ALU.add))
            then(v.reciprocal(total[:], total[:]))
            then(v.tensor_tensor(p[:], p[:], over_e(total[:]), ALU.mult))
            for n, (a, b) in enumerate(PAIRS):
                then(v.tensor_tensor(ge[:, n], p[:, :, a], p[:, :, b], ALU.is_ge))
            for e in range(E):
                lower = [n for n, (a, b) in enumerate(PAIRS) if b == e]
                higher = [n for n, (a, b) in enumerate(PAIRS) if a == e]
                terms = [(n, 1.0) for n in lower] + [(n, -1.0) for n in higher]
                then(v.tensor_scalar(r[:, 0], ge[:, terms[0][0]], terms[0][1], float(len(higher)), ALU.mult, ALU.add))
                for n, sign in terms[1:]:
                    then(v.scalar_tensor_tensor(out=r[:, 0], in0=ge[:, n], scalar=sign, in1=r[:, 0], op0=ALU.mult, op1=ALU.add))
                then(v.tensor_scalar(m[:, :, e], r[:, 0], 1.5, None, ALU.is_lt))
            then(v.tensor_tensor(pm[:], p[:], m[:], ALU.mult))
            wait(dve, "rank_mm", 1)
            for e in range(E):
                then(v.tensor_tensor_scan(incl[:, :, e], ones[:, 0:NT], ps[0:TT, 1, 0:NT * E].rearrange("p (i e) -> p i e", e=E)[:, :, e],
                                          0.0, ALU.mult, ALU.add))
            then(v.tensor_tensor(slot[:], incl[:], ps[0:TT, 1, 0:NT * E].rearrange("p (i e) -> p i e", e=E), ALU.subtract))
            then(v.tensor_tensor(slot[:], slot[:], ps[0:TT, 0, 0:NT * E].rearrange("p (i e) -> p i e", e=E), ALU.add))
            for e in range(E):
                then(v.tensor_scalar(slot[:, :, e], slot[:, :, e], float(e * SLOTS), None, ALU.add))
            FAR = float(E * SLOTS)
            then(v.tensor_scalar(tmp[:], slot[:], FAR, None, ALU.subtract))
            then(v.tensor_tensor(tmp[:], tmp[:], m[:], ALU.mult))
            then(v.tensor_reduce(choice[:, 0], tmp[:], AX.X, ALU.min))
            then(v.tensor_scalar(choice[:, 0], choice[:, 0], FAR, None, ALU.add))
            then(v.tensor_tensor(tmp[:], slot[:], m[:], ALU.mult))
            then(v.tensor_reduce(choice[:, 1], tmp[:], AX.X, ALU.max))
            for k in range(2):
                v.tensor_copy(index[:, k], choice[:, k]).then_inc(S["slots_done"], 1)
            for e in range(E):
                then(v.tensor_scalar(taken[:, e], starts[:], incl[0:1, NT - 1, e:e + 1], None, ALU.is_lt))
            then(v.tensor_reduce(count[:], taken[:], AX.X, ALU.add))
            then(v.memset(tiles[:], 0.0))
            then(v.tensor_copy(tiles[:, 0, 0:E], count[:]))
            for e in range(E):
                then(v.tensor_tensor(tiles[:, 1, e + 1:e + 2], tiles[:, 1, e:e + 1], count[:, e:e + 1], ALU.add))
            v.tensor_copy(tiles_i[:], tiles[:]).then_inc(S["tiles_done"], 1)
            for k in range(2):
                then(v.tensor_tensor(eq[:], slot[:], over_e(choice[:, k]), ALU.is_equal))
                then(v.tensor_tensor(eq[:], eq[:], pm[:], ALU.mult))
                then(v.tensor_reduce(gate[:, k], eq[:], AX.X, ALU.add))
            wait(dve, "consts", 16 * N_CONST)
            wait(dve, "tiles_done", 1)
            for e in range(E):
                def tokens(t):
                    for b in range(2):
                        wait(dve, "x_high", 2 * t + b + 1)
                        both = slice(2 * b, 2 * b + 2)
                        v.tensor_tensor(xTl[:, both].rearrange("p k t -> p (k t)"), ps[:, X_BANK + b],
                                        xTh[:, both].rearrange("p k t -> p (k t)").bitcast(F32), ALU.subtract).then_inc(S["x_split"], 1)

                def results(i, n, t):
                    for c in range(HC):
                        k = c % RING
                        wait(dve, "h_done", n * HC + c + 1)
                        wait(dve, "l2_mm", n * HC + c - RING + 1)
                        v.tensor_copy(hh[:, k], h[:, k]).then_inc(S["h_high"], 1)
                        wait(dve, "h_high", n * HC + c + 1)
                        v.tensor_tensor(hl[:, k], h[:, k], hh[:, k].bitcast(F32), ALU.subtract).then_inc(S["h_split"], 1)
                    tokens(t + 1)
                    wait(dve, "l2_mm", n * HC + HC)
                    wait(dve, "y_stored", n * 16)
                    for s in range(HALVES):
                        v.tensor_tensor(y[:, s], ps[:, Y_BANK + s], b2[:, e], ALU.add).then_inc(S["y_done"], 1)

                expert_tiles(dve, e, tokens, results)
            dve.wait_ge(S["x2_loaded"], 16 * 4)
            for i in range(NT):
                x2 = stage[0:TT, i // 4, i % 4]
                dve.wait_ge(r_gathered[i // 4], 16 * 2 * 4)
                for k in range(2):
                    v.scalar_tensor_tensor(out=x2, in0=back[k][:, i // 4, i % 4], scalar=gate[:, k, i:i + 1],
                                           in1=x2, op0=ALU.mult, op1=ALU.add).then_inc(S["combined"], 1)
                    if k == 0:
                        wait(dve, "combined", 2 * i + 1)

        @block.scalar
        def _(act):
            start(act, "exped x_high h_done y_stored")

            wait(act, "step", 2)
            nc.scalar.activation(p[:], p[:], ACT.Exp).then_inc(S["exped"], 1)
            for n in range(2 * WG):
                wait_weights(act, n)
                nc.scalar.activation(parts(n)[0], stage[:, n % 4], ACT.Copy).then_inc(S["w_high"], 1)
            wait(act, "consts", 16 * N_CONST)
            wait(act, "tiles_done", 1)
            for e in range(E):
                def tokens(t):
                    wait(act, "x_mm", t + 1)
                    for b in range(2):
                        nc.scalar.activation(xTh[:, 2 * b:2 * b + 2].rearrange("p k t -> p (k t)"), ps[:, X_BANK + b],
                                             ACT.Copy).then_inc(S["x_high"], 1)

                def hidden(i, n, t):
                    for c in range(HC):
                        wait(act, "h_mm", n * HC + c + 1)
                        wait(act, "h_split", n * HC + c - RING + 1)
                        nc.scalar.activation(h[:, c % RING], ps[:, H_BANK + c % RING, 0:GT], ACT.Gelu,
                                             bias=b1[:, e * HC + c:e * HC + c + 1]).then_inc(S["h_done"], 1)
                    tokens(t + 1)
                    wait(act, "y_done", 2 * n + 2)
                    act.dma_start(xs_v[bass.ds(i + e * EG, 1)].rearrange("a p h d -> (a p) h d"), y[:]).then_inc(S["y_stored"], 16)

                expert_tiles(act, e, tokens, hidden)
            for i in range(1, NT, 2):
                wait(act, "combined", 2 * i + 2)
                act.dma_start(out_v[i], stage[0:TT, i // 4, i % 4]).then_inc(S["out_stored"], 16)

        @block.tensor
        def _(pe):
            start(pe, "rank_mm x_mm h_mm l2_mm")

            wait(pe, "consts", 16 * N_CONST)
            wait(pe, "ones_set", 2)
            wait(pe, "step", STEPS_TO_MASK)
            for bank, w in ((0, upper), (1, ones)):
                ins = nc.tensor.matmul(ps[0:TT, bank, 0:NT * E], w[:], m[:].rearrange("p i e -> p (i e)"), start=True, stop=True)
            ins.then_inc(S["rank_mm"], 1)
            wait(pe, "tiles_done", 1)

            def products(out, stationary, moving, first, last):
                (sh, sl), (mh, ml) = stationary, moving
                nc.tensor.matmul(out, sh, mh, start=first, stop=False)
                nc.tensor.matmul(out, sh, ml, start=False, stop=False)
                return nc.tensor.matmul(out, sl, mh, start=False, stop=last)

            for e in range(E):
                def tokens(t):
                    pe.wait_ge(S["x_loaded"], 16 * t + 17)
                    wait(pe, "x_split", 2 * t)
                    for q in range(KC):
                        for s in range(HALVES):
                            at = (q % 2) * GT + s * P
                            ins = nc.tensor.transpose(ps[:, X_BANK + q // 2, at:at + P], xt[:, s, q * P:(q + 1) * P], ident[:])
                    ins.then_inc(S["x_mm"], 1)

                def tile(i, n, t):
                    wait(pe, "x_split", 2 * t + 2)
                    for step in range(HC + AHEAD):
                        if step < HC:
                            c = step
                            g, w = c // CW, slice(c % CW * P, c % CW * P + P)
                            if c % CW == 0:
                                pe.wait_ge(S["w_split"], 2 * WG * e + 2 * g + 1)
                            wait(pe, "h_done", n * HC + c - RING + 1)
                            for q in range(KC):
                                ins = products(ps[:, H_BANK + c % RING, 0:GT], (w1h[:, g, q, w], w1l[:, g, q, w]),
                                               (xTh[:, q], xTl[:, q]), q == 0, q == KC - 1)
                            ins.then_inc(S["h_mm"], 1)
                        if step == HC - 1:
                            tokens(t + 1)
                        if step >= AHEAD:
                            c = step - AHEAD
                            g, k = c // CW, c % RING
                            if c % CW == 0:
                                pe.wait_ge(S["w_split"], 2 * WG * e + 2 * g + 2)
                            if c == 0:
                                wait(pe, "y_done", 2 * n)
                            wait(pe, "h_split", n * HC + c + 1)
                            for s in range(HALVES):
                                rows = slice(s * P, s * P + P)
                                ins = products(ps[:, Y_BANK + s], (hh[:, k, rows], hl[:, k, rows]),
                                               (w2h[:, g, c % CW], w2l[:, g, c % CW]), c == 0, c == HC - 1)
                            ins.then_inc(S["l2_mm"], 1)

                expert_tiles(pe, e, tokens, tile)


def decoder(nc, a, out):
    def scratch(name, shape):
        return nc.dram_tensor(name, shape, F32, kind="Internal").ap()

    xb_d, z_d, dt_d, u_d, y_d = (scratch(n, (CC, P, T)) for n in ("xb_d", "z_d", "dt_d", "u_d", "y_d"))
    bc_d = scratch("bc_d", (2 * NS, T))
    k_d, v_d = scratch("k_d", (B, KC, P, CTX)), scratch("v_d", (B, NC, CT, DM))
    x2_d, xn_d, logits_d = (scratch(n, (B, TT, 2, w)) for n, w in (("x2_d", DM), ("xn_d", DM), ("logits_d", E)))
    xs_d = scratch("xs_d", (XS, DM))
    s, t, f = "L0_attn_", "L0_xattn_", "L0_ffn_"
    mamba_in(nc, a["x"], a[s + "W_in"], a[s + "conv_w"], a[s + "conv_b"], a[s + "W_x"], a[s + "W_dt"], a[s + "b_dt"],
             a["identity"], xb_d, z_d, dt_d, u_d, bc_d, xs_d)
    state_space(nc, a[s + "A_log"], a[s + "D"], a["identity"], xb_d, z_d, dt_d, u_d, bc_d, y_d,
                a["ctxT"], a[t + "Wk"], a[t + "bk"], a[t + "Wv"], k_d, v_d)
    attention(nc, a["x"], k_d, v_d, y_d, a[s + "W_out"], a[t + "Wq"], a[t + "bq"], a[t + "bv"], a[t + "Wo"], a[t + "bo"], a[f + "rW1"], a[f + "rb1"], a[f + "rW2"], a[f + "rb2"],
              a["identity"], x2_d, xn_d, logits_d)
    experts(nc, a[f + "We1"], a[f + "be1"], a[f + "We2"], a[f + "be2"], a["upper"], a["identity"], a["tile_starts"],
            x2_d, xn_d, logits_d, xs_d, out)


_INS = ["x", "ctx_512"] + ["L0_attn_" + n for n in ("W_in", "conv_w", "conv_b", "W_x", "W_dt", "b_dt", "A_log", "D", "W_out")] \
    + ["L0_xattn_" + n for n in ("Wq", "bq", "Wk", "bk", "Wv", "bv", "Wo", "bo")] \
    + ["L0_ffn_" + n for n in ("rW1", "rb1", "rW2", "rb2", "We1", "be1", "We2", "be2")]
_COLUMNS = ["L0_attn_conv_b", "L0_attn_b_dt", "L0_attn_D", "L0_xattn_bq", "L0_xattn_bk", "L0_xattn_bv", "L0_ffn_rb1", "L0_ffn_be1"]


def kernel(**inputs):
    import numpy as np
    import concourse.bacc as bacc
    from concourse.bass_utils import run_bass_kernel_spmd

    arrays = {name: np.asarray(inputs[name]) for name in _INS}
    for name in _COLUMNS:
        arrays[name] = arrays[name].reshape(-1, P).T
    arrays["ctxT"] = arrays.pop("ctx_512").transpose(0, 2, 1)
    arrays["identity"] = np.eye(P, dtype=np.float32)
    arrays["upper"] = np.triu(np.ones((TT, TT), np.float32), 1)
    arrays["tile_starts"] = np.arange(0, SLOTS, GT, dtype=np.float32)[None]
    arrays = {name: np.ascontiguousarray(a) for name, a in arrays.items()}

    nc = bacc.Bacc("TRN2", target_bir_lowering=False, num_devices=1)
    a = {name: nc.dram_tensor("in_" + name, v.shape, F32, kind="ExternalInput").ap() for name, v in arrays.items()}
    out = nc.dram_tensor("out", (B, L, DM), F32, kind="ExternalOutput").ap()
    decoder(nc, a, out)
    r = run_bass_kernel_spmd(nc, [{"in_" + name: v for name, v in arrays.items()}], core_ids=[0])
    return r.results[0]["out"]
```

```python
from contextlib import ExitStack

import concourse.bass as bass
from concourse import mybir

F32 = mybir.dt.float32
F32R = mybir.dt.float32r
I32 = mybir.dt.int32
U32 = mybir.dt.uint32
ALU = mybir.AluOpType
ACT = mybir.ActivationFunctionType
AX = mybir.AxisListType

P = 128
EPS = 1e-5

B, L, DM = 8, 224, 512
T = B * L
TT = 112
NT = T // TT
KC = DM // P
DI = 1024
CC = DI // P
TAPS = 4
R, NS = 64, 16
XR = R + 2 * NS
GB = 2
G = B // GB
GL = GB * L
HS = NS // 2
HBUF, DBUF = 4, 2
UB_FREE = 3
CTX, CD = 750, 256
CT = 125
NC = CTX // CT
CK = CD // P
HEADS, DK = 16, 32
HALF = CTX // 2
RH = 1024
RC = RH // P
E, H = 4, 2048
HC = H // P
SLOTS = T
GT = 2 * P
EG = SLOTS // GT
XS = (E * SLOTS // 512 + 1) * 512


def mamba_in(nc, x, W_in, conv_w, conv_b, W_x, W_dt, b_dt, ident_in, xb_d, z_d, dt_d, u_d, bc_d, xs_d):
    ctx = ExitStack()
    sems = []
    with ctx:
        def sb(name, shape, dt=F32):
            return ctx.enter_context(nc.sbuf_tensor("a_" + name, shape, dt))

        def sem(name):
            sems.append(nc.alloc_semaphore(name="a_" + name))
            return sems[-1]

        x_sb = sb("x", [TT, NT, DM])
        xn = sb("xn", [TT, 2, DM])
        xnTh, xnTl = sb("xnTh", [P, KC, T], F32R), sb("xnTl", [P, KC, T], F32R)
        st = sb("st", [TT, NT, 6])
        mv = sb("mv", [TT, NT, 2])
        rstd = sb("rstd", [TT, NT])
        ident = sb("ident", [P, P])
        win = sb("win", [P, 2, KC, P])
        winh, winl = sb("winh", [P, 2, KC, P], F32R), sb("winl", [P, 2, KC, P], F32R)
        one = sb("one", [P, 1])
        xpad = sb("xpad", [P, B, TAPS - 1 + L])
        acc = sb("acc", [P, 2, T])
        zs = sb("zs", [P, T])
        xb = sb("xb", [P, CC, T])
        cw = sb("cw", [P, CC, TAPS])
        cb = sb("cb", [P, CC])
        wx = sb("wx", [P, CC, XR])
        xdbl = sb("xdbl", [XR, T])
        wdt = sb("wdt", [R, DI])
        bdt = sb("bdt", [P, CC])
        zero = sb("zero", [P, 1024])
        ps = ctx.enter_context(nc.psum_tensor("a_ps", [P, 8, 512], F32))

        loaded = sem("loaded")
        x_loaded = [sem(f"x_loaded{g}") for g in range(G)]
        w_in_loaded = [sem("xb_w_loaded"), sem("z_w_loaded")]
        stats_done, mv_done, var_done, std_done, rstd_done = (sem(n) for n in ("stats", "mv", "var", "std", "rstd"))
        xn_done, transposed, xnT_high, xnT_split = sem("xn_done"), sem("transposed"), sem("xnT_high"), sem("xnT_split")
        w_high, w_split = [sem("w_high0"), sem("w_high1")], [sem("w_split0"), sem("w_split1")]
        pad_zeroed, zero_set = sem("pad_zeroed"), sem("zero_set")
        xb_mm, z_mm, padded, conv_step, conv_done, silu_done, z_done = (
            sem(n) for n in ("xb_mm", "z_mm", "padded", "conv_step", "conv_done", "silu_done", "z_done"))
        z_stored, xb_stored, zero_stored = sem("z_stored"), sem("xb_stored"), sem("zero_stored")
        xdbl_mm, xdbl_done, xdbl_stored = sem("xdbl_mm"), sem("xdbl_done"), sem("xdbl_stored")
        dt_mm, ln_done, soft_step, relu_done, dt_done, u_done, u_stored = (
            sem(n) for n in ("dt_mm", "ln_done", "soft_step", "relu_done", "dt_done", "u_done", "u_stored"))
        dt_stored = [sem("dt_stored0"), sem("dt_stored1")]
        N_LOADS = 7

        win_v = W_in.rearrange("(k p) n -> p k n", p=P)
        block = ctx.enter_context(nc.Block())

        @block.sync
        def _(sp):
            sp.sem_inc(z_stored, 1)
            x_v = x.rearrange("b (u p) d -> p (b u) d", p=TT)
            for g in range(G):
                sp.dma_start(x_sb[:, 4 * g:4 * g + 4], x_v[:, 4 * g:4 * g + 4]).then_inc(x_loaded[g], 16)
            sp.dma_start(ident[:], ident_in).then_inc(loaded, 16)
            sp.dma_start(cw[:], conv_w.rearrange("(c p) k -> p c k", p=P)).then_inc(loaded, 16)
            sp.dma_start(cb[:], conv_b).then_inc(loaded, 16)
            sp.dma_start(wx[:], W_x.rearrange("(c p) n -> p c n", p=P)).then_inc(loaded, 16)
            sp.dma_start(wdt[:], W_dt).then_inc(loaded, 16)
            sp.dma_start(bdt[:], b_dt).then_inc(loaded, 16)
            sp.dma_start(win[:, 0], win_v[:, :, 0:P]).then_inc(w_in_loaded[0], 16)
            sp.dma_start(win[:, 1], win_v[:, :, DI:DI + P]).then_inc(w_in_loaded[1], 16)
            with sp.Fori(0, CC - 1) as c:
                sp.wait_ge(xb_mm, c + 1)
                sp.dma_start(win[:, 0], win_v[:, :, bass.ds(c * P + P, P)]).then_inc(w_in_loaded[0], 16)
                sp.wait_ge(z_mm, c + 1)
                sp.dma_start(win[:, 1], win_v[:, :, bass.ds(c * P + (DI + P), P)]).then_inc(w_in_loaded[1], 16)
                sp.wait_ge(z_done, c + 2)
                sp.dma_start(z_d[bass.ds(c, 1)].rearrange("a p t -> (a p) t"), zs[:]).then_inc(z_stored, 16)
            sp.wait_ge(z_done, CC + 1)
            sp.dma_start(z_d[CC - 1], zs[:]).then_inc(z_stored, 16)
            sp.wait_ge(silu_done, CC + 1)
            sp.dma_start(xb_d.rearrange("c p t -> p c t"), xb[:]).then_inc(xb_stored, 16)
            sp.wait_ge(xdbl_done, 1)
            sp.dma_start(bc_d, xdbl[R:XR, :]).then_inc(xdbl_stored, 16)
            for c in range(CC):
                sp.wait_ge(dt_done, c + 1)
                sp.dma_start(dt_d[c], acc[:, c % 2]).then_inc(dt_stored[c % 2], 16)
                sp.wait_ge(u_done, c + 1)
                sp.dma_start(u_d[c], xb[:, c]).then_inc(u_stored, 16)
            sp.wait_ge(z_stored, 16 * CC + 1)
            sp.wait_ge(xb_stored, 16)
            sp.wait_ge(xdbl_stored, 16)
            for s in dt_stored:
                sp.wait_ge(s, 16 * CC // 2)
            sp.wait_ge(u_stored, 16 * CC)

        @block.gpsimd
        def _(pool):
            nc.gpsimd.memset(zero[:], 0.0).then_inc(zero_set, 1)
            nc.gpsimd.memset(one[:], 1.0).then_inc(zero_set, 1)
            pool.wait_ge(zero_set, 2)

            def split(c, half):
                pool.wait_ge(w_in_loaded[half], c * 16 + 16)
                raw = win[:, half]
                nc.gpsimd.tensor_tensor(winh[:, half], raw, one[:].unsqueeze(2).to_broadcast([P, KC, P]),
                                        ALU.mult).then_inc(w_high[half], 1)
                pool.wait_ge(w_high[half], c + 1)
                nc.gpsimd.tensor_tensor(winl[:, half], raw, winh[:, half].bitcast(F32), ALU.subtract).then_inc(w_split[half], 1)

            for g in range(G):
                pool.wait_ge(x_loaded[g], 16)
            for half in range(2):
                split(0, half)
            xs_v = xs_d.rearrange("(a p r) d -> a p (r d)", p=P, r=2)
            with pool.Fori(0, XS // (P * 2)) as a:
                pool.dma_start(xs_v[bass.ds(a, 1)].rearrange("a p n -> (a p) n"), zero[:]).then_inc(zero_stored, 16)
            with pool.Fori(1, CC) as c:
                for half in range(2):
                    split(c, half)
            for c in range(CC):
                pool.wait_ge(xb_stored, 16)
                pool.wait_ge(xdbl_mm, 1)
                pool.wait_ge(dt_done, c + 1)
                nc.gpsimd.tensor_tensor(xb[:, c], xb[:, c], acc[:, c % 2], ALU.mult).then_inc(u_done, 1)
            pool.wait_ge(zero_stored, 16 * (XS // (P * 2)))

        @block.vector
        def _(dve):
            nc.vector.memset(xpad[:, :, 0:TAPS - 1], 0.0).then_inc(pad_zeroed, 1)
            for i in range(NT):
                if i % 4 == 0:
                    dve.wait_ge(x_loaded[i // 4], 16)
                nc.vector.bn_stats(st[:, i], x_sb[:, i]).then_inc(stats_done, 1)
            for i in range(NT):
                dve.wait_ge(stats_done, i + 1)
                nc.vector.bn_aggr(mv[:, i], st[:, i]).then_inc(mv_done, 1)
            dve.wait_ge(mv_done, NT)
            nc.vector.tensor_scalar(rstd[:], mv[:, :, 1], EPS, None, ALU.add).then_inc(var_done, 1)
            dve.wait_ge(std_done, 1)
            nc.vector.reciprocal(rstd[:], rstd[:]).then_inc(rstd_done, 1)
            dve.wait_ge(rstd_done, 1)
            def low(i):
                dve.wait_ge(xnT_high, i + 1)
                cols = slice(i * TT, (i + 1) * TT)
                nc.vector.tensor_tensor(xnTl[:, :, cols], ps[:, i % 2, 0:KC * TT].rearrange("p (k t) -> p k t", k=KC),
                                        xnTh[:, :, cols].bitcast(F32), ALU.subtract).then_inc(xnT_split, 1)

            for i in range(NT):
                if i >= 2:
                    dve.wait_ge(transposed, i - 1)
                nc.vector.tensor_scalar(xn[:, i % 2], x_sb[:, i], mv[:, i, 0:1], rstd[:, i:i + 1],
                                        ALU.subtract, ALU.mult).then_inc(xn_done, 1)
                if i >= 1:
                    low(i - 1)
            low(NT - 1)

            def taps(c, s):
                cwc = cw[:, c] if isinstance(c, int) else cw[:, bass.ds(c, 1)].rearrange("p a k -> p (a k)")
                out = acc[:, 0].rearrange("p (b t) -> p b t", b=B)
                for k in range(TAPS):
                    if k == 0:
                        nc.vector.tensor_scalar(out, xpad[:, :, 0:L], cwc[:, 0:1], None,
                                                ALU.mult).then_inc(conv_step, 1)
                    else:
                        dve.wait_ge(conv_step, s + k)
                        ins = nc.vector.scalar_tensor_tensor(out=out, in0=xpad[:, :, k:k + L], scalar=cwc[:, k:k + 1],
                                                             in1=out, op0=ALU.mult, op1=ALU.add)
                        ins.then_inc(conv_done if k == TAPS - 1 else conv_step, 1)

            dve.wait_ge(loaded, 16 * (N_LOADS - 1))
            with dve.Fori(0, CC) as c:
                dve.wait_ge(padded, c * G + (G + 1))
                dve.wait_ge(silu_done, c + 1)
                taps(c, c * (TAPS - 1))
            dve.wait_ge(xdbl_mm, 1)
            nc.vector.tensor_copy(xdbl[:].rearrange("p (g t) -> p g t", g=G), ps[0:XR, 0:G, 0:GL]).then_inc(xdbl_done, 1)
            dve.wait_ge(z_stored, 16 * CC + 1)
            for c in range(CC):
                q = 4 * (c % 2)
                dve.wait_ge(soft_step, 2 * c + 1)
                if c >= 1:
                    dve.wait_ge(dt_done, c)
                nc.vector.tensor_scalar(zs[:].rearrange("p (g t) -> p g t", g=G), ps[:, q:q + 4, 0:GL], bdt[:, c:c + 1],
                                        0.0, ALU.add, ALU.max).then_inc(relu_done, 1)
                dve.wait_ge(relu_done, c + 1)
                dve.wait_ge(ln_done, c + 1)
                nc.vector.tensor_tensor(acc[:, c % 2], acc[:, c % 2], zs[:], ALU.add).then_inc(dt_done, 1)

        @block.scalar
        def _(act):
            for s in (padded, z_done, silu_done):
                act.sem_inc(s, 1)
            act.wait_ge(var_done, 1)
            nc.scalar.activation(rstd[:], rstd[:], ACT.Sqrt).then_inc(std_done, 1)
            for i in range(NT):
                act.wait_ge(transposed, i + 1)
                nc.scalar.activation(xnTh[:, :, i * TT:(i + 1) * TT],
                                     ps[:, i % 2, 0:KC * TT].rearrange("p (k t) -> p k t", k=KC),
                                     ACT.Copy).then_inc(xnT_high, 1)
            act.wait_ge(pad_zeroed, 1)
            act.wait_ge(loaded, 16 * (N_LOADS - 1))

            def evacuate(c):
                for g in range(G):
                    act.wait_ge(xb_mm, c + 1)
                    nc.scalar.activation(xpad[:, GB * g:GB * g + GB, TAPS - 1:],
                                         ps[:, g, 0:GL].rearrange("p (b t) -> p b t", b=GB),
                                         ACT.Copy).then_inc(padded, 1)

            def gates(c):
                act.wait_ge(z_mm, c + 1)
                act.wait_ge(z_stored, c * 16 + 1)
                nc.scalar.activation(zs[:].rearrange("p (g t) -> p g t", g=G), ps[:, G:2 * G, 0:GL],
                                     ACT.Silu).then_inc(z_done, 1)
                act.wait_ge(conv_done, c + 1)
                out = xb[:, bass.ds(c, 1)].rearrange("p a t -> p (a t)")
                nc.scalar.activation(out, acc[:, 0], ACT.Silu,
                                     bias=cb[:, bass.ds(c, 1)]).then_inc(silu_done, 1)

            with act.Fori(0, CC) as c:
                evacuate(c)
                gates(c)
            for c in range(CC):
                q, a = 4 * (c % 2), acc[:, c % 2]
                av = a.rearrange("p (g t) -> p g t", g=G)
                act.wait_ge(dt_mm, c + 1)
                if c >= 2:
                    act.wait_ge(dt_stored[c % 2], 16 * (c // 2))
                    act.wait_ge(u_done, c - 1)
                nc.scalar.activation(av, ps[:, q:q + 4, 0:GL], ACT.Abs, bias=bdt[:, c:c + 1]).then_inc(soft_step, 1)
                act.wait_ge(soft_step, 2 * c + 1)
                nc.scalar.activation(a, a, ACT.Exp, scale=-1.0).then_inc(soft_step, 1)
                act.wait_ge(soft_step, 2 * c + 2)
                nc.scalar.activation(a, a, ACT.Ln, bias=1.0).then_inc(ln_done, 1)

        @block.tensor
        def _(pe):
            pe.wait_ge(loaded, 16 * (N_LOADS - 1))
            for i in range(NT):
                pe.wait_ge(xn_done, i + 1)
                if i >= 2:
                    pe.wait_ge(xnT_split, i - 1)
                for k in range(KC):
                    ins = nc.tensor.transpose(ps[:, i % 2, k * TT:(k + 1) * TT], xn[:, i % 2, k * P:(k + 1) * P],
                                              ident[0:TT, 0:TT])
                ins.then_inc(transposed, 1)
            pe.wait_ge(xnT_split, NT)
            with pe.Fori(0, CC) as c:
                for half, done in ((0, xb_mm), (1, z_mm)):
                    pe.wait_ge(w_split[half], c + 1)
                    pe.wait_ge(padded if half == 0 else z_done, c * G + 1 if half == 0 else c + 1)
                    for g in range(G):
                        for k in range(KC):
                            out, cols = ps[:, G * half + g, 0:GL], slice(g * GL, (g + 1) * GL)
                            nc.tensor.matmul(out, winh[:, half, k], xnTh[:, k, cols], start=(k == 0), stop=False)
                            nc.tensor.matmul(out, winh[:, half, k], xnTl[:, k, cols], start=False, stop=False)
                            ins = nc.tensor.matmul(out, winl[:, half, k], xnTh[:, k, cols], start=False, stop=(k == KC - 1))
                    ins.then_inc(done, 1)
            pe.wait_ge(silu_done, CC + 1)
            pe.wait_ge(z_done, CC + 1)
            for g in range(G):
                for c in range(CC):
                    ins = nc.tensor.matmul(ps[0:XR, g, 0:GL], wx[:, c], xb[:, c, g * GL:(g + 1) * GL],
                                           start=(c == 0), stop=(c == CC - 1))
            ins.then_inc(xdbl_mm, 1)
            pe.wait_ge(xdbl_done, 1)
            for c in range(CC):
                if c >= 2:
                    pe.wait_ge(dt_done, c - 1)
                for g in range(G):
                    ins = nc.tensor.matmul(ps[:, 4 * (c % 2) + g, 0:GL], wdt[:, c * P:(c + 1) * P],
                                           xdbl[0:R, g * GL:(g + 1) * GL], start=True, stop=True)
                ins.then_inc(dt_mm, 1)
    nc.clear_and_free_semaphores(sems)
    nc.all_engine_barrier()


def state_space(nc, A_log, D, ident_in, xb_d, z_d, dt_d, u_d, bc_d, y_d, ctxT_in, Wk, bk, Wv, kh_d, kl_d, v_d):
    ctx = ExitStack()
    with ctx:
        def sb(name, shape, dt=F32):
            return ctx.enter_context(nc.sbuf_tensor("s_" + name, shape, dt))

        def sem(name):
            return ctx.enter_context(nc.semaphore("s_" + name))

        ident = sb("ident", [P, P])
        A = sb("A", [P, CC, NS])
        Dv = sb("D", [P, CC])
        Bc = sb("Bc", [P, NS, GL])
        Cc = sb("Cc", [P, 2, NS, GL])
        decay = sb("decay", [P, DBUF, HS, GL])
        h = sb("h", [P, HBUF, HS, GL])
        early = sb("early", [P, 2, 2, GL])
        late = sb("late", [P, 2, 2, GL])
        wk, wv, bkc = sb("wk", [P, CK, DM]), sb("wv", [P, CK, DM]), sb("bkc", [P, KC])
        cxT = sb("cxT", [P, CK, CTX])
        kh, kl = sb("kh", [P, CTX], F32R), sb("kl", [P, CTX], F32R)
        v = sb("v", [CT, 2, DM])
        ps = ctx.enter_context(nc.psum_tensor("s_ps", [P, 2, 512], F32))
        kps = ctx.enter_context(nc.psum_tensor("s_kps", [P, 2, 2, 512], F32))
        vps = ctx.enter_context(nc.psum_tensor("s_vps", [P, 2, 512], F32))

        consts = sem("consts")
        a_step, a_done = sem("a_step"), sem("a_done")
        b_loaded = [sem("b_loaded0"), sem("b_loaded1")]
        c_loaded = [sem("c_loaded0"), sem("c_loaded1")]
        early_loaded = [sem("early_loaded0"), sem("early_loaded1")]
        late_loaded = [sem("late_loaded0"), sem("late_loaded1")]
        y_stored = [sem("y_stored0"), sem("y_stored1")]
        edge_done = sem("edge_done")
        decay_done, ub_done, scan_done, hc_done, sum_done, y1_done, y_done = (
            sem(n) for n in ("decay_done", "ub_done", "scan_done", "hc_done", "sum_done", "y1_done", "y_done"))
        ctx_loaded, kv_free, k_mm, v_mm, k_done, k_split, v_done, kh_stored, kl_stored = (
            sem(n) for n in ("ctx_loaded", "kv_free", "k_mm", "v_mm", "k_done", "k_split", "v_done", "kh_stored", "kl_stored"))
        v_stored = [sem("v_stored0"), sem("v_stored1")]
        V_TILES = [(0, 1), (2, 3), (4,), (5,)]
        block = ctx.enter_context(nc.Block())

        def batch(gg, pair, c):
            return gg * (2 * GB) + (GB * pair + c // 4)

        UNITS = 2 * CC

        def unit(gg, pair, n):
            return gg * (2 * UNITS) + (pair * UNITS + n)

        def chunk(gg, pair, n):
            return gg * (2 * CC) + (pair * CC + n)

        def cols(t, gg, pair, c=0):
            if c < 0:
                pair = pair - 1
            return t[:, bass.ds(gg * (2 * GL) + pair * GL, GL)]

        def behind(eng, gg, pair, c, body):
            if c >= 0 or pair > 0 or gg is LAST:
                body(gg, pair, c)
            else:
                with eng.If(gg > 0):
                    body(nc.s_assert_within(gg, 1, LAST - 1, skip_runtime_bounds_check_because="the branch is for gg > 0"),
                         pair, c)

        LAST = G // 2

        def wait_slot(eng, loaded, gg, pair, c, dmas):
            eng.wait_ge(loaded[c % 2], gg * (16 * dmas * CC) + 16 * dmas * ((pair * CC + c) // 2 + 1))

        @block.sync
        def _(sp):
            sp.dma_start(ident[:], ident_in).then_inc(consts, 16)
            sp.dma_start(A[:], A_log.rearrange("(c p) n -> p c n", p=P)).then_inc(consts, 16)
            sp.dma_start(Dv[:], D).then_inc(consts, 16)
            sp.dma_start(wk[:], Wk.rearrange("(k p) n -> p k n", p=P)).then_inc(consts, 16)
            sp.dma_start(wv[:], Wv.rearrange("(k p) n -> p k n", p=P)).then_inc(consts, 16)
            sp.dma_start(bkc[:], bk).then_inc(consts, 16)
            with sp.Fori(0, G // 2) as gg:
                for pair in range(2):
                    for c in range(CC):
                        sp.wait_ge(decay_done, unit(gg, pair, 2 * c + 1))
                        sp.wait_ge(ub_done, unit(gg, pair, 2 * c + 1))
                        for j, src in enumerate((dt_d, u_d)):
                            sp.dma_start(early[:, c % 2, j], cols(src[c], gg, pair)).then_inc(early_loaded[c % 2], 16)
                        if c == 0:
                            for s in range(2):
                                sp.wait_ge(ub_done, unit(gg, pair, UB_FREE - 1 + s))
                                sp.dma_start(Bc[:, s * HS:(s + 1) * HS], cols(bc_d[s * HS:(s + 1) * HS], gg, pair).partition_broadcast(P)
                                             ).then_inc(b_loaded[s], 16)
                        if c % 4 == 0:
                            b = batch(gg, pair, c)
                            sp.wait_ge(kv_free, b + 1)
                            sp.dma_start(cxT[:], ctxT_in[bass.ds(b, 1)].rearrange("a (k p) t -> p (a k) t", p=P)).then_inc(ctx_loaded, 16)

        @block.gpsimd
        def _(pool):
            nc.gpsimd.sem_inc(ub_done, UB_FREE)
            with pool.Fori(0, G // 2) as gg:
                for pair in range(2):
                    for c in range(CC):
                        wait_slot(pool, early_loaded, gg, pair, c, 2)
                        for s in range(2):
                            if c == 0:
                                pool.wait_ge(b_loaded[s], gg * 32 + pair * 16 + 16)
                            pool.wait_ge(sum_done, unit(gg, pair, 2 * c + s + 1))
                            u = early[:, c % 2, 1].unsqueeze(1).to_broadcast([P, HS, GL])
                            nc.gpsimd.tensor_tensor(h[:, (2 * c + s) % HBUF], Bc[:, s * HS:(s + 1) * HS], u,
                                                    ALU.mult).then_inc(ub_done, 1)

        @block.scalar
        def _(act):
            act.sem_inc(decay_done, UB_FREE)
            for s in (kh_stored, kl_stored, *v_stored, *y_stored, k_done, v_done):
                act.sem_inc(s, 1)
            act.wait_ge(consts, 96)
            nc.scalar.activation(A[:], A[:], ACT.Exp).then_inc(a_step, 1)
            act.wait_ge(a_step, 1)
            nc.scalar.activation(A[:], A[:], ACT.Copy, scale=-1.0).then_inc(a_done, 1)
            act.wait_ge(a_done, 1)

            def store(gg, pair, c):
                act.wait_ge(y_done, chunk(gg, pair, c + 3))
                act.dma_start(cols(y_d[c % CC], gg, pair, c), late[:, c % 2, 0]).then_inc(y_stored[c % 2], 16)

            def keys_values(gg, pair, c):
                b, q = batch(gg, pair, c), c % 4
                act.wait_ge(k_mm, b * KC + (q + 1))
                act.wait_ge(kh_stored, b * (16 * KC) + (16 * q + 1))
                act.wait_ge(k_split, b * KC + (q + 2))
                nc.scalar.activation(kh[:].rearrange("p (a c) -> p a c", a=2), kps[:, c % 2, :, 0:HALF], ACT.Identity,
                                     bias=bkc[:, q:q + 1]).then_inc(k_done, 1)
                for i in V_TILES[q]:
                    act.wait_ge(v_mm, b * NC + (i + 1))
                    act.wait_ge(v_stored[i % 2], b * (16 * NC // 2) + (16 * (i // 2) + 1))
                    nc.scalar.activation(v[:, i % 2], vps[0:CT, i % 2], ACT.Copy).then_inc(v_done, 1)
                act.wait_ge(k_done, b * KC + (q + 2))
                act.dma_start(kh_d[bass.ds(b, 1), q].rearrange("a p t -> (a p) t"), kh[:].bitcast(F32)).then_inc(kh_stored, 16)
                for i in V_TILES[q]:
                    act.wait_ge(v_done, b * NC + (i + 2))
                    act.dma_start(v_d[bass.ds(b, 1), i].rearrange("a p d -> (a p) d"), v[:, i % 2]).then_inc(v_stored[i % 2], 16)

            def store_low_keys(gg, pair, c):
                b, q = batch(gg, pair, c), c % 4
                act.wait_ge(k_split, b * KC + (q + 3))
                act.dma_start(kl_d[bass.ds(b, 1), q].rearrange("a p t -> (a p) t"), kl[:].bitcast(F32)).then_inc(kl_stored, 16)

            with act.Fori(0, G // 2) as gg:
                for pair in range(2):
                    act.wait_ge(hc_done, unit(gg, pair, 1))
                    act.dma_start(Cc[:, pair], cols(bc_d[NS:], gg, pair).partition_broadcast(P)).then_inc(c_loaded[pair], 16)
                    for c in range(CC):
                        wait_slot(act, early_loaded, gg, pair, c, 2)
                        for s in range(2):
                            act.wait_ge(scan_done, unit(gg, pair, 2 * c + s + 1))
                            for n in range(HS):
                                ins = nc.scalar.activation(decay[:, s, n], early[:, c % 2, 0], ACT.Exp,
                                                           scale=A[:, c, s * HS + n:s * HS + n + 1])
                            ins.then_inc(decay_done, 1)
                            if s == 0:
                                behind(act, gg, pair, c - 1, keys_values)
                                behind(act, gg, pair, c - 2, store)
                                behind(act, gg, pair, c - 2, store_low_keys)
                        act.wait_ge(y_stored[c % 2], gg * (16 * CC) + (16 * (pair * CC // 2 + c // 2) + 1))
                        for j, src in enumerate((xb_d, z_d)):
                            act.dma_start(late[:, c % 2, j], cols(src[c], gg, pair)).then_inc(late_loaded[c % 2], 16)
            keys_values(LAST, 0, -1)
            for c in (-2, -1):
                store(LAST, 0, c)
                store_low_keys(LAST, 0, c)
            for s in y_stored:
                act.wait_ge(s, 16 * G * CC // 2 + 1)
            act.wait_ge(kh_stored, 16 * B * KC + 1)
            act.wait_ge(kl_stored, 16 * B * KC + 1)
            for s in v_stored:
                act.wait_ge(s, 16 * B * NC // 2 + 1)

        @block.vector
        def _(dve):
            def outputs(gg, pair, c):
                wait_slot(dve, late_loaded, gg, pair, c, 2)
                dve.wait_ge(sum_done, unit(gg, pair, 2 * c + 2 + HBUF))
                xb = late[:, c % 2, 0]
                nc.vector.scalar_tensor_tensor(out=xb, in0=xb, scalar=Dv[:, c % CC:c % CC + 1],
                                               in1=ps[:, c % 2, 0:GL], op0=ALU.mult, op1=ALU.add).then_inc(y1_done, 1)
                dve.wait_ge(y1_done, chunk(gg, pair, c + 3))
                nc.vector.tensor_tensor(xb, xb, late[:, c % 2, 1], ALU.mult).then_inc(y_done, 1)

            def low_keys(gg, pair, c):
                b, q = batch(gg, pair, c), c % 4
                dve.wait_ge(k_done, b * KC + (q + 2))
                dve.wait_ge(kl_stored, b * (16 * KC) + (16 * q + 1))
                nc.vector.scalar_tensor_tensor(out=kl[:].rearrange("p (a c) -> p a c", a=2), in0=kps[:, c % 2, :, 0:HALF],
                                               scalar=bkc[:, q:q + 1], in1=kh[:].bitcast(F32).rearrange("p (a c) -> p a c", a=2),
                                               op0=ALU.add, op1=ALU.subtract).then_inc(k_split, 1)

            dve.sem_inc(scan_done, DBUF)
            dve.sem_inc(hc_done, UNITS + 1)
            dve.sem_inc(y1_done, 2)
            dve.sem_inc(y_done, 2)
            dve.sem_inc(k_split, 2)
            dve.wait_ge(consts, 96)
            with dve.Fori(0, G // 2) as gg:
                for pair in range(2):
                    for n in range(UNITS):
                        c, s, buf = n // 2, n % 2, n % HBUF
                        dve.wait_ge(decay_done, unit(gg, pair, n + 1 + UB_FREE))
                        nc.vector.memset(decay[:, s].rearrange("p n (b t) -> p (n b) t", b=GB)[:, :, 0:1],
                                         0.0).then_inc(edge_done, 1)
                        dve.wait_ge(edge_done, unit(gg, pair, n + 1))
                        dve.wait_ge(ub_done, unit(gg, pair, n + 1 + UB_FREE))
                        hv = h[:, buf].rearrange("p n t -> p (n t)")
                        nc.vector.tensor_tensor_scan(hv, decay[:, s].rearrange("p n t -> p (n t)"), hv, 0.0,
                                                     ALU.mult, ALU.add).then_inc(scan_done, 1)
                        dve.wait_ge(scan_done, unit(gg, pair, n + 1 + DBUF))
                        if n == 0:
                            dve.wait_ge(c_loaded[pair], gg * 16 + 16)
                        nc.vector.tensor_tensor(h[:, buf], h[:, buf], Cc[:, pair, s * HS:(s + 1) * HS],
                                                ALU.mult).then_inc(hc_done, 1)
                        if s == 0:
                            behind(dve, gg, pair, c - 1, outputs)
                        if s == 1:
                            low_keys(gg, pair, c)
            outputs(LAST, 0, -1)

        @block.tensor
        def _(pe):
            pe.sem_inc(sum_done, HBUF)
            pe.sem_inc(kv_free, 1)
            pe.wait_ge(consts, 96)
            with pe.Fori(0, G // 2) as gg:
                for pair in range(2):
                    for c in range(CC):
                        b, q = batch(gg, pair, c), c % 4
                        pe.wait_ge(ctx_loaded, b * 16 + 16)
                        pe.wait_ge(k_split, b * KC + (q + 1))
                        for a in range(2):
                            for k in range(CK):
                                ins = nc.tensor.matmul(kps[:, c % 2, a, 0:HALF], wk[:, k, q * P:(q + 1) * P],
                                                       cxT[:, k, a * HALF:(a + 1) * HALF], start=(k == 0), stop=(k == CK - 1))
                        ins.then_inc(k_mm, 1)
                        for i in V_TILES[q]:
                            pe.wait_ge(v_done, b * NC + max(i, 1))
                            for k in range(CK):
                                ins = nc.tensor.matmul(vps[0:CT, i % 2], cxT[:, k, i * CT:(i + 1) * CT], wv[:, k],
                                                       start=(k == 0), stop=(k == CK - 1))
                            ins.then_inc(v_mm, 1)
                        if q == 3:
                            pe.wait_ge(v_mm, b * NC + NC)
                            pe.sem_inc(kv_free, 1)
                        pe.wait_ge(y1_done, chunk(gg, pair, c + 1))
                        for s in range(2):
                            pe.wait_ge(hc_done, unit(gg, pair, 2 * c + s + 2 + UNITS))
                            for n in range(HS):
                                ins = nc.tensor.matmul(ps[:, c % 2, 0:GL], ident[:], h[:, (2 * c + s) % HBUF, n],
                                                       start=(s == 0 and n == 0), stop=(s == 1 and n == HS - 1))
                            ins.then_inc(sum_done, 1)

def attention(nc, x, kh_d, kl_d, v_d, y_d, W_out, Wq, bq, bv, Wo, bo, rW1, rb1, rW2, rb2, ident_in,
              x2_d, xn_d, logits_d):
    ctx = ExitStack()
    TURN_AT = (0, 2)
    HIDDEN_AT = tuple(range(4, 4 + 3 * RC, 3))
    PV_BANK = 7
    PARTS = ((0, kh_d), (1, kl_d), (2, kh_d))
    EVEN = HALF + 1
    ITEMS = 2 * HEADS
    with ctx:
        def sb(name, shape, dt=F32):
            return ctx.enter_context(nc.sbuf_tensor("t_" + name, shape, dt))

        def sem(name):
            return ctx.enter_context(nc.semaphore("t_" + name))

        ident = sb("ident", [P, P])
        wout, wq = sb("wout", [P, CC, DM]), sb("wq", [P, KC, DM])
        wo, rw1, rw2 = sb("wo", [P, KC, DM]), sb("rw1", [P, KC, RH]), sb("rw2", [P, RC, E])
        bqc, bvc, rb1c = sb("bqc", [P, KC]), sb("bvc", [P, KC]), sb("rb1c", [P, RC])
        bor, rb2r = sb("bor", [P, DM]), sb("rb2r", [P, E])
        warm = sb("warm", [1, 1])
        gT = sb("gT", [P, CC, L])
        xt = sb("xt", [TT, 2, DM])
        k3 = sb("k3", [3 * DK, 2, 4, CTX], F32R)
        v = sb("v", [CT, NC, DM])
        q3 = sb("q3", [3 * DK, HEADS, L], F32R)
        qf, qh, ql = sb("qf", [P, KC, L]), sb("qh", [P, L], F32R), sb("ql", [P, L], F32R)
        xr = [sb("x1", [TT, 2, DM]), sb("x2", [TT, 2, DM])]
        x1b = sb("x1b", [TT, 2, DM])
        xn = [sb("xn1", [TT, 2, DM]), sb("xn2", [TT, 2, DM])]
        xnT = [sb("xnT1", [P, KC, L]), sb("xnT2", [P, KC, L])]
        probs = sb("probs", [TT, 3, CTX])
        pT = sb("pT", [CT, 2, 4, NC, L])
        oT = sb("oT", [P, KC, L])
        rh = sb("rh", [P, RC, L])
        lg = sb("lg", [TT, B, 2, E])
        st, mv, rstd = sb("st", [TT, 4, 6]), sb("mv", [TT, 4, 2]), sb("rstd", [TT, 2, 2])
        nmax, rsum, rinv = sb("nmax", [TT, ITEMS]), sb("rsum", [TT, ITEMS]), sb("rinv", [TT, ITEMS])
        ps = ctx.enter_context(nc.psum_tensor("t_ps", [P, 8, 512], F32))

        S = {n: sem(n) for n in (
            "w_out w_q w_rest g_loaded x_loaded out_mm x1_done x2_done stat1 stat2 stat_seen mv1 mv2 var1 var2 "
            "std1 std2 rstd1 rstd2 xn1 xn2 xn1_mm xn2_mm xn1T xn2T "
            "q_mm q_full q_high q_low q_done q_moved score_mm max_done exp_done rinv_done norm_done turn_mm turn_done "
            "pv_mm o_done wo_mm x1b_done x2_stored xn_stored rh_mm rh_pre rh_done lg_mm lg_done lg_stored").split()}
        k_loaded = [sem(f"k_loaded{j}") for j in range(KC)]
        v_loaded = [sem(f"v_loaded{j}") for j in range(KC)]
        N_OUT, N_Q, N_REST = 2, 3, 6

        def item_scores(n):
            flat = ps[0:TT].rearrange("p b n -> p (b n)")
            return flat[:, 1024 * (n % 2):1024 * (n % 2) + 2 * 513].rearrange("p (a n) -> p a n", a=2)[:, :, 0:HALF]

        def start(eng, names):
            for name in names.split():
                eng.sem_inc(S[name], 1)

        def wait(eng, name, n):
            eng.wait_ge(S[name], n + 1)

        block = ctx.enter_context(nc.Block())

        @block.sync
        def _(sp):
            start(sp, "w_out w_q w_rest g_loaded x_loaded x2_stored xn_stored")

            def rows(w):
                return w.rearrange("(k p) n -> p k n", p=P)

            def loads(b, used):
                if used is not None:
                    wait(sp, "out_mm", used * 2)
                sp.dma_start(gT[:], y_d[:, :, bass.ds(b * L, L)].rearrange("c p t -> p c t")).then_inc(S["g_loaded"], 16)
                if used is not None:
                    wait(sp, "x1_done", used * 2)
                sp.dma_start(xt[:], x[bass.ds(b, 1)].rearrange("a (u p) d -> p (a u) d", p=TT)).then_inc(S["x_loaded"], 16)

            def load_heads(b, used, j):
                if used is not None or j >= 2:
                    wait(sp, "score_mm", (0 if used is None else used * ITEMS) + 8 * j - 8)
                for part, src in PARTS:
                    sp.dma_start(k3[part * DK:part * DK + DK, j % 2].bitcast(F32),
                                 src[bass.ds(b, 1), j].rearrange("a (r p) t -> p (a r) t", p=DK)).then_inc(k_loaded[j], 16)
                if used is not None:
                    wait(sp, "pv_mm", used * KC - (KC - j - 1))
                sp.dma_start(v[:, :, j * P:(j + 1) * P],
                             v_d[bass.ds(b, 1), :, :, j * P:(j + 1) * P].rearrange("a i p d -> p (a i) d")).then_inc(v_loaded[j], 16)

            def store(done, n, dst, src, stored):
                def of(b):
                    wait(sp, done, b * n + n)
                    sp.dma_start(dst[bass.ds(b, 1)].rearrange("a p u d -> p (a u) d"), src[:]).then_inc(S[stored], 16)
                return of

            store_x2 = store("x2_done", 2, x2_d, xr[1], "x2_stored")
            store_xn = store("xn2", 2, xn_d, xn[1], "xn_stored")

            sp.dma_start(ident[:], ident_in).then_inc(S["w_out"], 16)
            loads(0, None)
            sp.dma_start(wout[:], rows(W_out)).then_inc(S["w_out"], 16)
            for dst, src in ((bqc[:], bq), (bvc[:], bv), (wq[:], rows(Wq))):
                sp.dma_start(dst, src).then_inc(S["w_q"], 16)
            for j in range(2):
                load_heads(0, None, j)
            for dst, src in ((bor[:], bo.partition_broadcast(P)), (wo[:], rows(Wo)), (rb1c[:], rb1), (rw1[:], rows(rW1)),
                             (rw2[:], rows(rW2)), (rb2r[:], rb2.partition_broadcast(P))):
                sp.dma_start(dst, src).then_inc(S["w_rest"], 16)
            loads(1, 1)
            for j in range(2, KC):
                load_heads(0, None, j)

            def batch(b, last):
                for j in range(2):
                    load_heads(b, b, j)
                store_x2(b - 1)
                store_xn(b - 1)
                if not last:
                    loads(b + 1, b + 1)
                for j in range(2, KC):
                    load_heads(b, b, j)

            with sp.Fori(1, B - 1) as b:
                batch(b, False)
            batch(B - 1, True)
            store_x2(B - 1)
            store_xn(B - 1)
            wait(sp, "lg_done", 2 * B)
            sp.dma_start(logits_d.rearrange("b p u e -> p b u e"), lg[:]).then_inc(S["lg_stored"], 16)
            sp.wait_ge(S["lg_stored"], 16)
            for stored in ("x2_stored", "xn_stored"):
                wait(sp, stored, 16 * B)

        @block.gpsimd
        def _(pool):
            start(pool, "x1b_done")
            wait(pool, "w_rest", 16 * N_REST)
            with pool.Fori(0, B) as b:
                for u in range(2):
                    wait(pool, "x1_done", b * 2 + u + 1)
                    wait(pool, "x2_done", b * 2)
                    nc.gpsimd.tensor_tensor(x1b[:, u], xr[0][:, u], bor[0:TT], ALU.add).then_inc(S["x1b_done"], 1)

        @block.vector
        def _(dve):
            start(dve, "x1_done x2_done stat1 stat2 stat_seen mv1 mv2 var1 var2 rstd1 rstd2 xn1 xn2 q_full q_high q_low q_done "
                       "max_done rinv_done norm_done o_done rh_pre lg_done")

            def norm(b, w):
                nth = str(w + 1)
                for u in range(2):
                    wait(dve, "x" + nth + "_done", b * 2 + u + 1)
                    nc.vector.bn_stats(st[:, 2 * w + u], xr[w][:, u]).then_inc(S["stat" + nth], 1)
                wait(dve, "stat" + nth, b * 2 + 2)
                dve.sem_inc(S["stat_seen"])
                for u in range(2):
                    nc.vector.bn_aggr(mv[:, 2 * w + u], st[:, 2 * w + u]).then_inc(S["mv" + nth], 1)
                wait(dve, "mv" + nth, b * 2 + 2)
                r = rstd[:, w]
                nc.vector.tensor_scalar(r, mv[:, 2 * w:2 * w + 2, 1], EPS, None, ALU.add).then_inc(S["var" + nth], 1)
                wait(dve, "std" + nth, b + 1)
                nc.vector.reciprocal(r, r).then_inc(S["rstd" + nth], 1)
                wait(dve, "rstd" + nth, b + 1)
                wait(dve, "xn" + nth + "_mm", b * 2)
                if w == 1:
                    wait(dve, "xn_stored", b * 16)
                for u in range(2):
                    nc.vector.tensor_scalar(xn[w][:, u], xr[w][:, u], mv[:, 2 * w + u, 0:1], rstd[:, w, u:u + 1],
                                            ALU.subtract, ALU.mult).then_inc(S["xn" + nth], 1)

            def queries(b, j, steps):
                for step in steps:
                    if step == 0:
                        wait(dve, "q_full", b * KC + j + 1)
                        wait(dve, "q_done", b * KC + j)
                        nc.vector.tensor_copy(qh[:], qf[:, j]).then_inc(S["q_high"], 1)
                    elif step == 1:
                        wait(dve, "q_high", b * KC + j + 1)
                        wait(dve, "q_moved", b * KC + j)
                        nc.vector.tensor_tensor(ql[:], qf[:, j], qh[:].bitcast(F32), ALU.subtract).then_inc(S["q_low"], 1)
                    else:
                        for h in range(2 * step - 4, 2 * step - 2):
                            for part in range(2):
                                ins = nc.vector.tensor_copy(q3[part * DK:part * DK + DK, 4 * j + h],
                                                            qh[DK * h:DK * h + DK].bitcast(F32))
                        if step == 3:
                            ins.then_inc(S["q_done"], 1)

            def negative_max(b, n):
                wait(dve, "score_mm", b * ITEMS + n + 1)
                nc.vector.tensor_reduce(nmax[:, n:n + 1], item_scores(n), AX.XY, ALU.max,
                                        negate=True).then_inc(S["max_done"], 1)

            def normalise(b, n):
                wait(dve, "exp_done", b * ITEMS + n + 1)
                nc.vector.reciprocal(rinv[:, n:n + 1], rsum[:, n:n + 1]).then_inc(S["rinv_done"], 1)
                wait(dve, "rinv_done", b * ITEMS + n + 1)
                nc.vector.tensor_scalar(probs[:, n % 3], probs[:, n % 3], rinv[:, n:n + 1], None,
                                        ALU.mult).then_inc(S["norm_done"], 1)

            def outputs(b, j):
                wait(dve, "pv_mm", b * KC + j + 1)
                nc.vector.tensor_scalar(oT[:, j], ps[:, PV_BANK, 0:L], bvc[:, j:j + 1], None, ALU.add).then_inc(S["o_done"], 1)

            def logits(b):
                wait(dve, "lg_mm", b * 2 + 2)
                for u in range(2):
                    nc.vector.tensor_tensor(lg[:, bass.ds(b, 1), u].rearrange("p a e -> p (a e)") if not isinstance(b, int) else lg[:, b, u],
                                            ps[0:TT, PV_BANK, u * E:(u + 1) * E], rb2r[0:TT], ALU.add).then_inc(S["lg_done"], 1)

            def hidden(b, c, bank):
                if c == 0:
                    wait(dve, "lg_mm", b * 2)
                wait(dve, "rh_mm", b * RC + c + 1)
                nc.vector.tensor_scalar(rh[:, c], ps[:, bank, 0:L], rb1c[:, c:c + 1], None, ALU.add).then_inc(S["rh_pre"], 1)

            def projected(b):
                wait(dve, "x_loaded", b * 16 + 16)
                wait(dve, "xn1", b * 2)
                wait(dve, "x1b_done", b * 2)
                for u in range(2):
                    wait(dve, "out_mm", b * 2 + u + 1)
                    nc.vector.tensor_tensor(xr[0][:, u], ps[0:TT, u], xt[:, u], ALU.add).then_inc(S["x1_done"], 1)

            def opening(b):
                for j in range(KC):
                    wait(dve, "q_mm", b * KC + j + 1)
                    wait(dve, "q_low", b * KC)
                    nc.vector.tensor_scalar(qf[:, j], ps[:, 4 + j % 2, 0:L], bqc[:, j:j + 1], float(DK) ** -0.5,
                                            ALU.add, ALU.mult).then_inc(S["q_full"], 1)
                queries(b, 0, range(4))
                negative_max(b, 0)

            def batch(b, first=False, second=False, last=False):
                for n in range(ITEMS):
                    if n + 1 < ITEMS:
                        negative_max(b, n + 1)
                    normalise(b, n)
                    if n % 8 < 4 and n < ITEMS - 8:
                        queries(b, n // 8 + 1, [n % 8])
                    if n >= 8 and n % 8 == 4:
                        outputs(b, n // 8 - 1)
                    if not first and not second and n == 1:
                        logits(b - 2)
                    if not first and n - 2 in HIDDEN_AT:
                        hidden(b - 1, HIDDEN_AT.index(n - 2), 6)
                if not last:
                    projected(b + 1)
                outputs(b, KC - 1)
                if not last:
                    norm(b + 1, 0)
                wait(dve, "x2_stored", b * 16)
                for u in range(2):
                    wait(dve, "wo_mm", b * 2 + u + 1)
                    wait(dve, "x1b_done", b * 2 + u + 1)
                    nc.vector.tensor_tensor(xr[1][:, u], ps[0:TT, 4 + u], x1b[:, u], ALU.add).then_inc(S["x2_done"], 1)
                norm(b, 1)
                if not last:
                    opening(b + 1)

            wait(dve, "w_q", 16 * N_Q)
            projected(0)
            norm(0, 0)
            opening(0)
            batch(0, first=True)
            wait(dve, "w_rest", 16 * N_REST)
            batch(1, second=True)
            with dve.Fori(2, B - 1) as b:
                batch(b)
            batch(B - 1, last=True)
            logits(B - 2)
            for c in range(RC):
                hidden(B - 1, c, c % 4)
            logits(B - 1)

        @block.scalar
        def _(act):
            start(act, "q_moved std1 std2 xn1T xn2T exp_done turn_done rh_done")

            def deviation(b, w):
                wait(act, f"var{w + 1}", b + 1)
                nc.scalar.activation(rstd[:, w], rstd[:, w], ACT.Sqrt).then_inc(S[f"std{w + 1}"], 1)

            def turned_norm(b, w, u, bank):
                wait(act, f"xn{w + 1}_mm", b * 2 + u + 1)
                nc.scalar.activation(xnT[w][:, :, u * TT:(u + 1) * TT],
                                     ps[:, bank, 0:KC * TT].rearrange("p (k t) -> p k t", k=KC),
                                     ACT.Copy).then_inc(S[f"xn{w + 1}T"], 1)

            def gelu(b):
                wait(act, "rh_pre", b * RC + RC)
                nc.scalar.activation(rh[:], rh[:], ACT.Gelu).then_inc(S["rh_done"], 1)

            def low_queries(b, j, steps):
                for step in steps:
                    if step == 0:
                        wait(act, "q_low", b * KC + j + 1)
                    for h in range(2 * step, 2 * step + 2):
                        ins = nc.scalar.activation(q3[2 * DK:3 * DK, 4 * j + h], ql[DK * h:DK * h + DK].bitcast(F32), ACT.Copy)
                    if step == 1:
                        ins.then_inc(S["q_moved"], 1)

            def exponentials(b, n):
                wait(act, "max_done", b * ITEMS + n + 1)
                wait(act, "turn_mm", b * ITEMS + max(n - 2, 0))
                nc.scalar.activation(probs[:, n % 3].rearrange("p (a c) -> p a c", a=2),
                                     item_scores(n), ACT.Exp, bias=nmax[:, n:n + 1],
                                     accum_out=rsum[:, n:n + 1]).then_inc(S["exp_done"], 1)

            def turned_probs(b, n):
                h, u = n // 2, n % 2
                j = h // 4
                wait(act, "turn_mm", b * ITEMS + n + 1)
                wait(act, "pv_mm", b * KC + max(j - 1, 0))
                nc.scalar.activation(pT[:, j % 2, h % 4, :, u * TT:(u + 1) * TT].rearrange("p (a i) t -> p a i t", a=2),
                                     ps[0:CT, 4:6, 0:3 * TT].rearrange("p a (i t) -> p a i t", i=3),
                                     ACT.Copy).then_inc(S["turn_done"], 1)

            def projected(b):
                deviation(b, 0)
                for u in range(2):
                    turned_norm(b, 0, u, 6 + u)

            def opening(b):
                nc.scalar.activation(warm[:], ident[0:1, 0:1], ACT.Exp)
                low_queries(b, 0, range(2))
                exponentials(b, 0)

            def batch(b, first=False, second=False, last=False):
                for n in range(ITEMS):
                    if n + 1 < ITEMS:
                        exponentials(b, n + 1)
                    if n >= 1:
                        turned_probs(b, n - 1)
                    if n % 8 in (2, 3) and n < ITEMS - 8:
                        low_queries(b, n // 8 + 1, [n % 8 - 2])
                    if not first and n in TURN_AT:
                        turned_norm(b - 1, 1, TURN_AT.index(n), 6)
                turned_probs(b, ITEMS - 1)
                if not last:
                    projected(b + 1)
                deviation(b, 1)
                if not first:
                    gelu(b - 1)
                if not last:
                    opening(b + 1)

            projected(0)
            wait(act, "w_out", 16 * N_OUT)
            opening(0)
            batch(0, first=True)
            wait(act, "w_rest", 16 * N_REST)
            batch(1, second=True)
            with act.Fori(2, B - 1) as b:
                batch(b)
            batch(B - 1, last=True)
            for u in range(2):
                turned_norm(B - 1, 1, u, 6 + u)
            gelu(B - 1)

        @block.tensor
        def _(pe):
            start(pe, "out_mm xn1_mm xn2_mm q_mm score_mm turn_mm pv_mm wo_mm rh_mm lg_mm")

            def turn_norm(b, w, u, bank):
                wait(pe, f"xn{w + 1}", b * 2 + u + 1)
                for k in range(KC):
                    ins = nc.tensor.transpose(ps[:, bank, k * TT:(k + 1) * TT], xn[w][:, u, k * P:(k + 1) * P],
                                              ident[0:TT, 0:TT])
                ins.then_inc(S[f"xn{w + 1}_mm"], 1)

            def hidden(b, c, bank, halves, alone=False):
                for half in halves:
                    if half == 0:
                        if c == 0:
                            wait(pe, "xn2T", b * 2 + 2)
                        wait(pe, "rh_pre", b * RC + (max(c - 3, 0) if alone else c))
                    for k in range(2 * half, 2 * half + 2):
                        ins = nc.tensor.matmul(ps[:, bank, 0:L], rw1[:, k, c * P:(c + 1) * P], xnT[1][:, k],
                                               start=(k == 0), stop=(k == KC - 1))
                    if half == 1:
                        ins.then_inc(S["rh_mm"], 1)

            def logits(b, u):
                wait(pe, "rh_done", b + 1)
                for c in range(RC):
                    ins = nc.tensor.matmul(ps[0:TT, PV_BANK, u * E:(u + 1) * E], rh[:, c, u * TT:(u + 1) * TT], rw2[:, c],
                                           start=(c == 0), stop=(c == RC - 1))
                ins.then_inc(S["lg_mm"], 1)

            def scores(b, n):
                h, u = n // 2, n % 2
                if n % 8 == 0:
                    pe.wait_ge(k_loaded[h // 4], b * 48 + 48)
                    wait(pe, "q_done", b * KC + h // 4 + 1)
                    wait(pe, "q_moved", b * KC + h // 4 + 1)
                wait(pe, "exp_done", b * ITEMS + max(n - 1, 0))
                for a in range(2):
                    ins = nc.tensor.matmul(ps[0:TT, 2 * (n % 2) + a, 0:EVEN], q3[:, h, u * TT:(u + 1) * TT],
                                           k3[:, h // 4 % 2, h % 4, a * (CTX - EVEN):a * (CTX - EVEN) + EVEN], start=True, stop=True)
                ins.then_inc(S["score_mm"], 1)

            def turn_probs(b, n):
                wait(pe, "norm_done", b * ITEMS + n + 1)
                wait(pe, "turn_done", b * ITEMS + n)
                for i in range(NC):
                    ins = nc.tensor.transpose(ps[0:CT, 4 + i // 3, (i % 3) * TT:(i % 3 + 1) * TT],
                                              probs[:, n % 3, i * CT:(i + 1) * CT], ident[0:TT, 0:TT])
                ins.then_inc(S["turn_mm"], 1)

            def values(b, j):
                pe.wait_ge(v_loaded[j], b * 16 + 16)
                wait(pe, "turn_done", b * ITEMS + 8 * j + 8)
                wait(pe, "o_done", b * KC + j)
                for i in range(NC):
                    for r in range(4):
                        h = 4 * j + r
                        ins = nc.tensor.matmul(ps[DK * r:DK * r + DK, PV_BANK, 0:L], v[:, i, h * DK:(h + 1) * DK],
                                               pT[:, j % 2, r, i], start=(i == 0), stop=(i == NC - 1),
                                               tile_position=(0, DK * r))
                ins.then_inc(S["pv_mm"], 1)

            def project(b, u, first):
                if u == 0:
                    wait(pe, "g_loaded", b * 16 + 16)
                    if not first:
                        wait(pe, "exp_done", b * ITEMS - 1)
                for c in range(CC):
                    ins = nc.tensor.matmul(ps[0:TT, u], gT[:, c, u * TT:(u + 1) * TT], wout[:, c],
                                           start=(c == 0), stop=(c == CC - 1))
                ins.then_inc(S["out_mm"], 1)

            def opening(b, finished=None):
                for u in range(2):
                    turn_norm(b, 0, u, 6 + u)
                wait(pe, "xn1T", b * 2 + 2)
                wait(pe, "x2_done", b * 2)
                for j in range(KC):
                    if j >= 2:
                        wait(pe, "q_full", b * KC + j - 1)
                    for k in range(KC):
                        ins = nc.tensor.matmul(ps[:, 4 + j % 2, 0:L], wq[:, k, j * P:(j + 1) * P], xnT[0][:, k],
                                               start=(k == 0), stop=(k == KC - 1))
                    ins.then_inc(S["q_mm"], 1)
                if finished is not None:
                    logits(finished, 0)
                wait(pe, "q_full", b * KC + KC)
                wait(pe, "x1_done", b * 2 + 2)
                scores(b, 0)
                scores(b, 1)
                if finished is not None:
                    logits(finished, 1)

            def batch(b, first=False, second=False, last=False):
                for n in range(ITEMS):
                    if n + 2 < ITEMS:
                        scores(b, n + 2)
                    if not first and n in TURN_AT:
                        u = TURN_AT.index(n)
                        if u == 1:
                            wait(pe, "xn2T", b * 2 - 1)
                        turn_norm(b - 1, 1, u, 6)
                    for half in range(2):
                        if not first and n - half in HIDDEN_AT:
                            hidden(b - 1, HIDDEN_AT.index(n - half), 6, [half])
                    if n >= 1:
                        turn_probs(b, n - 1)
                    if n >= 8 and n % 8 == 2:
                        if n // 8 == 1 and not first and not second:
                            wait(pe, "lg_done", b * 2 - 2)
                        values(b, n // 8 - 1)
                if not last:
                    project(b + 1, 0, False)
                turn_probs(b, ITEMS - 1)
                if not last:
                    project(b + 1, 1, False)
                values(b, KC - 1)
                if first:
                    wait(pe, "w_rest", 16 * N_REST)
                wait(pe, "o_done", b * KC + KC)
                for u in range(2):
                    for j in range(KC):
                        ins = nc.tensor.matmul(ps[0:TT, 4 + u], oT[:, j, u * TT:(u + 1) * TT], wo[:, j],
                                               start=(j == 0), stop=(j == KC - 1))
                    ins.then_inc(S["wo_mm"], 1)
                if not last:
                    opening(b + 1, None if first else b - 1)

            wait(pe, "w_out", 16 * N_OUT)
            for u in range(2):
                project(0, u, True)
            wait(pe, "w_q", 16 * N_Q)
            opening(0)
            batch(0, first=True)
            batch(1, second=True)
            with pe.Fori(2, B - 1) as b:
                batch(b)
            batch(B - 1, last=True)
            wait(pe, "o_done", B * KC)
            for u in range(2):
                logits(B - 2, u)
            for u in range(2):
                if u == 1:
                    wait(pe, "lg_done", 2 * B - 2)
                turn_norm(B - 1, 1, u, 6 + u)
            for c in range(RC):
                hidden(B - 1, c, c % 4, range(2), alone=True)
            for u in range(2):
                if u == 0:
                    wait(pe, "xn2T", 2 * B)
                logits(B - 1, u)


def experts(nc, We1, be1, We2, be2, upper_in, ident_in, tile_starts_in, x2_d, xn_d, logits_d, xs_d, out):
    ctx = ExitStack()
    PAIRS = [(a, b) for a in range(E) for b in range(a + 1, E)]
    WG = 4
    CW = HC // WG
    GW = CW * P
    RING = 4
    AHEAD = 2
    HALVES = GT // P
    with ctx:
        def sb(name, shape, dt=F32):
            return ctx.enter_context(nc.sbuf_tensor("e_" + name, shape, dt))

        def sem(name):
            return ctx.enter_context(nc.semaphore("e_" + name))

        w1h, w1l = (sb(n, [P, WG, KC, GW], F32R) for n in ("w1h", "w1l"))
        w2h, w2l = (sb(n, [P, WG, CW, DM], F32R) for n in ("w2h", "w2l"))
        stage = sb("stage", [P, 4, 4, 512])
        b1, b2 = sb("b1", [P, E * HC]), sb("b2", [P, E, DM])
        ident, upper, ones = sb("ident", [P, P]), sb("upper", [TT, TT]), sb("ones", [TT, TT])
        one = sb("one", [P, 1])
        starts = sb("starts", [1, EG])
        lg, p, m, pm = (sb(n, [TT, NT, E]) for n in ("lg", "p", "m", "pm"))
        mx, total = sb("mx", [TT, NT]), sb("total", [TT, NT])
        ge = sb("ge", [TT, len(PAIRS), NT])
        r = sb("r", [TT, 2, NT])
        incl, slot, tmp, eq = (sb(n, [TT, NT, E]) for n in ("incl", "slot", "tmp", "eq"))
        choice = sb("choice", [TT, 2, NT])
        gate = sb("gate", [TT, 2, NT])
        index = sb("index", [TT, 2, NT], I32)
        taken = sb("taken", [1, E, EG])
        count = sb("count", [1, E])
        tiles = sb("tiles", [1, 2, E + 1])
        tiles_i = sb("tiles_i", [1, 2, E + 1], I32)
        xt = sb("xt", [P, HALVES, DM])
        xTh, xTl = sb("xTh", [P, KC, GT], F32R), sb("xTl", [P, KC, GT], F32R)
        h = sb("h", [P, RING, GT])
        hh, hl = sb("hh", [P, RING, GT], F32R), sb("hl", [P, RING, GT], F32R)
        y = sb("y", [P, HALVES, DM])
        ps = ctx.enter_context(nc.psum_tensor("e_ps", [P, 8, 512], F32))
        H_BANK, Y_BANK, X_BANK = 0, 4, 6

        xn = [part[0:TT, g].bitcast(F32) for part, g in ((w1l, 2), (w1l, 3), (w2l, 2), (w2l, 3))]
        back = [w1h[0:TT].bitcast(F32), w1l[0:TT].bitcast(F32)]

        S = {n: sem(n) for n in (
            "consts lg_loaded step ones_set exped n_loaded rank_mm slots_done tiles_done n_scattered "
            "w_high w_split_first w_split waited x_loaded x_mm x_high x_split h_mm h_done h_high h_split l2_mm y_done y_stored "
            "x2_loaded combined out_stored").split()}
        w_first = [sem(f"w_first{i}") for i in range(4)]
        w_loaded = [sem(f"w_loaded{i}") for i in range(4)]
        r_gathered = [sem(f"r_gathered{i}") for i in range(4)]
        FIRST = {n: 1 + HC for n in ("h_mm", "h_done", "h_high", "h_split", "l2_mm")}

        def start(eng, names):
            for name in names.split():
                eng.sem_inc(S[name], FIRST.get(name, 1))

        def wait(eng, name, n):
            eng.wait_ge(S[name], n + FIRST.get(name, 1))

        block = ctx.enter_context(nc.Block())
        N_CONST = 3
        xs_v = xs_d.rearrange("(i h p) d -> i p h d", h=HALVES, p=P)
        out_v = out.rearrange("b (u p) d -> (b u) p d", p=TT)
        xn_v = xn_d.rearrange("(g b) p u d -> g p b u d", g=4)
        x2_v = x2_d.rearrange("(g b) p u d -> g p b u d", g=4)

        def weights(eng, n):
            e, g, second = n // (2 * WG), n % (2 * WG) // 2, n % 2
            src = We2[e].rearrange("(g c p) n -> g p c n", p=P, g=WG)[g] if second else \
                We1[e].rearrange("(k p) n -> p k n", p=P)[:, :, g * GW:(g + 1) * GW]
            eng.dma_start(stage[:, n % 4], src).then_inc(w_first[n % 4] if n < 8 else w_loaded[n % 4], 16)

        def wait_weights(eng, n):
            if n < 8:
                eng.wait_ge(w_first[n % 4], 16 * (n // 4 + 1))
            else:
                eng.wait_ge(w_loaded[n % 4], 16 * (n // 4 - 1))

        def wait_split(eng, n):
            if n < 4:
                eng.wait_ge(S["w_split_first"], n + 1)
            else:
                eng.wait_ge(S["w_split"], n + 1)

        def parts(n):
            g = n % (2 * WG) // 2
            return (w2h[:, g], w2l[:, g]) if n % 2 else (w1h[:, g], w1l[:, g])

        STEPS_TO_MASK = 5 + len(PAIRS) + E * (len(PAIRS) * 2 // E + 1)

        def counts(eng, e):
            return [eng.value_load(tiles_i[0:1, j, e:e + 1], min_val=0, max_val=E * EG) for j in range(2)]

        def expert_tiles(eng, e, first, body):
            taken_e, before = counts(eng, e)
            first(before + e)
            with eng.Fori(0, EG) as i:
                with eng.If(i < taken_e):
                    body(i, before + i, before + e + i)

        @block.sync
        def _(sp):
            start(sp, "lg_loaded consts x_loaded")

            sp.dma_start(lg[:].rearrange("p (b u) e -> p b u e", u=2), logits_d.rearrange("b p u e -> p b u e")).then_inc(S["lg_loaded"], 16)
            for dst, src in ((upper[:], upper_in), (starts[:], tile_starts_in)):
                sp.dma_start(dst, src).then_inc(S["lg_loaded"], 16)
            for dst, src in ((ident[:], ident_in), (b1[:], be1)):
                sp.dma_start(dst, src).then_inc(S["consts"], 16)
            for g in range(4):
                sp.dma_start(xn[g].rearrange("p (b u) d -> p b u d", u=2), xn_v[g]).then_inc(S["n_loaded"], 16)
            for n in range(4):
                weights(sp, n)
            for n in range(4, 8):
                sp.wait_ge(S["w_split_first"], n - 3)
                weights(sp, n)
            sp.dma_start(b2[:], be2.partition_broadcast(P)).then_inc(S["consts"], 16)
            wait(sp, "tiles_done", 1)
            sp.wait_ge(S["n_scattered"], 32 * NT)
            for e in range(E):
                def load(row, t):
                    wait(sp, "x_mm", t)
                    sp.dma_start(xt[:], xs_v[bass.ds(row, 1)].rearrange("a p h d -> (a p) h d")).then_inc(S["x_loaded"], 16)

                expert_tiles(sp, e, lambda t: load(e * EG, t), lambda i, n, t: load(i + (e * EG + 1), t + 1))
            sp.wait_ge(S["w_split"], 2 * WG * E)
            for g in range(4):
                sp.dma_start(stage[0:TT, g].rearrange("p (b u) d -> p b u d", u=2), x2_v[g]).then_inc(S["x2_loaded"], 16)
            for i in range(0, NT, 2):
                wait(sp, "combined", 2 * i + 2)
                sp.dma_start(out_v[i], stage[0:TT, i // 4, i % 4]).then_inc(S["out_stored"], 16)
            sp.wait_ge(S["out_stored"], 16 * NT)

        @block.gpsimd
        def _(pool):
            start(pool, "ones_set waited")
            pool.sem_inc(S["w_split"], 4)

            nc.gpsimd.memset(ones[:], 1.0).then_inc(S["ones_set"], 1)
            nc.gpsimd.memset(one[:], 1.0).then_inc(S["ones_set"], 1)
            wait(pool, "ones_set", 2)

            def split(n):
                high, low = parts(n)
                wait_weights(pool, n)
                raw = stage[:, n % 4]
                if n >= 2 * WG:
                    nc.gpsimd.tensor_tensor(high, raw, one[:].unsqueeze(2).to_broadcast([P, 4, 512]), ALU.mult).then_inc(S["w_high"], 1)
                pool.wait_ge(S["w_high"], n + 1)
                nc.gpsimd.tensor_tensor(low, raw, high.bitcast(F32), ALU.subtract).then_inc(S["w_split"], 1)
                if n + 4 < 2 * WG * E:
                    pool.wait_ge(S["w_split"], n + 1)
                    weights(pool, n + 4)

            wait(pool, "slots_done", 2)
            pool.wait_ge(S["n_loaded"], 16 * 4)
            for i in range(NT):
                for k in range(2):
                    pool.indirect_dma_start(
                        out=xs_d, out_offset=bass.IndirectOffsetOnAxis(ap=index[:, k, i:i + 1], axis=0),
                        in_=xn[i // 4][:, i % 4], in_offset=None).then_inc(S["n_scattered"], 16)
            pool.wait_ge(S["n_scattered"], 32 * NT)
            for n in range(4, 2 * WG):
                split(n)
            wait(pool, "tiles_done", 1)
            for e in range(1, E):
                before = counts(pool, e)[1]
                for n in range(2 * WG * e, 2 * WG * (e + 1)):
                    g = n % (2 * WG) // 2
                    wait(pool, "l2_mm" if n % 2 else "h_mm", before * HC + (g + 1) * CW - HC)
                    pool.sem_inc(S["waited"])
                    split(n)

            last = counts(pool, E)[1]
            wait(pool, "y_stored", last * 16)
            pool.sem_inc(S["waited"])
            for i in range(NT):
                for k in range(2):
                    pool.indirect_dma_start(
                        out=back[k][:, i // 4, i % 4], out_offset=None, in_=xs_d,
                        in_offset=bass.IndirectOffsetOnAxis(ap=index[:, k, i:i + 1], axis=0)).then_inc(r_gathered[i // 4], 16)

        @block.vector
        def _(dve):
            start(dve, "step slots_done tiles_done x_split h_high h_split y_done combined")

            step = [0]

            def then(ins):
                step[0] += 1
                ins.then_inc(S["step"], 1)
                wait(dve, "step", step[0])

            def over_e(a):
                return a.unsqueeze(2).to_broadcast([TT, NT, E])

            v = nc.vector
            wait(dve, "lg_loaded", 48)
            then(v.tensor_reduce(mx[:], lg[:], AX.X, ALU.max))
            then(v.tensor_tensor(p[:], lg[:], over_e(mx[:]), ALU.subtract))
            wait(dve, "exped", 1)
            then(v.tensor_reduce(total[:], p[:], AX.X, ALU.add))
            then(v.reciprocal(total[:], total[:]))
            then(v.tensor_tensor(p[:], p[:], over_e(total[:]), ALU.mult))
            for n, (a, b) in enumerate(PAIRS):
                then(v.tensor_tensor(ge[:, n], p[:, :, a], p[:, :, b], ALU.is_ge))
            for e in range(E):
                lower = [n for n, (a, b) in enumerate(PAIRS) if b == e]
                higher = [n for n, (a, b) in enumerate(PAIRS) if a == e]
                terms = [(n, 1.0) for n in lower] + [(n, -1.0) for n in higher]
                then(v.tensor_scalar(r[:, 0], ge[:, terms[0][0]], terms[0][1], float(len(higher)), ALU.mult, ALU.add))
                for n, sign in terms[1:]:
                    then(v.scalar_tensor_tensor(out=r[:, 0], in0=ge[:, n], scalar=sign, in1=r[:, 0], op0=ALU.mult, op1=ALU.add))
                then(v.tensor_scalar(m[:, :, e], r[:, 0], 1.5, None, ALU.is_lt))
            then(v.tensor_tensor(pm[:], p[:], m[:], ALU.mult))
            wait(dve, "rank_mm", 1)
            for e in range(E):
                then(v.tensor_tensor_scan(incl[:, :, e], ones[:, 0:NT], ps[0:TT, 1, 0:NT * E].rearrange("p (i e) -> p i e", e=E)[:, :, e],
                                          0.0, ALU.mult, ALU.add))
            then(v.tensor_tensor(slot[:], incl[:], ps[0:TT, 1, 0:NT * E].rearrange("p (i e) -> p i e", e=E), ALU.subtract))
            then(v.tensor_tensor(slot[:], slot[:], ps[0:TT, 0, 0:NT * E].rearrange("p (i e) -> p i e", e=E), ALU.add))
            for e in range(E):
                then(v.tensor_scalar(slot[:, :, e], slot[:, :, e], float(e * SLOTS), None, ALU.add))
            FAR = float(E * SLOTS)
            then(v.tensor_scalar(tmp[:], slot[:], FAR, None, ALU.subtract))
            then(v.tensor_tensor(tmp[:], tmp[:], m[:], ALU.mult))
            then(v.tensor_reduce(choice[:, 0], tmp[:], AX.X, ALU.min))
            then(v.tensor_scalar(choice[:, 0], choice[:, 0], FAR, None, ALU.add))
            then(v.tensor_tensor(tmp[:], slot[:], m[:], ALU.mult))
            then(v.tensor_reduce(choice[:, 1], tmp[:], AX.X, ALU.max))
            for k in range(2):
                v.tensor_copy(index[:, k], choice[:, k]).then_inc(S["slots_done"], 1)
            for e in range(E):
                then(v.tensor_scalar(taken[:, e], starts[:], incl[0:1, NT - 1, e:e + 1], None, ALU.is_lt))
            then(v.tensor_reduce(count[:], taken[:], AX.X, ALU.add))
            then(v.memset(tiles[:], 0.0))
            then(v.tensor_copy(tiles[:, 0, 0:E], count[:]))
            for e in range(E):
                then(v.tensor_tensor(tiles[:, 1, e + 1:e + 2], tiles[:, 1, e:e + 1], count[:, e:e + 1], ALU.add))
            v.tensor_copy(tiles_i[:], tiles[:]).then_inc(S["tiles_done"], 1)
            for n in range(4):
                high, low = parts(n)
                wait_weights(dve, n)
                dve.wait_ge(S["w_high"], n + 1)
                v.tensor_tensor(low, stage[:, n % 4], high.bitcast(F32), ALU.subtract).then_inc(S["w_split_first"], 1)
            for k in range(2):
                then(v.tensor_tensor(eq[:], slot[:], over_e(choice[:, k]), ALU.is_equal))
                then(v.tensor_tensor(eq[:], eq[:], pm[:], ALU.mult))
                then(v.tensor_reduce(gate[:, k], eq[:], AX.X, ALU.add))
            wait(dve, "consts", 16 * N_CONST)
            wait(dve, "tiles_done", 1)
            for e in range(E):
                def tokens(t):
                    for b in range(2):
                        wait(dve, "x_high", 2 * t + b + 1)
                        both = slice(2 * b, 2 * b + 2)
                        v.tensor_tensor(xTl[:, both].rearrange("p k t -> p (k t)"), ps[:, X_BANK + b],
                                        xTh[:, both].rearrange("p k t -> p (k t)").bitcast(F32), ALU.subtract).then_inc(S["x_split"], 1)

                def results(i, n, t):
                    for c in range(HC):
                        k = c % RING
                        wait(dve, "h_done", n * HC + c + 1)
                        wait(dve, "l2_mm", n * HC + c - RING + 1)
                        v.tensor_copy(hh[:, k], h[:, k]).then_inc(S["h_high"], 1)
                        wait(dve, "h_high", n * HC + c + 1)
                        v.tensor_tensor(hl[:, k], h[:, k], hh[:, k].bitcast(F32), ALU.subtract).then_inc(S["h_split"], 1)
                    tokens(t + 1)
                    wait(dve, "l2_mm", n * HC + HC)
                    wait(dve, "y_stored", n * 16)
                    for s in range(HALVES):
                        v.tensor_tensor(y[:, s], ps[:, Y_BANK + s], b2[:, e], ALU.add).then_inc(S["y_done"], 1)

                expert_tiles(dve, e, tokens, results)
            dve.wait_ge(S["x2_loaded"], 16 * 4)
            for i in range(NT):
                x2 = stage[0:TT, i // 4, i % 4]
                dve.wait_ge(r_gathered[i // 4], 16 * 2 * 4)
                for k in range(2):
                    v.scalar_tensor_tensor(out=x2, in0=back[k][:, i // 4, i % 4], scalar=gate[:, k, i:i + 1],
                                           in1=x2, op0=ALU.mult, op1=ALU.add).then_inc(S["combined"], 1)
                    if k == 0:
                        wait(dve, "combined", 2 * i + 1)

        @block.scalar
        def _(act):
            start(act, "exped x_high h_done y_stored")

            wait(act, "step", 2)
            nc.scalar.activation(p[:], p[:], ACT.Exp).then_inc(S["exped"], 1)
            for n in range(2 * WG):
                wait_weights(act, n)
                nc.scalar.activation(parts(n)[0], stage[:, n % 4], ACT.Copy).then_inc(S["w_high"], 1)
            wait(act, "consts", 16 * N_CONST)
            wait(act, "tiles_done", 1)
            for e in range(E):
                def tokens(t):
                    wait(act, "x_mm", t + 1)
                    for b in range(2):
                        nc.scalar.activation(xTh[:, 2 * b:2 * b + 2].rearrange("p k t -> p (k t)"), ps[:, X_BANK + b],
                                             ACT.Copy).then_inc(S["x_high"], 1)

                def hidden(i, n, t):
                    for c in range(HC):
                        wait(act, "h_mm", n * HC + c + 1)
                        wait(act, "h_split", n * HC + c - RING + 1)
                        nc.scalar.activation(h[:, c % RING], ps[:, H_BANK + c % RING, 0:GT], ACT.Gelu,
                                             bias=b1[:, e * HC + c:e * HC + c + 1]).then_inc(S["h_done"], 1)
                    tokens(t + 1)
                    wait(act, "y_done", 2 * n + 2)
                    act.dma_start(xs_v[bass.ds(i + e * EG, 1)].rearrange("a p h d -> (a p) h d"), y[:]).then_inc(S["y_stored"], 16)

                expert_tiles(act, e, tokens, hidden)
            for i in range(1, NT, 2):
                wait(act, "combined", 2 * i + 2)
                act.dma_start(out_v[i], stage[0:TT, i // 4, i % 4]).then_inc(S["out_stored"], 16)

        @block.tensor
        def _(pe):
            start(pe, "rank_mm x_mm h_mm l2_mm")

            wait(pe, "lg_loaded", 48)
            wait(pe, "ones_set", 2)
            wait(pe, "step", STEPS_TO_MASK)
            for bank, w in ((0, upper), (1, ones)):
                ins = nc.tensor.matmul(ps[0:TT, bank, 0:NT * E], w[:], m[:].rearrange("p i e -> p (i e)"), start=True, stop=True)
            ins.then_inc(S["rank_mm"], 1)
            wait(pe, "consts", 16 * N_CONST)
            wait(pe, "tiles_done", 1)

            def products(out, stationary, moving, first, last):
                (sh, sl), (mh, ml) = stationary, moving
                nc.tensor.matmul(out, sh, mh, start=first, stop=False)
                nc.tensor.matmul(out, sh, ml, start=False, stop=False)
                return nc.tensor.matmul(out, sl, mh, start=False, stop=last)

            for e in range(E):
                def tokens(t):
                    pe.wait_ge(S["x_loaded"], 16 * t + 17)
                    wait(pe, "x_split", 2 * t)
                    for q in range(KC):
                        for s in range(HALVES):
                            at = (q % 2) * GT + s * P
                            ins = nc.tensor.transpose(ps[:, X_BANK + q // 2, at:at + P], xt[:, s, q * P:(q + 1) * P], ident[:])
                    ins.then_inc(S["x_mm"], 1)

                def tile(i, n, t):
                    wait(pe, "x_split", 2 * t + 2)
                    for step in range(HC + AHEAD):
                        if step < HC:
                            c = step
                            g, w = c // CW, slice(c % CW * P, c % CW * P + P)
                            if c % CW == 0:
                                wait_split(pe, 2 * WG * e + 2 * g)
                            wait(pe, "h_done", n * HC + c - RING + 1)
                            for q in range(KC):
                                ins = products(ps[:, H_BANK + c % RING, 0:GT], (w1h[:, g, q, w], w1l[:, g, q, w]),
                                               (xTh[:, q], xTl[:, q]), q == 0, q == KC - 1)
                            ins.then_inc(S["h_mm"], 1)
                        if step == HC - 1:
                            tokens(t + 1)
                        if step >= AHEAD:
                            c = step - AHEAD
                            g, k = c // CW, c % RING
                            if c % CW == 0:
                                wait_split(pe, 2 * WG * e + 2 * g + 1)
                            if c == 0:
                                wait(pe, "y_done", 2 * n)
                            wait(pe, "h_split", n * HC + c + 1)
                            for s in range(HALVES):
                                rows = slice(s * P, s * P + P)
                                ins = products(ps[:, Y_BANK + s], (hh[:, k, rows], hl[:, k, rows]),
                                               (w2h[:, g, c % CW], w2l[:, g, c % CW]), c == 0, c == HC - 1)
                            ins.then_inc(S["l2_mm"], 1)

                expert_tiles(pe, e, tokens, tile)


def decoder(nc, a, out):
    def scratch(name, shape):
        return nc.dram_tensor(name, shape, F32, kind="Internal").ap()

    xb_d, z_d, dt_d, u_d, y_d = (scratch(n, (CC, P, T)) for n in ("xb_d", "z_d", "dt_d", "u_d", "y_d"))
    bc_d = scratch("bc_d", (2 * NS, T))
    kh_d, kl_d, v_d = scratch("kh_d", (B, KC, P, CTX)), scratch("kl_d", (B, KC, P, CTX)), scratch("v_d", (B, NC, CT, DM))
    x2_d, xn_d, logits_d = (scratch(n, (B, TT, 2, w)) for n, w in (("x2_d", DM), ("xn_d", DM), ("logits_d", E)))
    xs_d = scratch("xs_d", (XS, DM))
    s, t, f = "L0_attn_", "L0_xattn_", "L0_ffn_"
    mamba_in(nc, a["x"], a[s + "W_in"], a[s + "conv_w"], a[s + "conv_b"], a[s + "W_x"], a[s + "W_dt"], a[s + "b_dt"],
             a["identity"], xb_d, z_d, dt_d, u_d, bc_d, xs_d)
    state_space(nc, a[s + "A_log"], a[s + "D"], a["identity"], xb_d, z_d, dt_d, u_d, bc_d, y_d,
                a["ctxT"], a[t + "Wk"], a[t + "bk"], a[t + "Wv"], kh_d, kl_d, v_d)
    attention(nc, a["x"], kh_d, kl_d, v_d, y_d, a[s + "W_out"], a[t + "Wq"], a[t + "bq"], a[t + "bv"], a[t + "Wo"], a[t + "bo"], a[f + "rW1"], a[f + "rb1"], a[f + "rW2"], a[f + "rb2"],
              a["identity"], x2_d, xn_d, logits_d)
    experts(nc, a[f + "We1"], a[f + "be1"], a[f + "We2"], a[f + "be2"], a["upper"], a["identity"], a["tile_starts"],
            x2_d, xn_d, logits_d, xs_d, out)


_INS = ["x", "ctx_512"] + ["L0_attn_" + n for n in ("W_in", "conv_w", "conv_b", "W_x", "W_dt", "b_dt", "A_log", "D", "W_out")] \
    + ["L0_xattn_" + n for n in ("Wq", "bq", "Wk", "bk", "Wv", "bv", "Wo", "bo")] \
    + ["L0_ffn_" + n for n in ("rW1", "rb1", "rW2", "rb2", "We1", "be1", "We2", "be2")]
_COLUMNS = ["L0_attn_conv_b", "L0_attn_b_dt", "L0_attn_D", "L0_xattn_bq", "L0_xattn_bk", "L0_xattn_bv", "L0_ffn_rb1", "L0_ffn_be1"]


def kernel(**inputs):
    import numpy as np
    import concourse.bacc as bacc
    from concourse.bass_utils import run_bass_kernel_spmd

    arrays = {name: np.asarray(inputs[name]) for name in _INS}
    for name in _COLUMNS:
        arrays[name] = arrays[name].reshape(-1, P).T
    arrays["ctxT"] = arrays.pop("ctx_512").transpose(0, 2, 1)
    arrays["identity"] = np.eye(P, dtype=np.float32)
    arrays["upper"] = np.triu(np.ones((TT, TT), np.float32), 1)
    arrays["tile_starts"] = np.arange(0, SLOTS, GT, dtype=np.float32)[None]
    arrays = {name: np.ascontiguousarray(a) for name, a in arrays.items()}

    nc = bacc.Bacc("TRN2", target_bir_lowering=False, num_devices=1)
    a = {name: nc.dram_tensor("in_" + name, v.shape, F32, kind="ExternalInput").ap() for name, v in arrays.items()}
    out = nc.dram_tensor("out", (B, L, DM), F32, kind="ExternalOutput").ap()
    decoder(nc, a, out)
    r = run_bass_kernel_spmd(nc, [{"in_" + name: v for name, v in arrays.items()}], core_ids=[0])
    return r.results[0]["out"]
```
